# Optimizing a Trainium2 kernel written in Bass

```python
import numpy as np
import jax
import jax.numpy as jnp

def _softmax(x, axis=-1):
    return jax.nn.softmax(x, axis=axis)

def _gelu(x):
    return jax.nn.gelu(x, approximate=True)

def _silu(x):
    return jax.nn.silu(x)

def _sigmoid(x):
    return jax.nn.sigmoid(x)

def _layernorm(x, axis=-1, eps=1e-05):
    m = jnp.mean(x, axis=axis, keepdims=True)
    v = jnp.var(x, axis=axis, keepdims=True)
    return (x - m) / jnp.sqrt(v + eps)

def _scatter_add(tgt, idx, src, axis=0):
    return tgt.at[idx].add(src)

def _segment_sum(src, seg, n):
    return jax.ops.segment_sum(src, seg, n)
kernel_name = 'mk_decoder_preln_d4_seqx_r8_b63dd3'

def setup_inputs(seed: int=0):
    np.random.seed(seed)
    _w = jnp.asarray

    def _rec_inputs():
        import jax
        import jax.numpy as jnp
        _rk = jax.random.key(seed)
        x = -0.0002928 + 1 * jax.random.normal(jax.random.fold_in(_rk, 1), (8, 128, 128), jnp.float32)
        _lenS = 128 - jax.random.randint(jax.random.fold_in(_rk, 7), (8,), 0, max(1, 128 // 4) + 1, jnp.int32)
        _lenS2 = 128 - jax.random.randint(jax.random.fold_in(_rk, 8), (8,), 0, max(1, 128 // 4) + 1, jnp.int32)
        _ctx_1024P = jax.random.normal(jax.random.fold_in(_rk, 11), (8, 16, 128), jnp.float32)
        _ctx_1024c = jax.random.dirichlet(jax.random.fold_in(_rk, 511), 0.3 * jnp.ones((16,), jnp.float32), (8, 128))
        _ctx_1024t = jnp.einsum('bsk,bkd->bsd', _ctx_1024c, _ctx_1024P)
        _ctx_1024t = _ctx_1024t * jax.lax.rsqrt(jnp.mean(jnp.square(_ctx_1024t)) + 1e-12) * 0.953939
        ctx_1024 = -1.39393e-06 + 0.999914 * (_ctx_1024t + 0.3 * jax.random.normal(jax.random.fold_in(_rk, 611), (8, 128, 128), jnp.float32))
        _validS = jnp.arange(128)[None, :] < _lenS[:, None]
        _validS2 = jnp.arange(128)[None, :] < _lenS2[:, None]
        _causal = jnp.tril(jnp.ones((128, 128), dtype=bool))
        mask_Bx1xSxS2_ik1 = jnp.where(jnp.broadcast_to(_validS2[:, None, None, :], (8, 1, 128, 128)), 1, 0).astype(jnp.int32)
        return (x, ctx_1024, mask_Bx1xSxS2_ik1)
    x, ctx_1024, mask_Bx1xSxS2_ik1 = _rec_inputs()

    def _L0_attn_setup():
        import jax, jax.numpy as jnp
        import numpy as np
        B, T, D = (4, 256, 128)
        EPS_BIT = 1e-08
        EPS_OUT = 1.1920929e-07

        def rms_norm(x, w, eps):
            var = jnp.mean(jnp.square(x), axis=-1, keepdims=True)
            return x * jax.lax.rsqrt(var + eps) * w

        def act_quant(x):
            scale = 127.0 / jnp.clip(jnp.max(jnp.abs(x), axis=-1, keepdims=True), 1e-05)
            return jnp.clip(jnp.round(x * scale), -128.0, 127.0) / scale

        def weight_quant(w):
            scale = 1.0 / jnp.clip(jnp.mean(jnp.abs(w)), 1e-05)
            return jnp.clip(jnp.round(w * scale), -1.0, 1.0) / scale

        def bit_linear(x, w, norm_w):
            xn = rms_norm(x, norm_w, EPS_BIT)
            xq = xn + jax.lax.stop_gradient(act_quant(xn) - xn)
            wq = w + jax.lax.stop_gradient(weight_quant(w) - w)
            return xq @ wq.T
        key = jax.random.key(seed)
        ks = jax.random.split(key, 5)
        gain = 2.0 ** (-2.5) * np.sqrt(2.0 / (D + D))
        inp = {'hidden_states': jax.random.normal(ks[0], (B, T, D), dtype=jnp.float32), 'Wi': jax.random.normal(ks[1], (D, D), dtype=jnp.float32) * gain, 'Wf': jax.random.normal(ks[2], (D, D), dtype=jnp.float32) * gain, 'Wg': jax.random.normal(ks[3], (D, D), dtype=jnp.float32) * gain, 'Wo': jax.random.normal(ks[4], (D, D), dtype=jnp.float32) * gain, 'ni': jnp.ones((D,), jnp.float32), 'nf': jnp.ones((D,), jnp.float32), 'ng': jnp.ones((D,), jnp.float32), 'no': jnp.ones((D,), jnp.float32), 'nout': jnp.ones((D,), jnp.float32)}
        return inp
    _L0_attn_all = _L0_attn_setup()
    _L0_attn_in = {k: v for k, v in _L0_attn_all.items() if k in ('Wi', 'Wf', 'Wg', 'Wo', 'ni', 'nf', 'ng', 'no', 'nout')}
    del _L0_attn_all

    def _L0_xattn_setup():
        import jax, jax.numpy as jnp
        import numpy as np
        B, S, D, H = (2, 256, 128, 16)
        DK = D // H
        EPS = 1e-10
        ROPE_BASE = 500000.0

        def _rms_norm(x, w):
            return w * x * jax.lax.rsqrt(jnp.mean(x * x, axis=-1, keepdims=True) + EPS)

        def _rope_tables(seq_len, dk):
            inv_freq = 1.0 / ROPE_BASE ** (jnp.arange(0, dk, 2, dtype=jnp.float32) / dk)
            t = jnp.arange(seq_len, dtype=jnp.float32)
            freqs = jnp.outer(t, inv_freq)
            emb = jnp.concatenate([freqs, freqs], -1)
            return (jnp.cos(emb), jnp.sin(emb))

        def _rotate_half(x):
            x1, x2 = jnp.split(x, 2, axis=-1)
            return jnp.concatenate([-x2, x1], axis=-1)
        key = jax.random.key(seed)
        ks = jax.random.split(key, 8)
        scale = 1.0 / np.sqrt(D)
        return {'q': jax.random.normal(ks[0], (B, S, D), jnp.float32), 'k': jax.random.normal(ks[1], (B, S, D), jnp.float32), 'v': jax.random.normal(ks[2], (B, S, D), jnp.float32), 'Wq': jax.random.normal(ks[3], (D, D), jnp.float32) * scale, 'Wk': jax.random.normal(ks[4], (D, D), jnp.float32) * scale, 'Wv': jax.random.normal(ks[5], (D, D), jnp.float32) * scale, 'Wo': jax.random.normal(ks[6], (D, D), jnp.float32) * scale, 'q_norm_w': jnp.ones((DK,), jnp.float32) + 0.02 * jax.random.normal(ks[7], (DK,), jnp.float32), 'k_norm_w': jnp.ones((DK,), jnp.float32)}
    _L0_xattn_all = _L0_xattn_setup()
    _L0_xattn_in = {k: v for k, v in _L0_xattn_all.items() if k in ('Wq', 'Wk', 'Wv', 'Wo', 'q_norm_w', 'k_norm_w')}
    del _L0_xattn_all

    def _L0_ffn_setup():
        import jax, jax.numpy as jnp
        import numpy as np
        B, S, D, E, K = (4, 256, 128, 8, 2)
        key = jax.random.key(seed)
        k1, k2, k3 = jax.random.split(key, 3)
        scale = 1.0 / np.sqrt(D)
        x = jax.random.normal(k1, (B, S, D), dtype=jnp.float32)
        Wg = jax.random.normal(k2, (D, E), dtype=jnp.float32) * scale
        bg = jnp.zeros((E,), dtype=jnp.float32)
        We = jax.random.normal(k3, (E, D, D), dtype=jnp.float32) * scale
        be = jnp.zeros((E, D), dtype=jnp.float32)
        return {'x': x, 'Wg': Wg, 'bg': bg, 'We': We, 'be': be}
    _L0_ffn_all = _L0_ffn_setup()
    _L0_ffn_in = {k: v for k, v in _L0_ffn_all.items() if k in ('Wg', 'bg', 'We', 'be')}
    del _L0_ffn_all

    def _L1_attn_setup():
        import jax, jax.numpy as jnp
        import numpy as np
        D_MODEL = 128
        NUM_HEADS = 16
        D_K = D_MODEL // NUM_HEADS
        BATCH, SEQ = (2, 256)
        key = jax.random.key(seed)
        k = jax.random.split(key, 5)
        std = np.sqrt(2.0 / (D_MODEL + D_MODEL)).astype(np.float32)
        return {'x': jax.random.normal(k[0], (BATCH, SEQ, D_MODEL), dtype=jnp.float32), 'WQ': jax.random.normal(k[1], (D_MODEL, D_MODEL), dtype=jnp.float32) * std, 'WK': jax.random.normal(k[2], (D_MODEL, D_MODEL), dtype=jnp.float32) * std, 'WV': jax.random.normal(k[3], (D_MODEL, D_MODEL), dtype=jnp.float32) * std, 'WO': jax.random.normal(k[4], (D_MODEL, D_MODEL), dtype=jnp.float32) * std}
    _L1_attn_all = _L1_attn_setup()
    _L1_attn_in = {k: v for k, v in _L1_attn_all.items() if k in ('WQ', 'WK', 'WV', 'WO')}
    del _L1_attn_all

    def _L1_xattn_setup():
        import jax, jax.numpy as jnp
        import numpy as np
        import math
        EMBED = 128
        HEADS = 16
        HEAD_DIM = EMBED // HEADS

        def alibi_slopes(heads: int) -> jnp.ndarray:
            return jnp.asarray([2.0 ** (-8.0 * (h + 1) / heads) for h in range(heads)], dtype=jnp.float32)
        key = jax.random.key(seed)
        ks = jax.random.split(key, 8)
        B, Nq, Nk = (2, 256, 256)
        s = 0.02
        return {'query': jax.random.normal(ks[0], (B, Nq, EMBED), jnp.float32), 'kv': jax.random.normal(ks[1], (B, Nk, EMBED), jnp.float32), 'Wq': jax.random.normal(ks[2], (EMBED, EMBED), jnp.float32) * s, 'bq': jnp.zeros((EMBED,), jnp.float32), 'Wkv': jax.random.normal(ks[3], (EMBED, 2 * EMBED), jnp.float32) * s, 'bkv': jnp.zeros((2 * EMBED,), jnp.float32), 'Wo': jax.random.normal(ks[4], (EMBED, EMBED), jnp.float32) * s, 'bo': jnp.zeros((EMBED,), jnp.float32)}
    _L1_xattn_all = _L1_xattn_setup()
    _L1_xattn_in = {k: v for k, v in _L1_xattn_all.items() if k in ('Wq', 'bq', 'Wkv', 'bkv', 'Wo', 'bo')}
    del _L1_xattn_all

    def _L1_ffn_setup():
        import jax, jax.numpy as jnp
        import numpy as np
        DIM = 128
        NUM_EXPERTS = 6
        TOP_K = 2
        HIDDEN = DIM * 2
        key = jax.random.key(seed)
        ks = jax.random.split(key, 7)
        s_in = 1.0 / np.sqrt(DIM)
        s_h = 1.0 / np.sqrt(HIDDEN)
        x = jax.random.normal(ks[0], (4, 256, DIM), dtype=jnp.float32)
        Wg = jax.random.uniform(ks[1], (DIM, NUM_EXPERTS), jnp.float32, -s_in, s_in)
        bg = jax.random.uniform(ks[2], (NUM_EXPERTS,), jnp.float32, -s_in, s_in)
        W1 = jax.random.uniform(ks[3], (NUM_EXPERTS, DIM, HIDDEN), jnp.float32, -s_in, s_in)
        b1 = jax.random.uniform(ks[4], (NUM_EXPERTS, HIDDEN), jnp.float32, -s_in, s_in)
        W2 = jax.random.uniform(ks[5], (NUM_EXPERTS, HIDDEN, DIM), jnp.float32, -s_h, s_h)
        b2 = jax.random.uniform(ks[6], (NUM_EXPERTS, DIM), jnp.float32, -s_h, s_h)
        return {'x': x, 'Wg': Wg, 'bg': bg, 'W1': W1, 'b1': b1, 'W2': W2, 'b2': b2}
    _L1_ffn_all = _L1_ffn_setup()
    _L1_ffn_in = {k: v for k, v in _L1_ffn_all.items() if k in ('Wg', 'bg', 'W1', 'b1', 'W2', 'b2')}
    del _L1_ffn_all

    def _L2_attn_setup():
        import jax, jax.numpy as jnp
        import numpy as np
        from functools import partial
        LN_EPS = 1000000.0
        FEAT_EPS = 1e-06

        def _layernorm(x, gamma, beta):
            mu = jnp.mean(x, axis=-1, keepdims=True)
            var = jnp.var(x, axis=-1, keepdims=True)
            return gamma * (x - mu) / jnp.sqrt(var + LN_EPS) + beta

        def _phi(x, omega):
            m = omega.shape[0]
            proj = jnp.einsum('bhsd,md->bhsm', x, omega)
            z = proj - 0.5 * jnp.sum(x * x, axis=-1, keepdims=True)
            z = z - jnp.max(z, axis=-1, keepdims=True)
            return jnp.exp(z) / jnp.sqrt(jnp.asarray(m, x.dtype)) + FEAT_EPS

        def _forward(batch, Wq, Wk, Wv, Wo, omega, W1, b1, W2, b2, gamma, beta):
            B, S, D = batch.shape
            M, dh = omega.shape
            H = D // dh
            scale = dh ** (-0.25)

            def heads(W):
                return (batch @ W).reshape(B, S, H, dh).transpose(0, 2, 1, 3)
            q = heads(Wq) * scale
            k = heads(Wk) * scale
            v = heads(Wv)
            qp = _phi(q, omega)
            kp = _phi(k, omega)
            qs = qp.transpose(2, 0, 1, 3)
            ks = kp.transpose(2, 0, 1, 3)
            vs = v.transpose(2, 0, 1, 3)

            def step(carry, qkv):
                S_kv, s_k = carry
                qt, kt, vt = qkv
                S_kv = S_kv + kt[..., :, None] * vt[..., None, :]
                s_k = s_k + kt
                num = jnp.einsum('bhm,bhmd->bhd', qt, S_kv)
                den = jnp.einsum('bhm,bhm->bh', qt, s_k)
                return ((S_kv, s_k), num / (den[..., None] + FEAT_EPS))
            carry0 = (jnp.zeros((B, H, M, dh), batch.dtype), jnp.zeros((B, H, M), batch.dtype))
            _, outs = jax.lax.scan(step, carry0, (qs, ks, vs))
            attn = outs.transpose(1, 0, 2, 3).reshape(B, S, D) @ Wo
            h = _layernorm(batch + attn, gamma, beta)
            out = jnp.maximum(h @ W1 + b1, 0.0) @ W2 + b2
            return out
        key = jax.random.key(seed)
        ks = jax.random.split(key, 8)
        B, S, D, H, dh, M, DFF = (4, 128, 128, 16, 64, 128, 512)
        w = 0.02
        return {'batch': jax.random.normal(ks[0], (B, S, D), jnp.float32), 'Wq': jax.random.normal(ks[1], (D, D), jnp.float32) * w, 'Wk': jax.random.normal(ks[2], (D, D), jnp.float32) * w, 'Wv': jax.random.normal(ks[3], (D, D), jnp.float32) * w, 'Wo': jax.random.normal(ks[4], (D, D), jnp.float32) * w, 'omega': jax.random.normal(ks[5], (M, dh), jnp.float32), 'W1': jax.random.normal(ks[6], (D, DFF), jnp.float32) * w, 'b1': jnp.zeros((DFF,), jnp.float32), 'W2': jax.random.normal(ks[7], (DFF, D), jnp.float32) * w, 'b2': jnp.zeros((D,), jnp.float32), 'gamma': jnp.ones((D,), jnp.float32), 'beta': jnp.zeros((D,), jnp.float32)}
    _L2_attn_all = _L2_attn_setup()
    _L2_attn_in = {k: v for k, v in _L2_attn_all.items() if k in ('Wq', 'Wk', 'Wv', 'Wo', 'omega', 'W1', 'b1', 'W2', 'b2', 'gamma', 'beta')}
    del _L2_attn_all

    def _L2_xattn_setup():
        import jax, jax.numpy as jnp
        import numpy as np
        EMBED = 128
        HEADS = 16
        HEAD_DIM = EMBED // HEADS
        key = jax.random.key(seed)
        ks = jax.random.split(key, 12)
        B, S, E = (2, 256, EMBED)
        s = 1.0 / np.sqrt(E)
        inp = {'queries': jax.random.normal(ks[0], (B, S, E), jnp.float32), 'keys': jax.random.normal(ks[1], (B, S, E), jnp.float32), 'values': jax.random.normal(ks[2], (B, S, E), jnp.float32), 'mask': jax.random.randint(ks[3], (B, 1, S, S), 0, 2, jnp.int32), 'Wq': jax.random.normal(ks[4], (E, E), jnp.float32) * s, 'bq': jax.random.normal(ks[5], (E,), jnp.float32) * s, 'Wk': jax.random.normal(ks[6], (E, E), jnp.float32) * s, 'bk': jax.random.normal(ks[7], (E,), jnp.float32) * s, 'Wv': jax.random.normal(ks[8], (E, E), jnp.float32) * s, 'bv': jax.random.normal(ks[9], (E,), jnp.float32) * s, 'Wo': jax.random.normal(ks[10], (E, E), jnp.float32) * s, 'bo': jax.random.normal(ks[11], (E,), jnp.float32) * s}
        return inp
    _L2_xattn_all = _L2_xattn_setup()
    _L2_xattn_in = {k: v for k, v in _L2_xattn_all.items() if k in ('Wq', 'bq', 'Wk', 'bk', 'Wv', 'bv', 'Wo', 'bo')}
    del _L2_xattn_all

    def _L2_ffn_setup():
        import jax, jax.numpy as jnp
        import numpy as np
        B, L, D = (4, 128, 128)
        E, H, K = (16, 64, 8)
        EPS = 1e-12

        def _l2norm(v, axis=-1):
            n = jnp.sqrt(jnp.sum(v * v, axis=axis, keepdims=True))
            return v / jnp.maximum(n, EPS)
        if __name__ == '__main__':
            out = reference(**setup_inputs())
            print(out.shape)
        key = jax.random.key(seed)
        ks = jax.random.split(key, 8)
        s = lambda fan_in: 1.0 / np.sqrt(fan_in)
        return {'x': jax.random.normal(ks[0], (B, L, D), jnp.float32), 'gate_w': jax.random.normal(ks[1], (E, D), jnp.float32) * s(D), 'w_gate': jax.random.normal(ks[2], (E, D, H), jnp.float32) * s(D), 'w_up': jax.random.normal(ks[3], (E, D, H), jnp.float32) * s(D), 'w_down': jax.random.normal(ks[4], (E, H, D), jnp.float32) * s(H), 'sw_gate': jax.random.normal(ks[5], (D, H), jnp.float32) * s(D), 'sw_up': jax.random.normal(ks[6], (D, H), jnp.float32) * s(D), 'sw_down': jax.random.normal(ks[7], (H, D), jnp.float32) * s(H)}
    _L2_ffn_all = _L2_ffn_setup()
    _L2_ffn_in = {k: v for k, v in _L2_ffn_all.items() if k in ('gate_w', 'w_gate', 'w_up', 'w_down', 'sw_gate', 'sw_up', 'sw_down')}
    del _L2_ffn_all

    def _L3_attn_setup():
        import jax, jax.numpy as jnp
        import numpy as np
        from math import sqrt
        D_MODEL = 128
        NUM_HEADS = 16
        D_HEAD = D_MODEL // NUM_HEADS
        THETA = 10000.0

        def _rope(x, freqs):
            xr = x[..., ::2]
            xi = x[..., 1::2]
            cos = jnp.cos(freqs)
            sin = jnp.sin(freqs)
            yr = xr * cos - xi * sin
            yi = xr * sin + xi * cos
            return jnp.stack([yr, yi], axis=-1).reshape(x.shape)
        key = jax.random.key(seed)
        k1, k2, k3 = jax.random.split(key, 3)
        X = jax.random.normal(k1, (4, 256, D_MODEL), dtype=jnp.float32)
        std_kqv = sqrt(2.0 / (D_MODEL + 3 * D_MODEL))
        W_KQV = std_kqv * jax.random.truncated_normal(k2, -3.0, 3.0, (3 * D_MODEL, D_MODEL), dtype=jnp.float32)
        std_o = sqrt(2.0 / (D_MODEL + D_MODEL))
        W_O = std_o * jax.random.truncated_normal(k3, -3.0, 3.0, (D_MODEL, D_MODEL), dtype=jnp.float32)
        return {'X': X, 'W_KQV': W_KQV, 'W_O': W_O}
    _L3_attn_all = _L3_attn_setup()
    _L3_attn_in = {k: v for k, v in _L3_attn_all.items() if k in ('W_KQV', 'W_O')}
    del _L3_attn_all

    def _L3_xattn_setup():
        import jax, jax.numpy as jnp
        import numpy as np
        D_MODEL = 128
        B, S = (4, 256)
        key = jax.random.key(seed)
        ks = jax.random.split(key, 10)
        s = 1.0 / np.sqrt(D_MODEL)
        return {'k': jax.random.normal(ks[0], (B, S, D_MODEL), jnp.float32), 'v': jax.random.normal(ks[1], (B, S, D_MODEL), jnp.float32), 'q': jax.random.normal(ks[2], (B, S, D_MODEL), jnp.float32), 'Wk': jax.random.normal(ks[3], (D_MODEL, D_MODEL), jnp.float32) * s, 'Wv': jax.random.normal(ks[4], (D_MODEL, D_MODEL), jnp.float32) * s, 'bv': jnp.zeros((D_MODEL,), jnp.float32), 'Wq': jax.random.normal(ks[5], (D_MODEL, D_MODEL), jnp.float32) * s, 'bq': jnp.zeros((D_MODEL,), jnp.float32), 'Wo': jax.random.normal(ks[6], (D_MODEL, D_MODEL), jnp.float32) * s, 'bo': jnp.zeros((D_MODEL,), jnp.float32)}
    _L3_xattn_all = _L3_xattn_setup()
    _L3_xattn_in = {k: v for k, v in _L3_xattn_all.items() if k in ('Wk', 'Wv', 'bv', 'Wq', 'bq', 'Wo', 'bo')}
    del _L3_xattn_all

    def _L3_ffn_setup():
        import jax, jax.numpy as jnp
        import numpy as np
        DIM = 128
        NUM_HEAVY = 128
        N_ITERS = 50
        EPS = 1.0
        FETCH_K_RATIO = 9.0 / 8.0

        def rms_norm(x, gamma):
            norm = jnp.maximum(jnp.linalg.norm(x, axis=-1, keepdims=True), 1e-12)
            return x / norm * x.shape[-1] ** 0.5 * gamma

        def feed_forward(x, gamma, w1, b1, w2, b2):
            h = jax.nn.gelu(rms_norm(x, gamma) @ w1 + b1, approximate=False)
            return h @ w2 + b2

        def coor_descent(s, k, n_iters, eps):
            logk = jnp.log(jnp.asarray(k, dtype=s.dtype))

            def step(ab, _):
                a, b = ab
                sb = (s + b) / eps
                a = eps * (logk - jax.scipy.special.logsumexp(sb, axis=-1, keepdims=True))
                b = -jax.nn.relu(s + a)
                return ((a, b), None)
            a0 = jnp.zeros_like(s[..., :1])
            b0 = -s
            (a, b), _ = jax.lax.scan(step, (a0, b0), None, length=n_iters)
            return jnp.exp((s + a + b) / eps)
        key = jax.random.key(seed)
        ks = jax.random.split(key, 8)
        b, n, d = (4, 1024, DIM)
        dl, dh = (int(d * 0.5), d * 4)
        u = lambda k, shape, fan_in: jax.random.uniform(k, shape, jnp.float32, -1.0, 1.0) / np.sqrt(fan_in)
        return {'x': jax.random.normal(ks[0], (b, n, d), jnp.float32), 'routing_token': jax.random.normal(ks[1], (d,), jnp.float32), 'light_gamma': jnp.ones((d,), jnp.float32), 'light_w1': u(ks[2], (d, dl), d), 'light_b1': jnp.zeros((dl,), jnp.float32), 'light_w2': u(ks[3], (dl, d), dl), 'light_b2': jnp.zeros((d,), jnp.float32), 'heavy_gamma': jnp.ones((d,), jnp.float32), 'heavy_w1': u(ks[4], (d, dh), d), 'heavy_b1': jnp.zeros((dh,), jnp.float32), 'heavy_w2': u(ks[5], (dh, d), dh), 'heavy_b2': jnp.zeros((d,), jnp.float32)}
    _L3_ffn_all = _L3_ffn_setup()
    _L3_ffn_in = {k: v for k, v in _L3_ffn_all.items() if k in ('routing_token', 'light_gamma', 'light_w1', 'light_b1', 'light_w2', 'light_b2', 'heavy_gamma', 'heavy_w1', 'heavy_b1', 'heavy_w2', 'heavy_b2')}
    del _L3_ffn_all
    return {'x': x, 'ctx_1024': ctx_1024, 'mask_Bx1xSxS2_ik1': mask_Bx1xSxS2_ik1, 'L0_attn_Wi': _L0_attn_in['Wi'], 'L0_attn_Wf': _L0_attn_in['Wf'], 'L0_attn_Wg': _L0_attn_in['Wg'], 'L0_attn_Wo': _L0_attn_in['Wo'], 'L0_attn_ni': _L0_attn_in['ni'], 'L0_attn_nf': _L0_attn_in['nf'], 'L0_attn_ng': _L0_attn_in['ng'], 'L0_attn_no': _L0_attn_in['no'], 'L0_attn_nout': _L0_attn_in['nout'], 'L0_xattn_Wq': _L0_xattn_in['Wq'], 'L0_xattn_Wk': _L0_xattn_in['Wk'], 'L0_xattn_Wv': _L0_xattn_in['Wv'], 'L0_xattn_Wo': _L0_xattn_in['Wo'], 'L0_xattn_q_norm_w': _L0_xattn_in['q_norm_w'], 'L0_xattn_k_norm_w': _L0_xattn_in['k_norm_w'], 'L0_ffn_Wg': _L0_ffn_in['Wg'], 'L0_ffn_bg': _L0_ffn_in['bg'], 'L0_ffn_We': _L0_ffn_in['We'], 'L0_ffn_be': _L0_ffn_in['be'], 'L1_attn_WQ': _L1_attn_in['WQ'], 'L1_attn_WK': _L1_attn_in['WK'], 'L1_attn_WV': _L1_attn_in['WV'], 'L1_attn_WO': _L1_attn_in['WO'], 'L1_xattn_Wq': _L1_xattn_in['Wq'], 'L1_xattn_bq': _L1_xattn_in['bq'], 'L1_xattn_Wkv': _L1_xattn_in['Wkv'], 'L1_xattn_bkv': _L1_xattn_in['bkv'], 'L1_xattn_Wo': _L1_xattn_in['Wo'], 'L1_xattn_bo': _L1_xattn_in['bo'], 'L1_ffn_Wg': _L1_ffn_in['Wg'], 'L1_ffn_bg': _L1_ffn_in['bg'], 'L1_ffn_W1': _L1_ffn_in['W1'], 'L1_ffn_b1': _L1_ffn_in['b1'], 'L1_ffn_W2': _L1_ffn_in['W2'], 'L1_ffn_b2': _L1_ffn_in['b2'], 'L2_attn_Wq': _L2_attn_in['Wq'], 'L2_attn_Wk': _L2_attn_in['Wk'], 'L2_attn_Wv': _L2_attn_in['Wv'], 'L2_attn_Wo': _L2_attn_in['Wo'], 'L2_attn_omega': _L2_attn_in['omega'], 'L2_attn_W1': _L2_attn_in['W1'], 'L2_attn_b1': _L2_attn_in['b1'], 'L2_attn_W2': _L2_attn_in['W2'], 'L2_attn_b2': _L2_attn_in['b2'], 'L2_attn_gamma': _L2_attn_in['gamma'], 'L2_attn_beta': _L2_attn_in['beta'], 'L2_xattn_Wq': _L2_xattn_in['Wq'], 'L2_xattn_bq': _L2_xattn_in['bq'], 'L2_xattn_Wk': _L2_xattn_in['Wk'], 'L2_xattn_bk': _L2_xattn_in['bk'], 'L2_xattn_Wv': _L2_xattn_in['Wv'], 'L2_xattn_bv': _L2_xattn_in['bv'], 'L2_xattn_Wo': _L2_xattn_in['Wo'], 'L2_xattn_bo': _L2_xattn_in['bo'], 'L2_ffn_gate_w': _L2_ffn_in['gate_w'], 'L2_ffn_w_gate': _L2_ffn_in['w_gate'], 'L2_ffn_w_up': _L2_ffn_in['w_up'], 'L2_ffn_w_down': _L2_ffn_in['w_down'], 'L2_ffn_sw_gate': _L2_ffn_in['sw_gate'], 'L2_ffn_sw_up': _L2_ffn_in['sw_up'], 'L2_ffn_sw_down': _L2_ffn_in['sw_down'], 'L3_attn_W_KQV': _L3_attn_in['W_KQV'], 'L3_attn_W_O': _L3_attn_in['W_O'], 'L3_xattn_Wk': _L3_xattn_in['Wk'], 'L3_xattn_Wv': _L3_xattn_in['Wv'], 'L3_xattn_bv': _L3_xattn_in['bv'], 'L3_xattn_Wq': _L3_xattn_in['Wq'], 'L3_xattn_bq': _L3_xattn_in['bq'], 'L3_xattn_Wo': _L3_xattn_in['Wo'], 'L3_xattn_bo': _L3_xattn_in['bo'], 'L3_ffn_routing_token': _L3_ffn_in['routing_token'], 'L3_ffn_light_gamma': _L3_ffn_in['light_gamma'], 'L3_ffn_light_w1': _L3_ffn_in['light_w1'], 'L3_ffn_light_b1': _L3_ffn_in['light_b1'], 'L3_ffn_light_w2': _L3_ffn_in['light_w2'], 'L3_ffn_light_b2': _L3_ffn_in['light_b2'], 'L3_ffn_heavy_gamma': _L3_ffn_in['heavy_gamma'], 'L3_ffn_heavy_w1': _L3_ffn_in['heavy_w1'], 'L3_ffn_heavy_b1': _L3_ffn_in['heavy_b1'], 'L3_ffn_heavy_w2': _L3_ffn_in['heavy_w2'], 'L3_ffn_heavy_b2': _L3_ffn_in['heavy_b2']}

def reference(x, ctx_1024, mask_Bx1xSxS2_ik1, L0_attn_Wi, L0_attn_Wf, L0_attn_Wg, L0_attn_Wo, L0_attn_ni, L0_attn_nf, L0_attn_ng, L0_attn_no, L0_attn_nout, L0_xattn_Wq, L0_xattn_Wk, L0_xattn_Wv, L0_xattn_Wo, L0_xattn_q_norm_w, L0_xattn_k_norm_w, L0_ffn_Wg, L0_ffn_bg, L0_ffn_We, L0_ffn_be, L1_attn_WQ, L1_attn_WK, L1_attn_WV, L1_attn_WO, L1_xattn_Wq, L1_xattn_bq, L1_xattn_Wkv, L1_xattn_bkv, L1_xattn_Wo, L1_xattn_bo, L1_ffn_Wg, L1_ffn_bg, L1_ffn_W1, L1_ffn_b1, L1_ffn_W2, L1_ffn_b2, L2_attn_Wq, L2_attn_Wk, L2_attn_Wv, L2_attn_Wo, L2_attn_omega, L2_attn_W1, L2_attn_b1, L2_attn_W2, L2_attn_b2, L2_attn_gamma, L2_attn_beta, L2_xattn_Wq, L2_xattn_bq, L2_xattn_Wk, L2_xattn_bk, L2_xattn_Wv, L2_xattn_bv, L2_xattn_Wo, L2_xattn_bo, L2_ffn_gate_w, L2_ffn_w_gate, L2_ffn_w_up, L2_ffn_w_down, L2_ffn_sw_gate, L2_ffn_sw_up, L2_ffn_sw_down, L3_attn_W_KQV, L3_attn_W_O, L3_xattn_Wk, L3_xattn_Wv, L3_xattn_bv, L3_xattn_Wq, L3_xattn_bq, L3_xattn_Wo, L3_xattn_bo, L3_ffn_routing_token, L3_ffn_light_gamma, L3_ffn_light_w1, L3_ffn_light_b1, L3_ffn_light_w2, L3_ffn_light_b2, L3_ffn_heavy_gamma, L3_ffn_heavy_w1, L3_ffn_heavy_b1, L3_ffn_heavy_w2, L3_ffn_heavy_b2):
    import jax
    import jax.numpy as jnp

    def _L0_attn_ref(hidden_states, Wi, Wf, Wg, Wo, ni, nf, ng, no, nout):
        import jax, jax.numpy as jnp
        import numpy as np
        B, T, D = (4, 256, 128)
        EPS_BIT = 1e-08
        EPS_OUT = 1.1920929e-07

        def rms_norm(x, w, eps):
            var = jnp.mean(jnp.square(x), axis=-1, keepdims=True)
            return x * jax.lax.rsqrt(var + eps) * w

        def act_quant(x):
            scale = 127.0 / jnp.clip(jnp.max(jnp.abs(x), axis=-1, keepdims=True), 1e-05)
            return jnp.clip(jnp.round(x * scale), -128.0, 127.0) / scale

        def weight_quant(w):
            scale = 1.0 / jnp.clip(jnp.mean(jnp.abs(w)), 1e-05)
            return jnp.clip(jnp.round(w * scale), -1.0, 1.0) / scale

        def bit_linear(x, w, norm_w):
            xn = rms_norm(x, norm_w, EPS_BIT)
            xq = xn + jax.lax.stop_gradient(act_quant(xn) - xn)
            wq = w + jax.lax.stop_gradient(weight_quant(w) - w)
            return xq @ wq.T
        i = bit_linear(hidden_states, Wi, ni)
        f = jax.nn.sigmoid(bit_linear(hidden_states, Wf, nf))
        g = bit_linear(hidden_states, Wg, ng)
        t_steps = hidden_states.shape[1]
        c = 1.0 - f ** t_steps
        o = i * jnp.sum(c * g, axis=-1, keepdims=True)
        o = rms_norm(o, nout, EPS_OUT)
        return bit_linear(o, Wo, no)

    def _L0_xattn_ref(q, k, v, Wq, Wk, Wv, Wo, q_norm_w, k_norm_w):
        import jax, jax.numpy as jnp
        import numpy as np
        B, S, D, H = (2, 256, 128, 16)
        DK = D // H
        EPS = 1e-10
        ROPE_BASE = 500000.0

        def _rms_norm(x, w):
            return w * x * jax.lax.rsqrt(jnp.mean(x * x, axis=-1, keepdims=True) + EPS)

        def _rope_tables(seq_len, dk):
            inv_freq = 1.0 / ROPE_BASE ** (jnp.arange(0, dk, 2, dtype=jnp.float32) / dk)
            t = jnp.arange(seq_len, dtype=jnp.float32)
            freqs = jnp.outer(t, inv_freq)
            emb = jnp.concatenate([freqs, freqs], -1)
            return (jnp.cos(emb), jnp.sin(emb))

        def _rotate_half(x):
            x1, x2 = jnp.split(x, 2, axis=-1)
            return jnp.concatenate([-x2, x1], axis=-1)
        Bq, Sq, _ = q.shape

        def proj(x, W):
            return (x @ W.T).reshape(Bq, Sq, H, DK).transpose(0, 2, 1, 3)
        query, key_, value = (proj(q, Wq), proj(k, Wk), proj(v, Wv))
        query = _rms_norm(query, q_norm_w)
        key_ = _rms_norm(key_, k_norm_w)
        cos, sin = _rope_tables(Sq, DK)
        query = query * cos + _rotate_half(query) * sin
        key_ = key_ * cos + _rotate_half(key_) * sin
        scale = 1.0 / np.sqrt(DK)
        scores = jnp.einsum('bhqd,bhkd->bhqk', query, key_) * scale
        causal = jnp.tril(jnp.ones((Sq, Sq), bool))
        scores = jnp.where(causal, scores, -jnp.inf)
        probs = jax.nn.softmax(scores, axis=-1)
        attn = jnp.einsum('bhqk,bhkd->bhqd', probs, value)
        attn = attn.transpose(0, 2, 1, 3).reshape(Bq, Sq, D)
        return attn @ Wo.T

    def _L0_ffn_ref(x, Wg, bg, We, be):
        import jax, jax.numpy as jnp
        import numpy as np
        B, S, D, E, K = (4, 256, 128, 8, 2)
        gate_scores = jnp.einsum('bsd,de->bse', x, Wg) + bg
        topk_values, topk_indices = jax.lax.top_k(gate_scores, K)
        sel = jax.nn.one_hot(topk_indices, E, dtype=jnp.bool_).any(axis=-2)
        masked = jnp.where(sel, gate_scores, -jnp.inf)
        gate_weights = jax.nn.softmax(masked, axis=-1)
        expert_outputs = jnp.einsum('bsd,edh->bseh', x, We) + be
        fused = jnp.einsum('bse,bseh->bsh', gate_weights, expert_outputs)
        return fused

    def _L1_attn_ref(x, WQ, WK, WV, WO):
        import jax, jax.numpy as jnp
        import numpy as np
        D_MODEL = 128
        NUM_HEADS = 16
        D_K = D_MODEL // NUM_HEADS
        BATCH, SEQ = (2, 256)
        B, S, E = x.shape
        mask = jnp.where(jnp.triu(jnp.ones((S, S), dtype=bool), k=1), -jnp.inf, 0.0).astype(x.dtype)

        def heads(W):
            return (x @ W).reshape(B, S, NUM_HEADS, D_K).transpose(0, 2, 1, 3)
        Q, K, V = (heads(WQ), heads(WK), heads(WV))
        score = jnp.einsum('bhqd,bhkd->bhqk', Q, K) / jnp.sqrt(jnp.asarray(D_K, x.dtype))
        score = score + mask
        score = score - jnp.max(score, axis=-1, keepdims=True)
        score = jnp.exp(score)
        score = score / jnp.sum(score, axis=-1, keepdims=True)
        out = jnp.einsum('bhqk,bhkd->bhqd', score, V)
        out = out.transpose(0, 2, 1, 3).reshape(B, S, E)
        return out @ WO

    def _L1_xattn_ref(query, kv, Wq, bq, Wkv, bkv, Wo, bo):
        import jax, jax.numpy as jnp
        import numpy as np
        import math
        EMBED = 128
        HEADS = 16
        HEAD_DIM = EMBED // HEADS

        def alibi_slopes(heads: int) -> jnp.ndarray:
            return jnp.asarray([2.0 ** (-8.0 * (h + 1) / heads) for h in range(heads)], dtype=jnp.float32)
        B, Nq, E = query.shape
        Nk = kv.shape[1]
        H, D = (HEADS, HEAD_DIM)
        q = query @ Wq + bq
        kvp = kv @ Wkv + bkv
        k, v = jnp.split(kvp, 2, axis=-1)
        q = q.reshape(B, Nq, H, D).transpose(0, 2, 1, 3)
        k = k.reshape(B, Nk, H, D).transpose(0, 2, 1, 3)
        v = v.reshape(B, Nk, H, D).transpose(0, 2, 1, 3)
        slopes = alibi_slopes(H)
        rel = jnp.abs(jnp.arange(Nk)[None, :] - jnp.arange(Nq)[:, None] - (Nk - Nq))
        bias = -slopes[:, None, None] * rel.astype(jnp.float32)
        scale = 1.0 / math.sqrt(D)
        scores = jnp.einsum('bhqd,bhkd->bhqk', q, k) * scale + bias[None]
        attn = jax.nn.softmax(scores, axis=-1)
        out = jnp.einsum('bhqk,bhkd->bhqd', attn, v)
        out = out.transpose(0, 2, 1, 3).reshape(B, Nq, E)
        return out @ Wo + bo

    def _L1_ffn_ref(x, Wg, bg, W1, b1, W2, b2):
        import jax, jax.numpy as jnp
        import numpy as np
        DIM = 128
        NUM_EXPERTS = 6
        TOP_K = 2
        HIDDEN = DIM * 2
        gate_logits = jnp.einsum('bsd,de->bse', x, Wg) + bg
        topk_w, topk_idx = jax.lax.top_k(gate_logits, TOP_K)
        topk_w = jax.nn.softmax(topk_w, axis=-1)
        combine = jnp.sum(jax.nn.one_hot(topk_idx, NUM_EXPERTS, dtype=x.dtype) * topk_w[..., None], axis=-2)
        h = jnp.einsum('bsd,edh->ebsh', x, W1) + b1[:, None, None, :]
        h = jax.nn.gelu(h, approximate=False)
        y = jnp.einsum('ebsh,ehd->ebsd', h, W2) + b2[:, None, None, :]
        out = jnp.einsum('ebsd,bse->bsd', y, combine)
        return out

    def _L2_attn_ref(batch, Wq, Wk, Wv, Wo, omega, W1, b1, W2, b2, gamma, beta):
        import jax, jax.numpy as jnp
        import numpy as np
        from functools import partial
        LN_EPS = 1000000.0
        FEAT_EPS = 1e-06

        def _layernorm(x, gamma, beta):
            mu = jnp.mean(x, axis=-1, keepdims=True)
            var = jnp.var(x, axis=-1, keepdims=True)
            return gamma * (x - mu) / jnp.sqrt(var + LN_EPS) + beta

        def _phi(x, omega):
            m = omega.shape[0]
            proj = jnp.einsum('bhsd,md->bhsm', x, omega)
            z = proj - 0.5 * jnp.sum(x * x, axis=-1, keepdims=True)
            z = z - jnp.max(z, axis=-1, keepdims=True)
            return jnp.exp(z) / jnp.sqrt(jnp.asarray(m, x.dtype)) + FEAT_EPS

        def _forward(batch, Wq, Wk, Wv, Wo, omega, W1, b1, W2, b2, gamma, beta):
            B, S, D = batch.shape
            M, dh = omega.shape
            H = D // dh
            scale = dh ** (-0.25)

            def heads(W):
                return (batch @ W).reshape(B, S, H, dh).transpose(0, 2, 1, 3)
            q = heads(Wq) * scale
            k = heads(Wk) * scale
            v = heads(Wv)
            qp = _phi(q, omega)
            kp = _phi(k, omega)
            qs = qp.transpose(2, 0, 1, 3)
            ks = kp.transpose(2, 0, 1, 3)
            vs = v.transpose(2, 0, 1, 3)

            def step(carry, qkv):
                S_kv, s_k = carry
                qt, kt, vt = qkv
                S_kv = S_kv + kt[..., :, None] * vt[..., None, :]
                s_k = s_k + kt
                num = jnp.einsum('bhm,bhmd->bhd', qt, S_kv)
                den = jnp.einsum('bhm,bhm->bh', qt, s_k)
                return ((S_kv, s_k), num / (den[..., None] + FEAT_EPS))
            carry0 = (jnp.zeros((B, H, M, dh), batch.dtype), jnp.zeros((B, H, M), batch.dtype))
            _, outs = jax.lax.scan(step, carry0, (qs, ks, vs))
            attn = outs.transpose(1, 0, 2, 3).reshape(B, S, D) @ Wo
            h = _layernorm(batch + attn, gamma, beta)
            out = jnp.maximum(h @ W1 + b1, 0.0) @ W2 + b2
            return out
        return _forward(batch, Wq, Wk, Wv, Wo, omega, W1, b1, W2, b2, gamma, beta)

    def _L2_xattn_ref(queries, keys, values, mask, Wq, bq, Wk, bk, Wv, bv, Wo, bo):
        import jax, jax.numpy as jnp
        import numpy as np
        EMBED = 128
        HEADS = 16
        HEAD_DIM = EMBED // HEADS
        B, Q, E = queries.shape
        K = keys.shape[1]
        q = (queries @ Wq.T + bq).reshape(B, Q, HEADS, HEAD_DIM)
        k = (keys @ Wk.T + bk).reshape(B, K, HEADS, HEAD_DIM)
        v = (values @ Wv.T + bv).reshape(B, K, HEADS, HEAD_DIM)
        energy = jnp.einsum('nqhd,nkhd->nhqk', q, k)
        energy = jnp.where(mask == 0, jnp.float32(-1e+20), energy)
        attn = jax.nn.softmax(energy / jnp.sqrt(jnp.float32(E)), axis=3)
        out = jnp.einsum('nhqk,nkhd->nqhd', attn, v).reshape(B, Q, E)
        return out @ Wo.T + bo

    def _L2_ffn_ref(x, gate_w, w_gate, w_up, w_down, sw_gate, sw_up, sw_down):
        import jax, jax.numpy as jnp
        import numpy as np
        B, L, D = (4, 128, 128)
        E, H, K = (16, 64, 8)
        EPS = 1e-12

        def _l2norm(v, axis=-1):
            n = jnp.sqrt(jnp.sum(v * v, axis=axis, keepdims=True))
            return v / jnp.maximum(n, EPS)
        if __name__ == '__main__':
            out = reference(**setup_inputs())
            print(out.shape)
        b, l, d = x.shape
        xf = x.reshape(-1, d)
        logits = _l2norm(xf) @ _l2norm(gate_w).T
        scores = jax.nn.sigmoid(logits)
        topk_scores, topk_idx = jax.lax.top_k(scores, K)
        topk_w = topk_scores / jnp.sum(topk_scores, axis=-1, keepdims=True)
        combine = jnp.sum(jax.nn.one_hot(topk_idx, E, dtype=xf.dtype) * topk_w[..., None], axis=1)
        g = jnp.einsum('nd,edh->neh', xf, w_gate)
        u = jnp.einsum('nd,edh->neh', xf, w_up)
        y = jnp.einsum('neh,ehd->ned', jax.nn.silu(g) * u, w_down)
        routed = jnp.einsum('ned,ne->nd', y, combine)
        shared = jax.nn.silu(xf @ sw_gate) * (xf @ sw_up) @ sw_down
        return (routed + shared).reshape(b, l, d)

    def _L3_attn_ref(X, W_KQV, W_O):
        import jax, jax.numpy as jnp
        import numpy as np
        from math import sqrt
        D_MODEL = 128
        NUM_HEADS = 16
        D_HEAD = D_MODEL // NUM_HEADS
        THETA = 10000.0

        def _rope(x, freqs):
            xr = x[..., ::2]
            xi = x[..., 1::2]
            cos = jnp.cos(freqs)
            sin = jnp.sin(freqs)
            yr = xr * cos - xi * sin
            yi = xr * sin + xi * cos
            return jnp.stack([yr, yi], axis=-1).reshape(x.shape)
        B, S, D = X.shape
        H, d = (NUM_HEADS, D_HEAD)
        KQV = jnp.einsum('bsd,ed->bse', X, W_KQV)
        K, Q, V = jnp.split(KQV, [D, 2 * D], axis=-1)

        def to_heads(t):
            return t.reshape(B, S, H, d).transpose(0, 2, 1, 3)
        K, Q, V = (to_heads(K), to_heads(Q), to_heads(V))
        inv_freq = 1.0 / THETA ** (jnp.arange(0, d, 2, dtype=jnp.float32) / d)
        pos = jnp.arange(S, dtype=jnp.float32)
        freqs = pos[:, None] * inv_freq[None, :]
        Q = _rope(Q, freqs)
        K = _rope(K, freqs)
        scores = jnp.einsum('bhqd,bhkd->bhqk', Q, K) / sqrt(d)
        causal = jnp.triu(jnp.ones((S, S), dtype=bool), k=1)
        scores = jnp.where(causal, -jnp.inf, scores)
        probs = jax.nn.softmax(scores, axis=-1)
        heads = jnp.einsum('bhqk,bhkd->bhqd', probs, V)
        acts = heads.transpose(0, 2, 1, 3).reshape(B, S, D)
        return jnp.einsum('bsd,ed->bse', acts, W_O)

    def _L3_xattn_ref(k, v, q, Wk, Wv, bv, Wq, bq, Wo, bo):
        import jax, jax.numpy as jnp
        import numpy as np
        D_MODEL = 128
        B, S = (4, 256)
        kp = jnp.einsum('bsd,ed->bse', k, Wk)
        vp = jnp.einsum('bsd,ed->bse', v, Wv) + bv
        qp = jnp.einsum('bsd,ed->bse', q, Wq) + bq
        scale = 1.0 / jnp.sqrt(jnp.float32(kp.shape[-1]))
        scores = jnp.einsum('bqd,bkd->bqk', qp, kp) * scale
        probs = jax.nn.softmax(scores, axis=-1)
        ctx = jnp.einsum('bqk,bkd->bqd', probs, vp)
        return jnp.einsum('bqd,ed->bqe', ctx, Wo) + bo

    def _L3_ffn_ref(x, routing_token, light_gamma, light_w1, light_b1, light_w2, light_b2, heavy_gamma, heavy_w1, heavy_b1, heavy_w2, heavy_b2):
        import jax, jax.numpy as jnp
        import numpy as np
        DIM = 128
        NUM_HEAVY = 128
        N_ITERS = 50
        EPS = 1.0
        FETCH_K_RATIO = 9.0 / 8.0

        def rms_norm(x, gamma):
            norm = jnp.maximum(jnp.linalg.norm(x, axis=-1, keepdims=True), 1e-12)
            return x / norm * x.shape[-1] ** 0.5 * gamma

        def feed_forward(x, gamma, w1, b1, w2, b2):
            h = jax.nn.gelu(rms_norm(x, gamma) @ w1 + b1, approximate=False)
            return h @ w2 + b2

        def coor_descent(s, k, n_iters, eps):
            logk = jnp.log(jnp.asarray(k, dtype=s.dtype))

            def step(ab, _):
                a, b = ab
                sb = (s + b) / eps
                a = eps * (logk - jax.scipy.special.logsumexp(sb, axis=-1, keepdims=True))
                b = -jax.nn.relu(s + a)
                return ((a, b), None)
            a0 = jnp.zeros_like(s[..., :1])
            b0 = -s
            (a, b), _ = jax.lax.scan(step, (a0, b0), None, length=n_iters)
            return jnp.exp((s + a + b) / eps)
        b, n, d = x.shape
        light_out = feed_forward(x, light_gamma, light_w1, light_b1, light_w2, light_b2)
        s = jnp.einsum('bnd,d->bn', x, routing_token)
        effective_k = min(NUM_HEAVY * FETCH_K_RATIO, n)
        scores = coor_descent(s, effective_k, N_ITERS, EPS)
        sel_scores, sel_idx = jax.lax.top_k(scores, NUM_HEAVY)
        sel_scores = sel_scores + jax.lax.stop_gradient(1.0 - sel_scores)
        routed = jnp.take_along_axis(x, sel_idx[..., None], axis=1)
        routed_out = feed_forward(routed, heavy_gamma, heavy_w1, heavy_b1, heavy_w2, heavy_b2)
        routed_out = routed_out * sel_scores[..., None]
        batch_idx = jnp.arange(b)[:, None]
        heavy_out = jnp.zeros_like(x).at[batch_idx, sel_idx].set(routed_out)
        return light_out + heavy_out
    x = x + _L0_attn_ref(_layernorm(x, axis=-1), L0_attn_Wi, L0_attn_Wf, L0_attn_Wg, L0_attn_Wo, L0_attn_ni, L0_attn_nf, L0_attn_ng, L0_attn_no, L0_attn_nout)
    x = x + _L0_xattn_ref(_layernorm(x, axis=-1), ctx_1024, ctx_1024, L0_xattn_Wq, L0_xattn_Wk, L0_xattn_Wv, L0_xattn_Wo, L0_xattn_q_norm_w, L0_xattn_k_norm_w)
    x = x + _L0_ffn_ref(_layernorm(x, axis=-1), L0_ffn_Wg, L0_ffn_bg, L0_ffn_We, L0_ffn_be)
    x = x + _L1_attn_ref(_layernorm(x, axis=-1), L1_attn_WQ, L1_attn_WK, L1_attn_WV, L1_attn_WO)
    x = x + _L1_xattn_ref(_layernorm(x, axis=-1), ctx_1024, L1_xattn_Wq, L1_xattn_bq, L1_xattn_Wkv, L1_xattn_bkv, L1_xattn_Wo, L1_xattn_bo)
    x = x + _L1_ffn_ref(_layernorm(x, axis=-1), L1_ffn_Wg, L1_ffn_bg, L1_ffn_W1, L1_ffn_b1, L1_ffn_W2, L1_ffn_b2)
    x = x + _L2_attn_ref(_layernorm(x, axis=-1), L2_attn_Wq, L2_attn_Wk, L2_attn_Wv, L2_attn_Wo, L2_attn_omega, L2_attn_W1, L2_attn_b1, L2_attn_W2, L2_attn_b2, L2_attn_gamma, L2_attn_beta)
    x = x + _L2_xattn_ref(_layernorm(x, axis=-1), ctx_1024, ctx_1024, mask_Bx1xSxS2_ik1, L2_xattn_Wq, L2_xattn_bq, L2_xattn_Wk, L2_xattn_bk, L2_xattn_Wv, L2_xattn_bv, L2_xattn_Wo, L2_xattn_bo)
    x = x + _L2_ffn_ref(_layernorm(x, axis=-1), L2_ffn_gate_w, L2_ffn_w_gate, L2_ffn_w_up, L2_ffn_w_down, L2_ffn_sw_gate, L2_ffn_sw_up, L2_ffn_sw_down)
    x = x + _L3_attn_ref(_layernorm(x, axis=-1), L3_attn_W_KQV, L3_attn_W_O)
    x = x + _L3_xattn_ref(ctx_1024, ctx_1024, _layernorm(x, axis=-1), L3_xattn_Wk, L3_xattn_Wv, L3_xattn_bv, L3_xattn_Wq, L3_xattn_bq, L3_xattn_Wo, L3_xattn_bo)
    x = x + _L3_ffn_ref(_layernorm(x, axis=-1), L3_ffn_routing_token, L3_ffn_light_gamma, L3_ffn_light_w1, L3_ffn_light_b1, L3_ffn_light_w2, L3_ffn_light_b2, L3_ffn_heavy_gamma, L3_ffn_heavy_w1, L3_ffn_heavy_b1, L3_ffn_heavy_w2, L3_ffn_heavy_b2)
    return x

_drawn_inputs = setup_inputs


def setup_inputs(seed=0):
    import zlib

    import numpy as np

    out = dict(_drawn_inputs(seed))
    spreads = {'L0_attn_ni': (1.0, 0.2),
     'L0_attn_nf': (1.0, 0.2),
     'L0_attn_ng': (1.0, 0.2),
     'L0_attn_no': (1.0, 0.2),
     'L0_attn_nout': (1.0, 0.2),
     'L0_xattn_k_norm_w': (1.0, 0.2),
     'L0_ffn_bg': (0.0, 0.1),
     'L0_ffn_be': (0.0, 0.1),
     'L1_xattn_bq': (0.0, 2.0),
     'L1_xattn_bkv': (0.0, 0.316),
     'L1_xattn_bo': (0.0, 0.1),
     'L2_attn_b1': (0.0, 0.336),
     'L2_attn_b2': (0.0, 0.1),
     'L2_attn_gamma': (1.0, 0.6),
     'L2_attn_beta': (0.0, 0.8),
     'L3_xattn_bv': (0.0, 0.1),
     'L3_xattn_bq': (0.0, 0.49),
     'L3_xattn_bo': (0.0, 0.1),
     'L3_ffn_light_gamma': (1.0, 0.6),
     'L3_ffn_light_b1': (0.0, 0.404),
     'L3_ffn_light_b2': (0.0, 0.1),
     'L3_ffn_heavy_gamma': (1.0, 0.6),
     'L3_ffn_heavy_b1': (0.0, 0.411),
     'L3_ffn_heavy_b2': (0.0, 0.1)}
    factors = {'L0_xattn_q_norm_w': 2.974,
     'L1_xattn_Wq': 56.897,
     'L1_ffn_b1': 4.77,
     'L2_attn_Wq': 64.0,
     'L2_attn_Wk': 64.0,
     'L2_attn_Wv': 64.0,
     'L2_attn_Wo': 64.0,
     'L2_attn_omega': 64.0,
     'L2_attn_W1': 8.0,
     'L2_xattn_bq': 8.0,
     'L2_xattn_bk': 64.0,
     'L1_ffn_b2': 2.776}
    for name, (base, spread) in spreads.items():
        noise = np.random.default_rng([zlib.crc32(name.encode()), seed]).standard_normal(out[name].shape)
        drawn = base * np.exp(spread * noise) if base else spread * noise
        out[name] = jnp.asarray(drawn.astype(out[name].dtype))
    for name, factor in factors.items():
        out[name] = (out[name] * factor).astype(out[name].dtype)
    return out
```

```python
from contextlib import ExitStack

import numpy as np

import concourse.bass as bass
from concourse import mybir

F32 = mybir.dt.float32
BF16 = mybir.dt.bfloat16
I32 = mybir.dt.int32
ALU = mybir.AluOpType
ACT = mybir.ActivationFunctionType
AX = mybir.AxisListType

P = 128
B = 8
GB = 4
GROUPS = B // GB
W4 = GB * P
H = 16
HD = P // H
HG = 4
E0, E1, E2, K2 = 8, 6, 16, 8
HID1 = 256
HE2 = 64
MH, MD = 2, 64
MAGIC = 12582912.0
NEG = -1.0e30
LAYERS = ["pre", "L0a", "L0x", "L0f", "L1a", "L1x", "L1f", "L2a", "L2x", "L2f", "L3a", "L3x", "L3f"]
DESCENT = 50
PICKED = float(min(128 * 9 // 8, P))
STAGES = 12


def weight_plan():
    return {
        "L0a": [("L0a_w", 4 * P), ("L2f_gw", P)],
        "L0x": [("L0x_wq", P), ("L0x_wk", P), ("L0x_wv", P), ("L0x_wo", P)],
        "L0f": [("L0f_wg", E0), ("L0f_we", E0 * P), ("L0f_be", P)],
        "L1a": [("L1a_wq", P), ("L1a_wk", P), ("L1a_wv", P), ("L1a_wo", P)],
        "L1x": [("L1x_wq", P), ("L1x_wk", P), ("L1x_wv", P), ("L1x_wo", P)],
        "L1f": [("L1f_wg", E1), ("L1f_w1", E1 * HID1), ("L1f_w2", E1 * 2 * P), ("L1f_b2", P)],
        "L2a": [("L2a_wq", P), ("L2a_wk", P), ("L2a_wv", P), ("L2a_wo", P), ("L2a_om", P),
                ("L2a_w1", 4 * P), ("L2a_w2", 4 * P)],
        "L2x": [("L2x_wq", P), ("L2x_wk", P), ("L2x_wv", P), ("L2x_wo", P)],
        "L2f": [("L2f_wg", E2 * HE2), ("L2f_wu", E2 * HE2), ("L2f_wd", E2 * HE2),
                ("L2f_sg", HE2), ("L2f_su", HE2), ("L2f_sd", P)],
        "L3a": [("L3a_wk", P), ("L3a_wq", P), ("L3a_wv", P), ("L3a_wo", P)],
        "L3x": [("L3x_wq", P), ("L3x_wk", P), ("L3x_wv", P), ("L3x_wo", P)],
        "L3f": [("L3f_lw1", HE2), ("L3f_lw2", P), ("L3f_hw1", 4 * P), ("L3f_hw2", 4 * P), ("L3f_rt", 1)],
    }


ROWS = [("ni", P), ("nf", P), ("ng", P), ("nout", P), ("no", P), ("qn", HD), ("kn", HD), ("bg0", E0), ("bg1", E1),
        ("L1x_bv", P), ("L1x_bo", P), ("L2a_b2", P), ("L2x_bv", P), ("L2x_bo", P), ("L3x_bv", P), ("L3x_bo", P),
        ("L3f_lb2", P), ("L3f_hb2", P)]
COLS = [("L1x_bq", 1), ("L1x_bk", 1), ("L2x_bq", 1), ("L2x_bk", 1), ("L3x_bq", 1), ("L1f_b1", 2 * E1),
        ("L2a_b1", 4), ("gamma", 1), ("beta", 1), ("L3f_lg", 1), ("L3f_lb1", 1), ("L3f_hg", 1), ("L3f_hb1", 4)]
CONSTS = [("ident", P), ("heads", H), ("c0", HD), ("s0", HD), ("c3", HD), ("s3", HD), ("keepT", P), ("tri", E0 * E0), ("ident3", E2),
          ("causal", P), ("alibi", H * P)]
BCONSTS = [("identb", P)]


def offsets(plan):
    at, out = 0, {}
    for name, n in plan:
        out[name] = (at, n)
        at += n
    return out, at


WPLAN = weight_plan()
WOFF, NW = offsets([x for v in WPLAN.values() for x in v])
ROFF, NR = offsets(ROWS)
COFF, NC = offsets(COLS)
KOFF, NK = offsets(CONSTS)
BOFF, NB = offsets(BCONSTS)


def weave(*programs):
    at = [next(p, None) for p in programs]
    while any(a is not None for a in at):
        i = min((a, i) for i, a in enumerate(at) if a is not None)[1]
        at[i] = next(programs[i], None)


def build(nc, x_d, ctx_d, mask_d, w_d, r_d, c_d, k_d, b_d, out_d, marks):
    stack = ExitStack()
    known = dict(marks)

    def sb(name, shape, dt=F32):
        return stack.enter_context(nc.sbuf_tensor(name, shape, dt))

    wt = sb("wt", [P, NW])
    rowt = sb("rowt", [P, NR])
    colt = sb("colt", [P, NC])
    kt = sb("kt", [P, NK])
    bt = sb("bt", [P, NB], BF16)
    ones = sb("ones", [P, P])
    negh = sb("negh", [P, GB])
    wtern = sb("wtern", [P, 4 * P], BF16)
    wabs, wmean, wrec = sb("wabs", [P, 4]), sb("wmean", [P, 4]), sb("wrec", [P, 4])
    wsc = sb("wsc", [P, 4])
    wtmp = sb("wtmp", [P, 4 * P])
    cw = [sb(f"cw{n}", [P, HD]) for n in range(2)]
    sw = [sb(f"sw{n}", [P, HD]) for n in range(2)]
    gwT = sb("gwT", [P, E2])
    gwn = sb("gwn", [E2, P])
    gsc = sb("gsc", [E2, 2])
    pairs = sb("pairs", [3 * E2, E2 * HE2], BF16)
    rt_s = sb("rt_s", [P, B])
    rt_r = sb("rt_r", [B, P])
    rt_b, rt_e, rt_k = sb("rt_b", [B, P]), sb("rt_e", [B, P]), sb("rt_k", [B, P])
    rt_u = sb("rt_u", [B, 2])
    rt_f = sb("rt_f", [P, B])

    class Tiles:

        def __init__(self, g):
            def own(name, shape, dt=F32):
                return sb(f"{name}{g}", shape, dt)
            self.x = own("x", [P, GB, P])
            self.xn = own("xn", [P, GB, P])
            self.xnT = own("xnT", [P, W4])
            self.ctxT = own("ctxT", [P, W4])
            self.st, self.mv = own("st", [P, GB, 6]), own("mv", [P, GB, 2])
            self.ve, self.rs = own("ve", [P, GB]), own("rs", [P, GB])
            self.tc, self.td = own("tc", [P, GB, P]), own("td", [P, GB, P])
            big = own("big", [P, 8 * W4])
            self.pr = big[:, 0:4 * W4].rearrange("p (h k) -> p h k", k=P)
            self.PT = big[:, 4 * W4:8 * W4].rearrange("p (h k) -> p h k", k=P)
            self.hid = big[:, :].rearrange("p (n c) -> p n c", c=W4)
            self.ta, self.tb = self.PT[:, 0:12, :], self.PT[:, 12:16, :]
            self.s12, self.s12b, self.deq = own("s12", [P, 12]), own("s12b", [P, 12]), own("deq", [P, 12])
            self.ndeq = own("ndeq", [P, 4])
            self.s4, self.s4b = own("s4", [P, 8]), own("s4b", [P, 8])
            self.v2, self.y2, self.h2 = (own(n, [P, 2 * GB * H]) for n in ("v2", "y2", "h2"))
            qk = own("qk", [P, 2 * W4])
            self.QT, self.KT = qk[:, 0:W4], qk[:, W4:2 * W4]
            self.qT3 = qk[:, :].bitcast(BF16)[:, 0:3 * W4].rearrange("p (j n) -> p j n", j=3)
            self.KTm = own("KTm", [P, 2, H // 2, P])
            self.vaug = own("vaug", [P, GB, H, HD + 1])
            self.vv = own("vv", [P, GB, MH, MD + 1])
            self.mx, self.rc = own("mx", [P, 2, H // 2]), own("rc", [P, H])
            self.co, self.coT = own("co", [P, GB, P]), own("coT", [P, W4])
            self.cin = self.co
            self.mask = self.coT[:, :].bitcast(I32).rearrange("p (b k) -> p b k", b=GB)
            self.dmask = own("dmask", [P, GB, P], BF16)
            self.lg, self.lgm = own("lg", [P, GB, E2]), own("lgm", [P, GB, E2])
            self.sel, self.gw = own("sel", [P, GB, E2]), own("gw", [P, GB, E2])
            self.gws = own("gws", [P, GB, 3, E2], BF16)
            self.gt, self.eq = own("gt", [P, GB, E0, E0]), own("eq", [P, GB, E0, E0])
            self.m8 = own("m8", [P, GB, 8])
            self.gwTT = own("gwTT", [E2, W4])
            self.gwsT = own("gwsT", [3 * E2, W4], BF16)

    tiles = [Tiles(g) for g in range(GROUPS)]
    ps = stack.enter_context(nc.psum_tensor("ps", [P, 8 * 512], F32))

    def banks_of(g):
        def bank(i, n=1):
            return ps[:, (4 * g + i) * 512:(4 * g + i + n) * 512]
        return bank

    def w(name, rows=P):
        at, n = WOFF[name]
        return wt[0:rows, at:at + n]

    def row(name, rows=P):
        at, n = ROFF[name]
        return rowt[0:rows, at:at + n]

    def col(name, i=0, rows=P):
        return colt[0:rows, COFF[name][0] + i:COFF[name][0] + i + 1]

    def const(name):
        at, n = KOFF[name]
        return kt[:, at:at + n]

    def four(t):
        return t.rearrange("p (b d) -> p b d", b=GB)

    ident = const("ident")
    identb = bt[:, BOFF["identb"][0]:BOFF["identb"][0] + P]
    causal = const("causal")
    alibi = const("alibi").rearrange("p (h k) -> p h k", h=H)

    loaded = {n: stack.enter_context(nc.semaphore(f"loaded_{n}"))
              for n in list(WPLAN) + ["rows", "consts", "alibi", "x0", "x1", "ctx0", "ctx1", "mask0", "mask1"]}
    stored = stack.enter_context(nc.semaphore("stored"))
    descent = stack.enter_context(nc.semaphore("descent_step"))
    semaphores = {f"pre_{e}": stack.enter_context(nc.semaphore(f"pre_{e}")) for e in ("tensor", "vector", "gpsimd")}
    semaphores |= {f"{l}_{e}{g}": stack.enter_context(nc.semaphore(f"{l}_{e}{g}"))
                   for l in LAYERS[1:] for e in ("tensor", "vector", "scalar", "gpsimd") for g in range(GROUPS)}

    class Steps:

        def __init__(self, who, group=None):
            self.who, self.group, self.count = who, group, {}

        def begin(self, layer):
            self.layer = layer
            self.sem = f"{layer}_{self.who}" + ("" if self.group is None else str(self.group))

        def step(self, name=None):
            n = self.count[self.sem] = self.count.get(self.sem, 0) + 1
            if name is not None:
                marks[self.group, f"{self.layer}.{name}"] = (self.sem, n)
            return semaphores[self.sem], 1

        def at(self, name, group=None):
            g = None if name.startswith("pre.") else self.group if group is None else group
            sem, n = known.get((g, name), ("pre_vector", 1))
            return semaphores[sem], n

        def last(self, back=0):
            return semaphores[self.sem], self.count[self.sem] - back

    def beat(g, u, k=0):
        return 20 + 10 * u + 5 * g + k

    SCALES = {l: float(P if l == "L2x" else HD) ** -0.5 for l in ("L0x", "L1a", "L1x", "L2x", "L3a")}
    UNITS = 2 * GB
    HH = H // 2
    OW = HD + 1
    LAST_BIAS = {"L1x": "L1x_bo", "L2a": "L2a_b2", "L2x": "L2x_bo", "L3x": "L3x_bo", "L3f": "L3f_lb2"}

    def keys_of(t, b):
        return t.KT[:, b * P:(b + 1) * P].unsqueeze(1).to_broadcast([P, HH, P])

    def heads_of(u):
        return const("heads")[:, (u % 2) * HH:(u % 2 + 1) * HH].unsqueeze(2).to_broadcast([P, HH, P])

    block = stack.enter_context(nc.Block())

    @block.sync
    def _(sp):
        def load_group(g):
            t, mine = tiles[g], slice(g * GB, (g + 1) * GB)
            sp.dma_start(t.x[:, :, :], x_d[mine, :, :].rearrange("b p d -> p b d")).then_inc(loaded[f"x{g}"], 16)
            sp.dma_start(t.cin[:, :, :], ctx_d[mine, :, :].rearrange("b p d -> p b d")).then_inc(loaded[f"ctx{g}"], 16)
            sp.dma_start(t.mask, mask_d[mine, :, :].rearrange("b p d -> p b d")).then_inc(loaded[f"mask{g}"], 16)

        def load_weights(l):
            at = WOFF[WPLAN[l][0][0]][0]
            n = sum(c for _, c in WPLAN[l])
            sp.dma_start(wt[:, at:at + n], w_d[:, at:at + n]).then_inc(loaded[l], 16)

        sp.dma_start(tiles[0].x[:, :, :], x_d[0:GB, :, :].rearrange("b p d -> p b d")).then_inc(loaded["x0"], 16)
        sp.dma_start(tiles[1].x[:, :, :], x_d[GB:B, :, :].rearrange("b p d -> p b d")).then_inc(loaded["x1"], 16)
        sp.dma_start(rowt[:, :], r_d.to_broadcast([P, NR])).then_inc(loaded["rows"], 16)
        sp.dma_start(colt[:, :], c_d).then_inc(loaded["rows"], 16)
        load_weights("L0a")
        first = KOFF["alibi"][0]
        sp.dma_start(kt[:, 0:first], k_d[:, 0:first]).then_inc(loaded["consts"], 16)
        sp.dma_start(bt[:, :], b_d).then_inc(loaded["consts"], 16)
        for g in range(GROUPS):
            t, mine = tiles[g], slice(g * GB, (g + 1) * GB)
            sp.dma_start(t.cin[:, :, :], ctx_d[mine, :, :].rearrange("b p d -> p b d")).then_inc(loaded[f"ctx{g}"], 16)
            sp.dma_start(t.mask, mask_d[mine, :, :].rearrange("b p d -> p b d")).then_inc(loaded[f"mask{g}"], 16)
        for l in list(WPLAN)[1:]:
            load_weights(l)
            if l == "L1a":
                sp.dma_start(kt[:, first:], k_d[:, first:]).then_inc(loaded["alibi"], 16)
        s = [Steps("sync", g) for g in range(GROUPS)]
        for g in range(GROUPS):
            sp.wait_ge(*s[g].at(f"{LAYERS[STAGES]}.x"))
            sp.dma_start(out_d[g * GB:(g + 1) * GB, :, :].rearrange("b p d -> p b d"), tiles[g].x[:, :, :]).then_inc(stored, 16)
        sp.wait_ge(stored, 16 * GROUPS)

    @block.gpsimd
    def _(pool):
        p = Steps("gpsimd")
        p.begin("pre")
        pool.memset(negh[:, :], -0.5).then_inc(*p.step("negh"))
        pool.memset(ones[:, :], 1.0).then_inc(*p.step("ones"))
        for t in tiles:
            pool.memset(t.vaug[:, :, :, :], 1.0).then_inc(*p.step("vaug"))
            pool.memset(t.vv[:, :, :, :], 1.0).then_inc(*p.step("vv"))
        pool.memset(rt_k[:, :], 1.0 / PICKED).then_inc(*p.step("rt_k"))
        pool.wait_ge(*p.last())

        def program(g):
            s, t = Steps("gpsimd", g), tiles[g]

            def rsqrt(out, src, name):
                pool.wait_ge(*s.at(f"{s.layer}.{name}"))
                pool.tensor_tensor(out, src, negh[:, :], ALU.pow).then_inc(*s.step(name + "_r"))

            def spread_keys(n, l):
                first = 0 if l in ("L1x", "L2x") else 1
                for u in range(first, UNITS):
                    b = u // 2
                    yield n, ((1 if first == 0 else 19) if u < 2 else beat(g, 0, 1) if u == 2 else beat(g, u - 3, 3))
                    if u == first:
                        pool.wait_ge(*s.at(f"{l}.KT"))
                    if u >= 2:
                        pool.wait_ge(*s.at(f"{l}.S{u - 2}"))
                    pool.tensor_tensor(t.KTm[:, u % 2, :, :], keys_of(t, b), heads_of(u), ALU.mult).then_inc(*s.step(f"keys{u}"))
                    if u == 1:
                        yield from add_bias(n, 19, l)

            def add_bias(n, phase, l):
                if l in LAST_BIAS:
                    yield n, phase
                    pool.wait_ge(*s.at(f"{l}.xn"))
                    pool.tensor_tensor(t.x[:, :, :], t.x[:, :, :], row(LAST_BIAS[l]).unsqueeze(1).to_broadcast([P, GB, P]), ALU.add)\
                        .then_inc(*s.step("xb"))

            for n, l in enumerate(LAYERS[1:STAGES + 1]):
                s.begin(l)
                yield n, 0
                rsqrt(t.rs[:, :], t.ve[:, :], "var")
                if l == "L0a":
                    for k, name in ((2, "ms"), (11, "ms1"), (12, "ms2")):
                        yield n, k
                        rsqrt(t.s4b[:, 0:GB], t.s4[:, 0:GB], name)
                        if g == 0 and k == 2:
                            pool.wait_ge(*p.at("pre.gss"))
                            pool.tensor_tensor(gsc[:, 1:2], gsc[:, 0:1], negh[0:E2, 0:1], ALU.pow).then_inc(*p.step("gss_r"))
                if l in ("L2a", "L3x"):
                    yield from add_bias(n, 4, l)
                if l == "L2a":
                    yield n, 30
                    rsqrt(t.rs[:, :], t.ve[:, :], "var2")
                if l in ("L0x", "L1a", "L1x", "L2x", "L3a"):
                    yield from spread_keys(n, l)
                if l in ("L2f", "L3f"):
                    yield n, 2
                    rsqrt(t.s4b[:, 0:GB], t.s4[:, 0:GB], "ms")
                    yield from add_bias(n, 4, l)
        weave(*(program(g) for g in range(GROUPS)))

    @block.tensor
    def _(pe):
        def mm(out, lhsT, rhs, start=True, stop=True, **k):
            return pe.matmul(out, lhsT, rhs, start=start, stop=stop, **k)

        p = Steps("tensor")
        p.begin("pre")
        pe.wait_ge(*p.at("pre.ones"))
        pe.wait_ge(*p.at("pre.wabs"))
        mm(ps[:, 0:4], ones[:, :], wabs[:, :]).then_inc(*p.step("wsum"))
        pe.wait_ge(loaded["consts"], 32)
        pe.wait_ge(*p.at("pre.gwn"))
        pe.transpose(ps[:, 512:512 + E2], gwn[:, :], ident[0:E2, 0:E2]).then_inc(*p.step("gwTp"))
        pe.wait_ge(*p.at("pre.gwT"))

        def program(g):
            s, t, bank = Steps("tensor", g), tiles[g], banks_of(g)
            x, xn, xnT, ctxT, QT, KT, pr, PT, hid = t.x, t.xn, t.xnT, t.ctxT, t.QT, t.KT, t.pr, t.PT, t.hid

            def seq(bk, b):
                return bank(bk)[:, b * P:(b + 1) * P]

            def turn_rows(bk, src, name):
                for b in range(GB):
                    ins = pe.transpose(seq(bk, b), src[:, b, :], ident)
                ins.then_inc(*s.step(name))

            def project_rows(bk, srcT, weight, name):
                for b in range(GB):
                    ins = mm(seq(bk, b), srcT[:, b * P:(b + 1) * P], weight)
                ins.then_inc(*s.step(name))

            def project_cols(bk, srcT, weight, name):
                mm(bank(bk), weight, srcT[:, :]).then_inc(*s.step(name))

            def attend(n, l):
                def scores(u):
                    b = u // 2
                    pe.wait_ge(*s.at(f"{l}.keys{u}"))
                    for i in range(2):
                        ins = mm(bank(i), QT[:, b * P:(b + 1) * P], t.KTm[:, u % 2, HG * i:HG * i + HG, :])
                    ins.then_inc(*s.step(f"S{u}"))

                def turned(u, i):
                    if u + i:
                        pe.wait_ge(*s.at(f"{l}.PT{u - 1 + i}.{1 - i}"))
                    for j in range(HG):
                        ins = pe.transpose(seq(2, j), pr[:, (u % 2) * HH + HG * i + j, :], ident)
                    ins.then_inc(*s.step(f"T{u}.{i}"))

                def weighted(u, i):
                    b, half = divmod(u, 2)
                    if i == 0:
                        if half == 0 and b:
                            pe.wait_ge(*s.at(f"{l}.co{b - 1}"))
                        pe.wait_ge(*s.at(f"{l}.PT{u}.1"))
                    for j in range(HG * i, HG * i + HG):
                        h = HH * half + j
                        ins = mm(bank(3)[:, h * OW:(h + 1) * OW], PT[:, (u % 2) * HH + j, :], t.vaug[:, b, h, :])
                    if i == 1:
                        ins.then_inc(*s.step(f"O{u}"))

                yield n, 20
                pe.wait_ge(*s.at(f"{l}.QT"))
                pe.wait_ge(*s.at(f"{l}.KT"))
                pe.wait_ge(*s.at(f"{l}.vaug"))
                scores(0)
                for u in range(UNITS):
                    if u + 1 < UNITS:
                        yield n, beat(g, u, 2)
                        pe.wait_ge(*s.at(f"{l}.masked{u}"))
                        scores(u + 1)
                    yield n, beat(g, u, 4)
                    for i in range(2):
                        pe.wait_ge(*s.at(f"{l}.exp{u}.{i}"))
                        turned(u, i)
                        if u:
                            weighted(u - 1, i)
                yield n, beat(g, UNITS)
                for i in range(2):
                    weighted(UNITS - 1, i)

            def out_proj(n, l, weight, turn=2, out=0):
                yield n, 130
                pe.wait_ge(*s.at(f"{l}.co{GB - 1}"))
                turn_rows(turn, t.co, "coTp")
                yield n, 131
                pe.wait_ge(*s.at(f"{l}.coT"))
                project_rows(out, t.coT, weight, "y")

            def gates(bk, weight, n):
                for b in range(GB):
                    ins = mm(bank(bk)[:, b * n:(b + 1) * n], xnT[:, b * P:(b + 1) * P], weight)
                ins.then_inc(*s.step("lg"))

            def gate_bias(n, l, k, bias):
                yield n, 12
                pe.wait_ge(*s.at(f"{l}.gw"))
                for b in range(GB):
                    ins = pe.transpose(bank(3)[0:k, b * P:(b + 1) * P], t.gw[:, b, 0:k], ident)
                ins.then_inc(*s.step("gwTp"))
                yield n, 14
                pe.wait_ge(*s.at(f"{l}.gwT"))
                for b in range(GB):
                    ins = mm(seq(3, b), t.gwTT[0:k, b * P:(b + 1) * P], bias)
                ins.then_inc(*s.step("gb"))

            for n, l in enumerate(LAYERS[1:STAGES + 1]):
                s.begin(l)
                if l != "L0a":
                    yield n, 0
                    if g == 0:
                        pe.wait_ge(loaded[l], 16)
                if l in ("L0x", "L1x", "L2x", "L3x"):
                    if l == "L0x":
                        pe.wait_ge(*s.at("L0a.x"))
                        project_rows(1, ctxT, w("L0x_wk"), "k")
                    else:
                        project_cols(1, ctxT, w(f"{l}_wk"), "k")
                    project_rows(2, ctxT, w(f"{l}_wv"), "v")
                if l != "L0a":
                    yield n, 2
                    pe.wait_ge(*s.at(f"{l}.xn"))
                    turn_rows(3, xn, "xnTp")
                if l == "L0a":
                    yield n, 2
                    pe.wait_ge(loaded[f"ctx{g}"], 16)
                    turn_rows(3, t.cin, "cTp")
                    yield n, 4
                    pe.wait_ge(*s.at("L0a.q3"))
                    for j in range(3):
                        for b in range(GB):
                            ins = pe.transpose(seq(j, b), t.ta[:, j * GB + b, :], ident)
                    ins.then_inc(*s.step("q3Tp"))
                    yield n, 6
                    pe.wait_ge(*s.at("L0a.q3T"))
                    for j in range(3):
                        for b in range(GB):
                            ins = mm(seq(j, b), t.qT3[:, j, b * P:(b + 1) * P], wtern[:, j * P:(j + 1) * P])
                    ins.then_inc(*s.step("ifg"))
                    yield n, 14
                    pe.wait_ge(*s.at("L0a.ctxT"))
                    pe.wait_ge(*s.at("L0a.qo"))
                    turn_rows(3, t.ta, "qoTp")
                    yield n, 16
                    pe.wait_ge(*s.at("L0a.qoT"))
                    for b in range(GB):
                        ins = mm(seq(1, b), t.qT3[:, 0, b * P:(b + 1) * P], wtern[:, 3 * P:4 * P])
                    ins.then_inc(*s.step("y"))
                if l in ("L0x", "L3a"):
                    yield n, 4
                    pe.wait_ge(*s.at(f"{l}.xnT"))
                    project_rows(0, xnT, w(f"{l}_wq"), "q")
                    if l == "L3a":
                        project_rows(1, xnT, w("L3a_wk"), "k")
                        project_rows(2, xnT, w("L3a_wv"), "v")
                    yield n, 8
                    pe.wait_ge(*s.at(f"{l}.qrot"))
                    turn_rows(0, t.tc, "QTp")
                    pe.wait_ge(*s.at(f"{l}.krot"))
                    turn_rows(1, t.td, "KTp")
                    yield from attend(n, l)
                    yield from out_proj(n, l, w(f"{l}_wo"))
                if l in ("L1a", "L1x", "L2x"):
                    yield n, 4
                    pe.wait_ge(*s.at(f"{l}.xnT"))
                    project_cols(0, xnT, w(f"{l}_wq"), "q")
                    if l == "L1a":
                        project_cols(1, xnT, w("L1a_wk"), "k")
                        project_rows(2, xnT, w("L1a_wv"), "v")
                    yield from attend(n, l)
                    yield from out_proj(n, l, w(f"{l}_wo"))
                if l == "L0f":
                    yield n, 4
                    pe.wait_ge(*s.at("L0f.xnT"))
                    gates(3, w("L0f_wg"), E0)
                    for e in range(E0):
                        yield n, (5 if e < 3 else 10 + 4 * e)
                        if e >= 3:
                            pe.wait_ge(*s.at(f"L0f.x{e - 3}.{GB - 1}"))
                        for b in range(GB):
                            ins = mm(seq(e % 3, b), xnT[:, b * P:(b + 1) * P], w("L0f_we")[:, e * P:(e + 1) * P])
                        ins.then_inc(*s.step(f"e{e}"))
                        if e == 2:
                            yield from gate_bias(n, l, E0, w("L0f_be", E0))
                if l == "L1f":
                    yield n, 4
                    pe.wait_ge(*s.at("L1f.xnT"))
                    gates(3, w("L1f_wg"), E1)

                    def hidden(e):
                        for c in range(2):
                            k = 2 * e + c
                            if k >= 2:
                                pe.wait_ge(*s.at(f"L1f.h{k - 2}"))
                            mm(bank(c), w("L1f_w1")[:, k * P:(k + 1) * P], xnT[:, :]).then_inc(*s.step(f"a{k}"))
                    yield n, 10
                    hidden(0)
                    yield from gate_bias(n, l, E1, w("L1f_b2", E1))
                    for e in range(E1):
                        yield n, 20 + 4 * e
                        if e + 1 < E1:
                            hidden(e + 1)
                        yield n, 22 + 4 * e
                        pe.wait_ge(*s.at(f"L1f.h{2 * e + 1}"))
                        if e:
                            pe.wait_ge(*s.at(f"L1f.x{e - 1}.{GB - 1}"))
                        for b in range(GB):
                            for c in range(2):
                                ins = mm(seq(2, b), hid[:, 2 * (e % 2) + c, b * P:(b + 1) * P],
                                         w("L1f_w2")[:, (2 * e + c) * P:(2 * e + c + 1) * P], start=c == 0, stop=c == 1)
                        ins.then_inc(*s.step(f"e{e}"))
                if l == "L2a":
                    yield n, 4
                    pe.wait_ge(*s.at("L2a.xnT"))
                    project_cols(0, xnT, w("L2a_wq"), "q")
                    project_cols(1, xnT, w("L2a_wk"), "k")
                    project_rows(2, xnT, w("L2a_wv"), "v")
                    for m, src in enumerate((QT, KT)):
                        yield n, 6 + 2 * m
                        pe.wait_ge(*s.at(f"L2a.{'QK'[m]}T"))
                        pe.wait_ge(*s.at("L2a.v1"))
                        for h in range(MH):
                            r = slice(MD * h, MD * h + MD)
                            for b in range(GB):
                                ins = mm(seq(2 - 2 * m + h, b), src[r, b * P:(b + 1) * P], w("L2a_om")[r, :],
                                         tile_position=(MD * h, 0))
                        ins.then_inc(*s.step(f"z{m}"))
                    for m in range(2):
                        yield n, 14 + 2 * m
                        pe.wait_ge(*s.at(f"L2a.phi{m}"))
                        for h in range(MH):
                            for b in range(GB):
                                ins = pe.transpose(seq(2 - 2 * m + h, b), pr[:, 8 * m + GB * h + b, :], ident)
                        ins.then_inc(*s.step(f"phiTp{m}"))
                    yield n, 18
                    pe.wait_ge(*s.at("L2a.phiT0"))
                    pe.wait_ge(*s.at("L2a.phiT1"))
                    for h in range(MH):
                        for b in range(GB):
                            ins = mm(seq(2 + h, b), PT[:, 8 + GB * h + b, :], PT[:, GB * h + b, :])
                        ins.then_inc(*s.step(f"A{h}"))
                    for h in range(MH):
                        yield n, 20 + h
                        pe.wait_ge(*s.at(f"L2a.Am{h}"))
                        for b in range(GB):
                            ins = mm(bank(h)[:, b * (MD + 1):(b + 1) * (MD + 1)], pr[:, GB * h + b, :], t.vv[:, b, h, :])
                        ins.then_inc(*s.step(f"O{h}"))
                    yield n, 24
                    pe.wait_ge(*s.at("L2a.co3"))
                    turn_rows(2, t.co, "coTp")
                    yield n, 26
                    pe.wait_ge(*s.at("L2a.coT"))
                    project_rows(3, t.coT, w("L2a_wo"), "y")
                    yield n, 32
                    pe.wait_ge(*s.at("L2a.hn"))
                    turn_rows(2, t.tc, "hTp")
                    yield n, 34
                    pe.wait_ge(*s.at("L2a.hT"))
                    for c in range(4):
                        mm(bank(c), w("L2a_w1")[:, c * P:(c + 1) * P], KT).then_inc(*s.step(f"f{c}"))
                    yield n, 36
                    pe.wait_ge(*s.at("L2a.g3"))
                    for b in range(GB):
                        for c in range(4):
                            ins = mm(seq(0, b), hid[:, c, b * P:(b + 1) * P], w("L2a_w2")[:, c * P:(c + 1) * P], start=c == 0, stop=c == 3)
                    ins.then_inc(*s.step("y2"))
                if l == "L2f":
                    yield n, 4
                    pe.wait_ge(*s.at("L2f.xnT"))
                    gates(0, gwT[:, :], E2)
                    yield n, 8
                    pe.wait_ge(*s.at("L2f.gws"))
                    gwsTp = bank(1).bitcast(BF16)
                    for b in range(GB):
                        ins = pe.transpose(gwsTp[0:3 * E2, b * P:(b + 1) * P], t.gws[:, b, :, :].rearrange("p s e -> p (s e)"), identb)
                    ins.then_inc(*s.step("gwsTp"))
                    yield n, 10
                    pe.wait_ge(*s.at("L2f.gwsT"))
                    for c in range(10):
                        yield n, 20 + 4 * c
                        if 1 <= c < 9:
                            pe.wait_ge(*s.at(f"L2f.act{c - 1}"))
                        r = P if c < 8 else HE2
                        if c < 9:
                            mm(bank(0)[0:r, :], w("L2f_wg")[:, c * P:(c + 1) * P] if c < 8 else w("L2f_sg"), xnT[:, :])
                            ins = mm(bank(1)[0:r, :], w("L2f_wu")[:, c * P:(c + 1) * P] if c < 8 else w("L2f_su"), xnT[:, :])
                            if c < 8:
                                ins = mm(bank(2), pairs[:, c * P:(c + 1) * P], t.gwsT[:, :])
                            ins.then_inc(*s.step(f"gu{c}"))
                        if c >= 1:
                            d = c - 1
                            r = P if d < 8 else HE2
                            if d == 8:
                                pe.wait_ge(*s.at("L2f.act8"))
                            for b in range(GB):
                                ins = mm(seq(3, b), hid[0:r, d % 4, b * P:(b + 1) * P],
                                         w("L2f_wd")[:, d * P:(d + 1) * P] if d < 8 else w("L2f_sd", HE2),
                                         start=(d == 0 and b == 0), stop=(d == 8 and b == GB - 1), skip_group_check=True)
                            if d == 8:
                                ins.then_inc(*s.step("y"))
                if l == "L3x":
                    yield n, 4
                    pe.wait_ge(*s.at("L3x.xnT"))
                    project_cols(0, xnT, w("L3x_wq"), "q")
                    yield n, 6
                    pe.wait_ge(*s.at("L3x.QT"))
                    pe.wait_ge(*s.at("L3x.KT"))
                    for b in range(GB):
                        ins = mm(seq(3, b), QT[:, b * P:(b + 1) * P], KT[:, b * P:(b + 1) * P])
                    ins.then_inc(*s.step("S"))
                    yield n, 10
                    pe.wait_ge(*s.at("L3x.p"))
                    turn_rows(0, pr, "Tp")
                    yield n, 12
                    pe.wait_ge(*s.at("L3x.V"))
                    pe.wait_ge(*s.at("L3x.PT"))
                    for b in range(GB):
                        ins = mm(seq(1, b), t.tc[:, b, :], PT[:, b, :])
                    ins.then_inc(*s.step("O"))
                    yield n, 14
                    pe.wait_ge(*s.at("L3x.coT"))
                    project_rows(2, t.coT, w("L3x_wo"), "y")
                if l == "L3f":
                    yield n, 4
                    pe.wait_ge(*s.at("L3f.xnT"))
                    for b in range(GB):
                        ins = mm(bank(2)[:, b:b + 1], xnT[:, b * P:(b + 1) * P], w("L3f_rt"))
                    ins.then_inc(*s.step("s"))
                    pe.wait_ge(*s.at("L3f.xr"))
                    turn_rows(3, t.tc, "xrTp")
                    yield n, 8
                    if g == GROUPS - 1:
                        pe.wait_ge(*s.at("L3f.rs", 0))
                        pe.wait_ge(*s.at("L3f.rs"))
                        pe.transpose(bank(2)[0:B, 0:P], rt_s[:, :], ident).then_inc(*s.step("sT"))
                    yield n, 9
                    pe.wait_ge(*s.at("L3f.lT"))
                    pe.wait_ge(*s.at("L3f.hT"))
                    mm(bank(0)[0:HE2, :], w("L3f_lw1"), QT).then_inc(*s.step("a0"))
                    if g == GROUPS - 1:
                        pe.wait_ge(*s.at("L3f.smin"))
                    else:
                        pe.wait_ge(*s.at("L3f.rs"))
                    for c in range(4):
                        if c == 3:
                            yield n, 12
                            pe.wait_ge(*s.at("L3f.h0"))
                        mm(bank((c + 1) % 4), w("L3f_hw1")[:, c * P:(c + 1) * P], KT).then_inc(*s.step(f"a{c + 1}"))
                    yield n, 14
                    pe.wait_ge(*s.at("L3f.h4"))
                    for b in range(GB):
                        mm(seq(1, b), hid[0:HE2, 4, b * P:(b + 1) * P], w("L3f_lw2", HE2))
                    for b in range(GB):
                        for c in range(4):
                            mm(seq(2, b), hid[:, c, b * P:(b + 1) * P], w("L3f_hw2")[:, c * P:(c + 1) * P], start=c == 0, stop=False)
                        ins = mm(seq(2, b), ones[0:1, :], row("L3f_hb2", 1), start=False)
                    ins.then_inc(*s.step("y"))
                    if g == GROUPS - 1:
                        yield n, 16
                        pe.wait_ge(*s.at("L3f.f"))
                        pe.transpose(bank(3)[:, 0:B], rt_e[:, :], ident[0:B, 0:B]).then_inc(*s.step("fT"))
        weave(*(program(g) for g in range(GROUPS)))

    @block.scalar
    def _(act):
        p = Steps("scalar")
        act.wait_ge(loaded["rows"], 32)
        act.wait_ge(loaded["consts"], 32)
        act.wait_ge(*p.at("pre.vv"))

        def program(g):
            s, t, bank = Steps("scalar", g), tiles[g], banks_of(g)
            QT, KT, pr, PT, hid, tc = t.QT, t.KT, t.pr, t.PT, t.hid, t.tc

            def read(out, src, need, name):
                act.wait_ge(*s.at(f"{s.layer}.{need}"))
                act.activation(out, src, ACT.Copy).then_inc(*s.step(name))

            def values():
                act.wait_ge(*s.at(f"{s.layer}.v"))
                act.activation(t.vaug[:, :, :, 0:HD], bank(2).rearrange("p (b h d) -> p b h d", b=GB, h=H), ACT.Copy)\
                   .then_inc(*s.step("vaug"))

            def attend(n, l):
                for u in range(UNITS):
                    yield n, beat(g, u, 3)
                    act.wait_ge(*s.at(f"{l}.top{u}"))
                    for j in range(HH):
                        P_h = pr[:, (u % 2) * HH + j, :]
                        act.activation(P_h, P_h, ACT.Exp, scale=SCALES[l], bias=t.mx[:, u % 2, j:j + 1]).then_inc(*s.step(f"exp{u}.{j // HG}"))
                    for i in range(2):
                        yield n, beat(g, u, 4 + i)
                        if u >= 2 and i == 0:
                            act.wait_ge(*s.at(f"{l}.O{u - 2}"))
                        at = (u % 2) * HH + HG * i
                        read(PT[:, at:at + HG, :], bank(2).rearrange("p (j k) -> p j k", j=HG), f"T{u}.{i}", f"PT{u}.{i}")
                yield n, 130
                read(t.coT[:, :], bank(2), "coTp", "coT")

            for n, l in enumerate(LAYERS[1:STAGES + 1]):
                s.begin(l)
                if l in ("L1x", "L2x", "L3x"):
                    yield n, 1
                    act.wait_ge(*s.at(f"{l}.k"))
                    if l == "L3x":
                        act.activation(KT, bank(1), ACT.Copy).then_inc(*s.step("KT"))
                    else:
                        act.activation(KT, bank(1), ACT.Identity, bias=col(f"{l}_bk")).then_inc(*s.step("KT"))
                if l == "L0x":
                    yield n, 1
                    values()
                yield n, 2
                if l != "L0a":
                    read(t.xnT[:, :], bank(3), "xnTp", "xnT")
                if l == "L0a":
                    read(t.ctxT[:, :], bank(3), "cTp", "ctxT")
                    yield n, 7
                    act.wait_ge(*s.at("L0a.ndeq"))
                    act.wait_ge(*s.at("L0a.ifg"))
                    for b in range(GB):
                        act.activation(tc[:, b, :], bank(1)[:, b * P:(b + 1) * P], ACT.Exp, scale=t.ndeq[:, b:b + 1]).then_inc(*s.step("ef"))
                    yield n, 9
                    act.wait_ge(*s.at("L0a.efc"))
                    act.activation(tc[:, :, :], tc[:, :, :], ACT.Ln, bias=1.0).then_inc(*s.step("ln"))
                    yield n, 10
                    act.wait_ge(*s.last())
                    act.activation(tc[:, :, :], tc[:, :, :], ACT.Exp, scale=-float(P)).then_inc(*s.step("f128"))
                if l in ("L0x", "L3a"):
                    yield n, 5
                    if l == "L0x":
                        for m, nm in ((1, "k"), (0, "q")):
                            act.wait_ge(*s.at(f"L0x.{nm}"))
                            act.activation(t.ta[:, m * GB:m * GB + GB, :], four(bank(m)), ACT.Square).then_inc(*s.step(f"{nm}sq"))
                    if l == "L3a":
                        values()
                    yield n, 9
                    read(QT, bank(0), "QTp", "QT")
                    read(KT, bank(1), "KTp", "KT")
                    yield from attend(n, l)
                if l in ("L1a", "L1x", "L2x"):
                    yield n, 5
                    act.wait_ge(*s.at(f"{l}.q"))
                    if l == "L1a":
                        act.activation(QT, bank(0), ACT.Copy).then_inc(*s.step("QT"))
                    else:
                        act.activation(QT, bank(0), ACT.Identity, bias=col(f"{l}_bq")).then_inc(*s.step("QT"))
                    if l == "L1a":
                        read(KT, bank(1), "k", "KT")
                        values()
                    yield from attend(n, l)
                if l in ("L0f", "L1f"):
                    k = E0 if l == "L0f" else E1
                    yield n, 8
                    act.wait_ge(*s.at(f"{l}.lgs"))
                    act.activation(t.lgm[:, :, 0:k], t.lgm[:, :, 0:k], ACT.Exp).then_inc(*s.step("lge"))
                    if l == "L1f":
                        for i in range(2):
                            yield n, 11
                            act.wait_ge(*s.at(f"L1f.a{i}"))
                            act.activation(hid[:, i, :], bank(i), ACT.Gelu, bias=col("L1f_b1", i)).then_inc(*s.step(f"h{i}"))
                    yield n, 13
                    read(t.gwTT[0:k, :], bank(3)[0:k, :], "gwTp", "gwT")
                if l == "L1f":
                    for i in range(2, 2 * E1):
                        e, c = divmod(i, 2)
                        yield n, 16 + 4 * e
                        act.wait_ge(*s.at(f"L1f.a{i}"))
                        if e >= 2:
                            act.wait_ge(*s.at(f"L1f.e{e - 2}"))
                        act.activation(hid[:, 2 * (e % 2) + c, :], bank(c), ACT.Gelu, bias=col("L1f_b1", i)).then_inc(*s.step(f"h{i}"))
                if l == "L2a":
                    yield n, 5
                    for m, (dst, nm) in enumerate(((QT, "q"), (KT, "k"))):
                        act.wait_ge(*s.at(f"L2a.{nm}"))
                        act.activation(dst, bank(m), ACT.Copy, scale=float(MD) ** -0.25).then_inc(*s.step(nm.upper() + "T"))
                    act.wait_ge(*s.at("L2a.v"))
                    act.activation(t.vv[:, :, :, 0:MD], bank(2).rearrange("p (b h d) -> p b h d", b=GB, h=MH), ACT.Copy).then_inc(*s.step("v1"))
                    for m in range(2):
                        yield n, 10 + m
                        act.wait_ge(*s.at(f"L2a.zs{m}"))
                        act.activation(pr[:, 8 * m:8 * m + 8, :], pr[:, 8 * m:8 * m + 8, :], ACT.Exp).then_inc(*s.step(f"ze{m}"))
                    for m in range(2):
                        yield n, 15 + 2 * m
                        act.wait_ge(*s.at(f"L2a.phiTp{m}"))
                        act.activation(PT[:, 8 * m:8 * m + 8, :], bank(2 - 2 * m, 2).rearrange("p (h k) -> p h k", k=P), ACT.Copy)\
                           .then_inc(*s.step(f"phiT{m}"))
                    yield n, 25
                    read(t.coT[:, :], bank(2), "coTp", "coT")
                    yield n, 33
                    act.wait_ge(*s.at("L2a.hTp"))
                    act.activation(KT, bank(2), ACT.Identity, bias=col("beta"), scale=col("gamma")).then_inc(*s.step("hT"))
                    yield n, 35
                    for c in range(4):
                        act.wait_ge(*s.at(f"L2a.f{c}"))
                        act.activation(hid[:, c, :], bank(c), ACT.Relu, bias=col("L2a_b1", c)).then_inc(*s.step(f"g{c}"))
                if l == "L2f":
                    yield n, 6
                    act.wait_ge(*s.at("L2f.lgs"))
                    act.activation(t.lgm[:, :, :], t.lgm[:, :, :], ACT.Exp, scale=-1.0).then_inc(*s.step("lge"))
                    yield n, 9
                    read(t.gwsT[:, :], bank(1).bitcast(BF16)[0:3 * E2, 0:W4], "gwsTp", "gwsT")
                    for c in range(9):
                        r = P if c < 8 else HE2
                        yield n, 21 + 4 * c
                        act.wait_ge(*s.at(f"L2f.gu{c}"))
                        act.activation(hid[0:r, 4 + c % 2, :], bank(0)[0:r, :], ACT.Silu).then_inc(*s.step(f"silu{c}"))
                if l == "L3x":
                    yield n, 5
                    act.wait_ge(*s.at("L3x.q"))
                    act.activation(QT, bank(0), ACT.Identity, bias=col("L3x_bq")).then_inc(*s.step("QT"))
                    yield n, 8
                    act.wait_ge(*s.at("L3x.sub"))
                    act.activation(pr[:, 0:GB, :], pr[:, 0:GB, :], ACT.Exp, scale=float(P) ** -0.5).then_inc(*s.step("exp"))
                    yield n, 11
                    read(PT[:, 0:GB, :], four(bank(0)), "Tp", "PT")
                    yield n, 13
                    read(t.coT[:, :], bank(1), "O", "coT")
                if l == "L3f":
                    yield n, 7
                    act.wait_ge(*s.at("L3f.xrTp"))
                    act.activation(QT, bank(3), ACT.Copy, scale=col("L3f_lg")).then_inc(*s.step("lT"))
                    act.activation(KT, bank(3), ACT.Copy, scale=col("L3f_hg")).then_inc(*s.step("hT"))
                    if g == GROUPS - 1:
                        yield n, 9
                        act.wait_ge(*s.at("L3f.smin"))
                        act.activation(rt_e[:, :], rt_r[:, :], ACT.Exp).then_inc(*s.step("E"))
                    yield n, 10
                    act.wait_ge(*s.at("L3f.a0"))
                    act.activation(hid[0:HE2, 4, :], bank(0)[0:HE2, :], ACT.Gelu, bias=col("L3f_lb1", 0, HE2)).then_inc(*s.step("h0"))
                    for c in range(4):
                        if c == 3:
                            yield n, 13
                        act.wait_ge(*s.at(f"L3f.a{c + 1}"))
                        act.activation(hid[:, c, :], bank((c + 1) % 4), ACT.Gelu, bias=col("L3f_hb1", c)).then_inc(*s.step(f"h{c + 1}"))
        weave(*(program(g) for g in range(GROUPS)))

    @block.vector
    def _(dve):
        def wide(v, n=P):
            return v.unsqueeze(2).to_broadcast([P, v.shape[1], n])

        def over(v, n=GB):
            return v.unsqueeze(1).to_broadcast([P, n, v.shape[1]])

        p = Steps("vector")
        p.begin("pre")

        def prologue():
            dve.wait_ge(loaded["L0a"], 16)
            dve.wait_ge(loaded["rows"], 32)
            dve.wait_ge(loaded["consts"], 32)
            wv = w("L0a_w").rearrange("p (m n) -> p m n", m=4)
            dve.tensor_reduce(wabs[:, :], wv, AX.X, ALU.add, apply_absolute_value=True).then_inc(*p.step("wabs"))
            half = HD // 2
            for n, c in enumerate((row("qn"), row("kn"))):
                dve.tensor_tensor(cw[n][:, :], const("c0"), c, ALU.mult).then_inc(*p.step())
                dve.tensor_tensor(sw[n][:, 0:half], const("s0")[:, 0:half], c[:, half:HD], ALU.mult).then_inc(*p.step())
                dve.tensor_tensor(sw[n][:, half:HD], const("s0")[:, half:HD], c[:, 0:half], ALU.mult).then_inc(*p.step())
            dve.tensor_copy(pairs[:, :].rearrange("p (e k) -> p e k", e=E2),
                            const("ident3")[0:3 * E2, :].unsqueeze(2).to_broadcast([3 * E2, E2, HE2])).then_inc(*p.step("pairs"))
            gwr = w("L2f_gw", E2)
            dve.tensor_tensor(gwn[:, :], gwr, gwr, ALU.mult).then_inc(*p.step())
            dve.wait_ge(*p.last())
            dve.tensor_reduce(gsc[:, 0:1], gwn[:, :], AX.X, ALU.add).then_inc(*p.step())
            dve.wait_ge(*p.last())
            dve.tensor_scalar(gsc[:, 0:1], gsc[:, 0:1], 1e-24, None, ALU.max).then_inc(*p.step("gss"))
            dve.wait_ge(*p.at("pre.wsum"))
            dve.tensor_scalar(wmean[:, :], ps[:, 0:4], 1.0 / (P * P), 1e-5, ALU.mult, ALU.max).then_inc(*p.step())
            dve.wait_ge(*p.last())
            dve.tensor_scalar(wsc[:, :], wmean[:, :], 1.0 / 127.0, None, ALU.mult).then_inc(*p.step())
            dve.reciprocal(wrec[:, :], wmean[:, :]).then_inc(*p.step())
            dve.wait_ge(*p.last())
            wtv = wtmp[:, :].rearrange("p (m n) -> p m n", m=4)
            for m in range(4):
                dve.tensor_scalar(wtv[:, m, :], wv[:, m, :], wrec[:, m:m + 1], MAGIC, ALU.mult, ALU.add).then_inc(*p.step())
            dve.wait_ge(*p.last())
            dve.tensor_scalar(wtmp[:, :], wtmp[:, :], MAGIC, 1.0, ALU.subtract, ALU.min).then_inc(*p.step())
            dve.wait_ge(*p.last())
            dve.tensor_scalar(wtern[:, :], wtmp[:, :], -1.0, None, ALU.max).then_inc(*p.step("wtern"))
            dve.wait_ge(*p.at("pre.gss_r"))
            dve.tensor_scalar(gwn[:, :], gwr, gsc[:, 1:2], None, ALU.mult).then_inc(*p.step("gwn"))
            dve.wait_ge(*p.at("pre.gwTp"))
            dve.tensor_copy(gwT[:, :], ps[:, 512:512 + E2]).then_inc(*p.step("gwT"))

        def program(g):
            s, t, bank = Steps("vector", g), tiles[g], banks_of(g)
            x, xn, tc, td, ta, tb, s4, s4b, s12, s12b, deq = t.x, t.xn, t.tc, t.td, t.ta, t.tb, t.s4, t.s4b, t.s12, t.s12b, t.deq
            pr, PT, hid, lg, lgm, sel, gw, gt, eq, qT3 = t.pr, t.PT, t.hid, t.lg, t.lgm, t.sel, t.gw, t.gt, t.eq, t.qT3

            def variance(src, eps, name):
                for b in range(GB):
                    dve.bn_stats(t.st[:, b, :], src[:, b, :]).then_inc(*s.step())
                for b in range(GB):
                    dve.wait_ge(*s.last(GB - 1))
                    dve.bn_aggr(t.mv[:, b, :], t.st[:, b, :]).then_inc(*s.step())
                dve.wait_ge(*s.last())
                dve.tensor_scalar(t.ve[:, :], t.mv[:, :, 1], eps, None, ALU.add).then_inc(*s.step(name))

            def mean_square(src, eps, name):
                dve.tensor_tensor(tb, src, src, ALU.mult).then_inc(*s.step())
                dve.wait_ge(*s.last())
                dve.tensor_reduce(s4[:, 0:GB], tb, AX.X, ALU.add).then_inc(*s.step())
                dve.wait_ge(*s.last())
                dve.tensor_scalar(s4[:, 0:GB], s4[:, 0:GB], 1.0 / P, eps, ALU.mult, ALU.add).then_inc(*s.step(name))

            def by_rms(dst, src):
                for b in range(GB):
                    dve.tensor_scalar(dst[:, b, :], src[:, b, :], s4b[:, b:b + 1], None, ALU.mult).then_inc(*s.step())
                dve.wait_ge(*s.last())

            def quantise(k, name):
                dve.tensor_reduce(s12[:, 0:k], ta[:, 0:k, :], AX.X, ALU.max, apply_absolute_value=True).then_inc(*s.step())
                dve.wait_ge(*s.last())
                dve.tensor_scalar(s12[:, 0:k], s12[:, 0:k], 1e-5, None, ALU.max).then_inc(*s.step())
                dve.wait_ge(*s.last())
                dve.reciprocal(s12b[:, 0:k], s12[:, 0:k]).then_inc(*s.step())
                dve.wait_ge(*s.last())
                dve.tensor_scalar(s12b[:, 0:k], s12b[:, 0:k], 127.0, None, ALU.mult).then_inc(*s.step())
                dve.wait_ge(*s.last())
                for i in range(k):
                    dve.tensor_scalar(ta[:, i, :], ta[:, i, :], s12b[:, i:i + 1], MAGIC, ALU.mult, ALU.add).then_inc(*s.step())
                dve.wait_ge(*s.last())
                dve.tensor_scalar(ta[:, 0:k, :], ta[:, 0:k, :], MAGIC, 127.0, ALU.subtract, ALU.min).then_inc(*s.step(name))

            def rotate(v, cos, sin, out, name, swap):
                h = GB * H
                tmp = ta[:, 8:12, :].rearrange("p b (h d) -> p (b h) d", h=H)
                o = out[:, :, :].rearrange("p b (h d) -> p (b h) d", h=H)
                dve.tensor_tensor(o, v, cos.unsqueeze(1).to_broadcast([P, h, HD]), ALU.mult).then_inc(*s.step())
                one, two = (slice(0, HD // 2), slice(HD // 2, HD)) if swap == "half" else (slice(0, HD, 2), slice(1, HD, 2))
                for a, b in ((one, two), (two, one)):
                    dve.tensor_tensor(tmp[:, :, a], v[:, :, b], sin[:, a].unsqueeze(1).to_broadcast([P, h, HD // 2]), ALU.mult).then_inc(*s.step())
                dve.wait_ge(*s.last())
                dve.tensor_tensor(out[:, :, :], out[:, :, :], ta[:, 8:12, :], ALU.add).then_inc(*s.step(name))
                dve.wait_ge(*s.last())

            def attend(n, l):
                def normal(b):
                    dve.wait_ge(*s.at(f"{l}.O{2 * b + 1}"))
                    O = bank(3)[:, 0:H * OW].rearrange("p (h d) -> p h d", h=H)
                    dve.reciprocal(t.rc[:, :], O[:, :, HD]).then_inc(*s.step())
                    dve.wait_ge(*s.last())
                    dve.tensor_tensor(t.co[:, b, :].rearrange("p (h d) -> p h d", h=H), O[:, :, 0:HD],
                                      wide(t.rc[:, :], HD), ALU.mult).then_inc(*s.step(f"co{b}"))

                if l in ("L0x", "L1a", "L3a"):
                    yield n, 19
                    dve.wait_ge(*s.at(f"{l}.KT"))
                    dve.tensor_tensor(t.KTm[:, 0, :, :], keys_of(t, 0), heads_of(0), ALU.mult).then_inc(*s.step("keys0"))
                if l in ("L1x", "L2x"):
                    yield n, 3
                    dve.wait_ge(*s.at(f"{l}.v"))
                    for b in range(GB):
                        dve.tensor_tensor(t.vaug[:, b, :, 0:HD], bank(2)[:, b * P:(b + 1) * P].rearrange("p (h d) -> p h d", h=H),
                                          row(f"{l}_bv").rearrange("p (h d) -> p h d", h=H), ALU.add).then_inc(*s.step("vaug"))
                if l == "L1x" and g == 0:
                    dve.wait_ge(loaded["alibi"], 16)
                for u in range(UNITS):
                    yield n, beat(g, u, 1)
                    dve.wait_ge(*s.at(f"{l}.S{u}"))
                    if u >= 2:
                        dve.wait_ge(*s.at(f"{l}.T{u - 2}.1"))
                    b, half = divmod(u, 2)
                    S, mine = bank(0, 2).rearrange("p (h k) -> p h k", h=HH), pr[:, half * HH:(half + 1) * HH, :]
                    mask = alibi[:, half * HH:(half + 1) * HH, :] if l == "L1x" else over(t.dmask[:, b, :] if l == "L2x" else causal, HH)
                    dve.tensor_tensor(mine, S, mask, ALU.add).then_inc(*s.step(f"masked{u}"))
                    dve.wait_ge(*s.last())
                    dve.tensor_reduce(t.mx[:, half, :], mine, AX.X, ALU.max).then_inc(*s.step())
                    dve.wait_ge(*s.last())
                    dve.tensor_scalar(t.mx[:, half, :], t.mx[:, half, :], -SCALES[l], None, ALU.mult).then_inc(*s.step(f"top{u}"))
                    if u >= 3 and u % 2 == 1:
                        yield n, beat(g, u, 3)
                        normal(u // 2 - 1)
                yield n, beat(g, UNITS, 1)
                normal(GB - 1)

            def add(n, l, bk, need="y", name="x"):
                yield n, 200
                dve.wait_ge(*s.at(f"{l}.{need}"))
                if l in LAST_BIAS:
                    dve.wait_ge(*s.at(f"{l}.xb"))
                dve.tensor_tensor(x[:, :, :], four(bank(bk)), x[:, :, :], ALU.add).then_inc(*s.step(name))
                dve.wait_ge(*s.last())

            def top2(n, l, k, bias):
                yield n, 6
                dve.wait_ge(*s.at(f"{l}.lg"))
                L = lg[:, :, 0:k]
                dve.tensor_tensor(L, bank(3)[:, 0:GB * k].rearrange("p (b e) -> p b e", b=GB), over(row(bias)), ALU.add).then_inc(*s.step())
                dve.wait_ge(*s.last())
                dve.tensor_reduce(s4[:, 0:GB], L, AX.X, ALU.max).then_inc(*s.step())
                dve.wait_ge(*s.last())
                dve.tensor_tensor(lgm[:, :, 0:k], L, wide(s4[:, 0:GB], k), ALU.subtract).then_inc(*s.step("lgs"))
                mine = L.unsqueeze(3).to_broadcast([P, GB, k, k])
                other = L.unsqueeze(2).to_broadcast([P, GB, k, k])
                tri = const("tri").rearrange("p (a c) -> p a c", a=E0)[:, 0:k, 0:k]
                dve.tensor_tensor(gt[:, :, 0:k, 0:k], other, mine, ALU.is_gt).then_inc(*s.step())
                dve.tensor_tensor(eq[:, :, 0:k, 0:k], other, mine, ALU.is_equal).then_inc(*s.step())
                dve.wait_ge(*s.last())
                for b in range(GB):
                    dve.tensor_tensor(eq[:, b, 0:k, 0:k], eq[:, b, 0:k, 0:k], tri, ALU.mult).then_inc(*s.step())
                dve.wait_ge(*s.last())
                for b in range(GB):
                    dve.tensor_tensor(gt[:, b, 0:k, 0:k], gt[:, b, 0:k, 0:k], eq[:, b, 0:k, 0:k], ALU.add).then_inc(*s.step())
                dve.wait_ge(*s.last())
                for b in range(GB):
                    dve.tensor_reduce(sel[:, b, 0:k], gt[:, b, 0:k, 0:k], AX.X, ALU.add).then_inc(*s.step())
                dve.wait_ge(*s.last())
                yield n, 11
                dve.wait_ge(*s.at(f"{l}.lge"))
                dve.scalar_tensor_tensor(gw[:, :, 0:k], sel[:, :, 0:k], 2.0, lgm[:, :, 0:k], ALU.is_lt, ALU.mult).then_inc(*s.step())
                dve.wait_ge(*s.last())
                dve.tensor_reduce(s4[:, 0:GB], gw[:, :, 0:k], AX.X, ALU.add).then_inc(*s.step())
                dve.wait_ge(*s.last())
                dve.reciprocal(s4b[:, 0:GB], s4[:, 0:GB]).then_inc(*s.step())
                dve.wait_ge(*s.last())
                dve.tensor_tensor(gw[:, :, 0:k], gw[:, :, 0:k], wide(s4b[:, 0:GB], k), ALU.mult).then_inc(*s.step("gw"))
                dve.wait_ge(*s.last())

            def mix(n, l, k, banks, phase):
                for e in range(k):
                    yield n, phase(e)
                    dve.wait_ge(*s.at(f"{l}.e{e}"))
                    for b in range(GB):
                        dve.wait_ge(*s.last(GB - 1))
                        dve.scalar_tensor_tensor(x[:, b, :], bank(banks[e])[:, b * P:(b + 1) * P], gw[:, b, e:e + 1], x[:, b, :],
                                                 ALU.mult, ALU.add).then_inc(*s.step(f"x{e}.{b}"))
                dve.wait_ge(*s.last())
                yield from add(n, l, 3, "gb")

            for n, l in enumerate(LAYERS[1:STAGES + 1]):
                s.begin(l)
                yield n, 0
                if l == "L0a":
                    dve.wait_ge(loaded[f"x{g}"], 16)
                variance(x, 1e-5, "var")
                yield n, 1
                dve.wait_ge(*s.at(f"{l}.var_r"))
                for b in range(GB):
                    dve.tensor_scalar(xn[:, b, :], x[:, b, :], t.mv[:, b, 0:1], t.rs[:, b:b + 1], ALU.subtract, ALU.mult).then_inc(*s.step("xn"))
                if l == "L0a":
                    yield n, 2
                    dve.wait_ge(*s.last())
                    mean_square(xn[:, :, :], 1e-8, "ms")
                    if g == 0:
                        prologue()
                    yield n, 3
                    dve.wait_ge(loaded[f"mask{g}"], 16)
                    dve.tensor_scalar(t.dmask[:, :, :], t.mask, 0.0, -1e20, ALU.is_equal, ALU.mult).then_inc(*s.step("dmask"))
                    dve.wait_ge(*s.at("L0a.ms_r"))
                    by_rms(tc, xn)
                    for j, nm in enumerate(("ni", "nf", "ng")):
                        dve.tensor_tensor(ta[:, j * GB:(j + 1) * GB, :], tc[:, :, :], over(row(nm)), ALU.mult).then_inc(*s.step())
                    dve.wait_ge(*s.last())
                    quantise(12, "q3")
                    for j in range(3):
                        dve.tensor_scalar(deq[:, j * GB:(j + 1) * GB], s12[:, j * GB:(j + 1) * GB], wsc[:, j:j + 1], None, ALU.mult).then_inc(*s.step())
                    dve.wait_ge(*s.last())
                    dve.tensor_scalar(t.ndeq[:, :], deq[:, GB:2 * GB], -1.0, None, ALU.mult).then_inc(*s.step("ndeq"))
                    yield n, 5
                    dve.wait_ge(*s.at("L0a.q3Tp"))
                    dve.tensor_scalar(qT3, bank(0, 3).rearrange("p (j n) -> p j n", j=3), -128.0, None, ALU.max).then_inc(*s.step("q3T"))
                    yield n, 8
                    dve.wait_ge(*s.at("L0a.ef"))
                    dve.tensor_scalar(tc[:, :, :], tc[:, :, :], 1e18, None, ALU.min).then_inc(*s.step("efc"))
                    yield n, 11
                    dve.wait_ge(*s.at("L0a.f128"))
                    dve.tensor_scalar(tc[:, :, :], tc[:, :, :], -1.0, 1.0, ALU.mult, ALU.add).then_inc(*s.step())
                    dve.wait_ge(*s.last())
                    dve.tensor_tensor(tc[:, :, :], four(bank(2)), tc[:, :, :], ALU.mult).then_inc(*s.step())
                    dve.wait_ge(*s.last())
                    dve.tensor_reduce(s4[:, 0:GB], tc[:, :, :], AX.X, ALU.add).then_inc(*s.step())
                    dve.wait_ge(*s.last())
                    dve.tensor_tensor(s4[:, 0:GB], s4[:, 0:GB], deq[:, 2 * GB:3 * GB], ALU.mult).then_inc(*s.step())
                    dve.wait_ge(*s.last())
                    dve.tensor_tensor(s4[:, 0:GB], s4[:, 0:GB], deq[:, 0:GB], ALU.mult).then_inc(*s.step())
                    dve.wait_ge(*s.last())
                    for b in range(GB):
                        dve.tensor_scalar(td[:, b, :], bank(0)[:, b * P:(b + 1) * P], s4[:, b:b + 1], None, ALU.mult).then_inc(*s.step())
                    dve.wait_ge(*s.last())
                    mean_square(td[:, :, :], 1.1920929e-07, "ms1")
                    yield n, 12
                    dve.wait_ge(*s.at("L0a.ms1_r"))
                    by_rms(td, td)
                    dve.tensor_tensor(td[:, :, :], td[:, :, :], over(row("nout")), ALU.mult).then_inc(*s.step())
                    dve.wait_ge(*s.last())
                    mean_square(td[:, :, :], 1e-8, "ms2")
                    yield n, 13
                    dve.wait_ge(*s.at("L0a.ms2_r"))
                    by_rms(td, td)
                    dve.tensor_tensor(ta[:, 0:GB, :], td[:, :, :], over(row("no")), ALU.mult).then_inc(*s.step())
                    dve.wait_ge(*s.last())
                    quantise(GB, "qo")
                    dve.tensor_scalar(deq[:, 0:GB], s12[:, 0:GB], wsc[:, 3:4], None, ALU.mult).then_inc(*s.step())
                    yield n, 15
                    dve.wait_ge(*s.at("L0a.qoTp"))
                    dve.tensor_scalar(qT3[:, 0, :], bank(3), -128.0, None, ALU.max).then_inc(*s.step("qoT"))
                    dve.wait_ge(*s.last())
                    yield n, 17
                    dve.wait_ge(*s.at("L0a.y"))
                    for b in range(GB):
                        dve.scalar_tensor_tensor(x[:, b, :], bank(1)[:, b * P:(b + 1) * P], deq[:, b:b + 1], x[:, b, :],
                                                 ALU.mult, ALU.add).then_inc(*s.step("x"))
                    dve.wait_ge(*s.last())
                if l == "L0x":
                    v2, y2, h2, hh = t.v2, t.y2, t.h2, GB * H
                    yield n, 6
                    dve.wait_ge(*s.last())
                    for m, nm in ((0, "q"), (1, "k")):
                        dve.wait_ge(*s.at(f"L0x.{nm}sq"))
                        v = ta[:, m * GB:m * GB + GB, :].rearrange("p b (h d) -> p (b h) d", h=H)
                        dve.tensor_reduce(v2[:, m * hh:(m + 1) * hh], v, AX.X, ALU.add).then_inc(*s.step())
                    dve.wait_ge(*s.last())
                    dve.tensor_scalar(v2[:, :], v2[:, :], 1.0 / HD, 1e-10, ALU.mult, ALU.add).then_inc(*s.step())
                    dve.wait_ge(*s.last())
                    dve.tensor_scalar(h2[:, :].bitcast(I32), v2[:, :].bitcast(I32), 1, None, ALU.logical_shift_right).then_inc(*s.step())
                    dve.wait_ge(*s.last())
                    dve.tensor_scalar(y2[:, :].bitcast(I32), h2[:, :].bitcast(I32), -1.0, float(0x5F3759DF), ALU.mult, ALU.add).then_inc(*s.step())
                    dve.wait_ge(*s.last())
                    for _ in range(3):
                        dve.tensor_tensor(h2[:, :], y2[:, :], y2[:, :], ALU.mult).then_inc(*s.step())
                        dve.wait_ge(*s.last())
                        dve.scalar_tensor_tensor(h2[:, :], h2[:, :], -0.5, v2[:, :], ALU.mult, ALU.mult).then_inc(*s.step())
                        dve.wait_ge(*s.last())
                        dve.scalar_tensor_tensor(y2[:, :], h2[:, :], 1.5, y2[:, :], ALU.add, ALU.mult).then_inc(*s.step())
                        dve.wait_ge(*s.last())
                    for m, nm, out in ((0, "q", tc), (1, "k", td)):
                        v = ta[:, m * GB:m * GB + GB, :].rearrange("p b (h d) -> p (b h) d", h=H)
                        dve.tensor_tensor(v, bank(m).rearrange("p (h d) -> p h d", d=HD), wide(y2[:, m * hh:(m + 1) * hh], HD), ALU.mult).then_inc(*s.step())
                        dve.wait_ge(*s.last())
                        rotate(v, cw[m][:, :], sw[m][:, :], out, f"{nm}rot", "half")
                if l == "L3a":
                    yield n, 6
                    dve.wait_ge(*s.last())
                    for m, nm, out in ((0, "q", tc), (1, "k", td)):
                        dve.wait_ge(*s.at(f"L3a.{nm}"))
                        rotate(bank(m).rearrange("p (h d) -> p h d", d=HD), const("c3"), const("s3"), out, f"{nm}rot", "pair")
                if l in ("L0x", "L1a", "L1x", "L2x", "L3a"):
                    yield from attend(n, l)
                    yield from add(n, l, 0)
                if l == "L0f":
                    yield from top2(n, l, E0, "bg0")
                    yield from mix(n, l, E0, [e % 3 for e in range(E0)], lambda e: 21 + 4 * e)
                if l == "L1f":
                    yield from top2(n, l, E1, "bg1")
                    yield from mix(n, l, E1, [2] * E1, lambda e: 23 + 4 * e)
                if l == "L2a":
                    for m in range(2):
                        yield n, 7 + 2 * m
                        dve.wait_ge(*s.at(f"L2a.z{m}"))
                        Z = bank(2 - 2 * m, 2).rearrange("p (h k) -> p h k", k=P)
                        dve.tensor_reduce(s4[:, :], Z, AX.X, ALU.max).then_inc(*s.step())
                        dve.wait_ge(*s.last())
                        dve.tensor_tensor(pr[:, 8 * m:8 * m + 8, :], Z, wide(s4[:, :]), ALU.subtract).then_inc(*s.step(f"zs{m}"))
                        dve.wait_ge(*s.last())
                    for m in range(2):
                        yield n, 12 + m
                        dve.wait_ge(*s.at(f"L2a.ze{m}"))
                        dve.tensor_scalar(pr[:, 8 * m:8 * m + 8, :], pr[:, 8 * m:8 * m + 8, :], float(P) ** -0.5, 1e-6, ALU.mult, ALU.add).then_inc(*s.step(f"phi{m}"))
                    for h in range(MH):
                        yield n, 19 + h
                        dve.wait_ge(*s.at(f"L2a.A{h}"))
                        dve.tensor_tensor(pr[:, GB * h:GB * h + GB, :], four(bank(2 + h)), over(const("keepT")), ALU.mult).then_inc(*s.step(f"Am{h}"))
                    for h in range(MH):
                        yield n, 22 + h
                        dve.wait_ge(*s.at(f"L2a.O{h}"))
                        O = bank(h)[:, 0:GB * (MD + 1)].rearrange("p (b d) -> p b d", b=GB)
                        dve.tensor_scalar(s4[:, 0:GB], O[:, :, MD], 1e-6, None, ALU.add).then_inc(*s.step())
                        dve.wait_ge(*s.last())
                        dve.reciprocal(s4b[:, 0:GB], s4[:, 0:GB]).then_inc(*s.step())
                        dve.wait_ge(*s.last())
                        dve.tensor_tensor(t.co[:, :, h * MD:(h + 1) * MD], O[:, :, 0:MD], wide(s4b[:, 0:GB], MD), ALU.mult).then_inc(*s.step("co3"))
                        dve.wait_ge(*s.last())
                    yield n, 27
                    dve.wait_ge(*s.at("L2a.y"))
                    dve.tensor_tensor(tc[:, :, :], four(bank(3)), xn[:, :, :], ALU.add).then_inc(*s.step())
                    dve.wait_ge(*s.last())
                    variance(tc, 1e6, "var2")
                    yield n, 31
                    dve.wait_ge(*s.at("L2a.var2_r"))
                    for b in range(GB):
                        dve.tensor_scalar(tc[:, b, :], tc[:, b, :], t.mv[:, b, 0:1], t.rs[:, b:b + 1], ALU.subtract, ALU.mult).then_inc(*s.step("hn"))
                    yield from add(n, l, 0, "y2")
                if l == "L2f":
                    yield n, 2
                    dve.wait_ge(*s.last())
                    dve.tensor_tensor(tb, xn[:, :, :], xn[:, :, :], ALU.mult).then_inc(*s.step())
                    dve.wait_ge(*s.last())
                    dve.tensor_reduce(s4[:, 0:GB], tb, AX.X, ALU.add).then_inc(*s.step())
                    dve.wait_ge(*s.last())
                    dve.tensor_scalar(s4[:, 0:GB], s4[:, 0:GB], 1e-24, None, ALU.max).then_inc(*s.step("ms"))
                    yield n, 5
                    dve.wait_ge(*s.at("L2f.ms_r"))
                    dve.wait_ge(*s.at("L2f.lg"))
                    dve.tensor_tensor(lgm[:, :, :], bank(0)[:, 0:GB * E2].rearrange("p (b e) -> p b e", b=GB),
                                      wide(s4b[:, 0:GB], E2), ALU.mult).then_inc(*s.step("lgs"))
                    yield n, 7
                    dve.wait_ge(*s.at("L2f.lge"))
                    dve.tensor_scalar(lg[:, :, :], lgm[:, :, :], 1.0, None, ALU.add).then_inc(*s.step())
                    dve.wait_ge(*s.last())
                    dve.reciprocal(lgm[:, :, :], lg[:, :, :]).then_inc(*s.step())
                    dve.wait_ge(*s.last())
                    for b in range(GB):
                        dve.max(t.m8[:, b, :], lgm[:, b, :]).then_inc(*s.step())
                    dve.wait_ge(*s.last())
                    for b in range(GB):
                        dve.match_replace(sel[:, b, :], t.m8[:, b, :], lgm[:, b, :], -1.0).then_inc(*s.step())
                    dve.tensor_reduce(s4[:, 0:GB], t.m8[:, :, :], AX.X, ALU.add).then_inc(*s.step())
                    dve.wait_ge(*s.last())
                    dve.scalar_tensor_tensor(gw[:, :, :], sel[:, :, :], 0.0, lgm[:, :, :], ALU.is_lt, ALU.mult).then_inc(*s.step())
                    dve.reciprocal(s4b[:, 0:GB], s4[:, 0:GB]).then_inc(*s.step())
                    dve.wait_ge(*s.last())
                    dve.tensor_tensor(gw[:, :, :], gw[:, :, :], wide(s4b[:, 0:GB], E2), ALU.mult).then_inc(*s.step())
                    for part in range(3):
                        dve.wait_ge(*s.last())
                        dve.tensor_copy(t.gws[:, :, part, :], gw[:, :, :]).then_inc(*s.step("gws"))
                        if part < 2:
                            dve.wait_ge(*s.last())
                            dve.tensor_tensor(gw[:, :, :], gw[:, :, :], t.gws[:, :, part, :], ALU.subtract).then_inc(*s.step())
                    for c in range(9):
                        r = P if c < 8 else HE2
                        yield n, 22 + 4 * c
                        dve.wait_ge(*s.at(f"L2f.silu{c}"))
                        dve.tensor_tensor(hid[0:r, c % 4, :], bank(1)[0:r, :], hid[0:r, 4 + c % 2, :], ALU.mult)\
                           .then_inc(*s.step(f"act{c}" if c == 8 else None))
                        if c < 8:
                            dve.wait_ge(*s.last())
                            dve.tensor_tensor(hid[:, c % 4, :], bank(2), hid[:, c % 4, :], ALU.mult).then_inc(*s.step(f"act{c}"))
                    yield from add(n, l, 3)
                if l == "L3x":
                    yield n, 3
                    dve.wait_ge(*s.at("L3x.v"))
                    dve.tensor_tensor(tc[:, :, :], four(bank(2)), over(row("L3x_bv")), ALU.add).then_inc(*s.step("V"))
                    yield n, 7
                    dve.wait_ge(*s.at("L3x.S"))
                    S = four(bank(3))
                    dve.tensor_reduce(s4[:, 0:GB], S, AX.X, ALU.max).then_inc(*s.step())
                    dve.wait_ge(*s.last())
                    dve.tensor_tensor(pr[:, 0:GB, :], S, wide(s4[:, 0:GB]), ALU.subtract).then_inc(*s.step("sub"))
                    yield n, 9
                    dve.wait_ge(*s.at("L3x.exp"))
                    dve.tensor_reduce(s4[:, 0:GB], pr[:, 0:GB, :], AX.X, ALU.add).then_inc(*s.step())
                    dve.wait_ge(*s.last())
                    dve.reciprocal(s4b[:, 0:GB], s4[:, 0:GB]).then_inc(*s.step())
                    dve.wait_ge(*s.last())
                    for b in range(GB):
                        dve.tensor_scalar(pr[:, b, :], pr[:, b, :], s4b[:, b:b + 1], None, ALU.mult).then_inc(*s.step("p"))
                    yield from add(n, l, 2)
                if l == "L3f":
                    yield n, 2
                    dve.wait_ge(*s.last())
                    dve.tensor_tensor(tb, xn[:, :, :], xn[:, :, :], ALU.mult).then_inc(*s.step())
                    dve.wait_ge(*s.last())
                    dve.tensor_reduce(s4[:, 0:GB], tb, AX.X, ALU.add).then_inc(*s.step())
                    dve.wait_ge(*s.last())
                    dve.tensor_scalar(s4[:, 0:GB], s4[:, 0:GB], 1e-24, None, ALU.max).then_inc(*s.step("ms"))
                    yield n, 3
                    dve.wait_ge(*s.at("L3f.ms_r"))
                    dve.tensor_scalar(s4b[:, 0:GB], s4b[:, 0:GB], float(P) ** 0.5, None, ALU.mult).then_inc(*s.step())
                    dve.wait_ge(*s.last())
                    for b in range(GB):
                        dve.tensor_scalar(tc[:, b, :], xn[:, b, :], s4b[:, b:b + 1], None, ALU.mult).then_inc(*s.step("xr"))
                    yield n, 5
                    dve.wait_ge(*s.at("L3f.s"))
                    dve.tensor_copy(rt_s[:, g * GB:(g + 1) * GB], bank(2)[:, 0:GB]).then_inc(*s.step("rs"))
                    if g == GROUPS - 1:
                        yield n, 8
                        dve.wait_ge(*s.at("L3f.sT"))
                        dve.tensor_scalar(rt_r[:, :], bank(2)[0:B, 0:P], 0.0, None, ALU.min).then_inc(*s.step("smin"))
                        dve.memset(rt_u[:, 0:1], float(P) / PICKED).then_inc(descent, 1)
                        yield n, 10
                        dve.wait_ge(*s.at("L3f.E"))
                        dve.wait_ge(descent, 1)
                        dve.scalar_tensor_tensor(rt_b[:, :], rt_e[:, :], rt_u[:, 0:1], rt_k[:, :], ALU.min, ALU.mult,
                                                 accum_out=rt_u[:, 1:2]).then_inc(descent, 1)
                        with dve.Fori(0, (DESCENT - 2) // 2) as i:
                            dve.wait_ge(descent, 2 * i + 2)
                            dve.scalar_tensor_tensor(rt_b[:, :], rt_e[:, :], rt_u[:, 1:2], rt_k[:, :], ALU.min, ALU.mult,
                                                     accum_out=rt_u[:, 0:1]).then_inc(descent, 1)
                            dve.wait_ge(descent, 2 * i + 3)
                            dve.scalar_tensor_tensor(rt_b[:, :], rt_e[:, :], rt_u[:, 0:1], rt_k[:, :], ALU.min, ALU.mult,
                                                     accum_out=rt_u[:, 1:2]).then_inc(descent, 1)
                        dve.wait_ge(descent, DESCENT)
                        dve.tensor_scalar(rt_u[:, 1:2], rt_u[:, 1:2], 1e-37, None, ALU.max).then_inc(descent, 1)
                        dve.wait_ge(descent, DESCENT + 1)
                        dve.reciprocal(rt_u[:, 0:1], rt_u[:, 1:2]).then_inc(*s.step())
                        dve.wait_ge(*s.last())
                        dve.tensor_scalar(rt_b[:, :], rt_e[:, :], rt_u[:, 1:2], rt_u[:, 0:1], ALU.min, ALU.mult).then_inc(*s.step())
                        dve.wait_ge(*s.last())
                        dve.tensor_scalar(rt_r[:, :], rt_b[:, :], -1.0, 1.0, ALU.mult, ALU.add).then_inc(*s.step())
                        dve.wait_ge(*s.last())
                        dve.tensor_tensor(rt_e[:, :], rt_b[:, :], rt_r[:, :], ALU.add).then_inc(*s.step("f"))
                        yield n, 17
                        dve.wait_ge(*s.at("L3f.fT"))
                        dve.tensor_copy(rt_f[:, :], bank(3)[:, 0:B]).then_inc(*s.step("rf"))
                    yield n, 18
                    dve.wait_ge(*s.at("L3f.xb"))
                    dve.wait_ge(*s.at("L3f.y"))
                    dve.wait_ge(*s.at("L3f.rf", GROUPS - 1))
                    for b in range(GB):
                        dve.scalar_tensor_tensor(x[:, b, :], bank(2)[:, b * P:(b + 1) * P], rt_f[:, g * GB + b:g * GB + b + 1], x[:, b, :],
                                                 ALU.mult, ALU.add).then_inc(*s.step())
                    dve.wait_ge(*s.last())
                    yield from add(n, l, 1)
        weave(*(program(g) for g in range(GROUPS)))
    stack.close()


def constants():
    f = np.float32
    k = np.zeros((P, NK), f)

    def put(name, v):
        k[:, KOFF[name][0]:KOFF[name][0] + KOFF[name][1]] = v
    put("ident", np.eye(P, dtype=f))
    r = np.arange(P)
    put("heads", (r[:, None] // HD == np.arange(H)[None, :]).astype(f))
    pos = np.arange(P, dtype=f)
    inv = (f(1.0) / (f(500000.0) ** (np.arange(0, HD, 2, dtype=f) / f(HD)))).astype(f)
    fr = np.outer(pos, inv).astype(f)
    emb = np.concatenate([fr, fr], -1)
    put("c0", np.cos(emb))
    put("s0", np.concatenate([-np.sin(fr), np.sin(fr)], -1))
    inv3 = (f(1.0) / (f(10000.0) ** (np.arange(0, HD, 2, dtype=f) / f(HD)))).astype(f)
    fr3 = (pos[:, None] * inv3[None, :]).astype(f)
    put("c3", np.repeat(np.cos(fr3), 2, axis=1))
    s3 = np.repeat(np.sin(fr3), 2, axis=1)
    s3[:, 0::2] *= -1
    put("s3", s3)
    put("keepT", (r[:, None] <= r[None, :]).astype(f))
    put("ident3", (r[:, None] % E2 == np.arange(E2)[None, :]).astype(f))
    e = np.arange(E0)
    put("tri", np.tile((e[None, :] < e[:, None]).astype(f).reshape(1, -1), (P, 1)))
    bf = mybir.dt.np(BF16)
    kb = np.zeros((P, NB), bf)
    kb[:, 0:P] = np.eye(P)
    put("causal", np.where(r[None, :] > r[:, None], f(NEG), f(0.0)))
    slopes = np.array([2.0 ** (-8.0 * (h + 1) / H) for h in range(H)], f)
    rel = np.abs(r[None, :] - r[:, None]).astype(f)
    bias = (-slopes[None, :, None] * rel[:, None, :]).reshape(P, H * P)
    put("alibi", (bias.astype(np.float64) * np.sqrt(float(HD))).astype(f))
    return k, kb


def pack(a):
    f = np.float32
    w = np.zeros((P, NW), f)

    def put(name, v):
        at, n = WOFF[name]
        w[0:v.shape[0], at:at + n] = v
    put("L0a_w", np.concatenate([a[f"L0_attn_W{c}"].T for c in "ifgo"], axis=1))
    for l, pre, t in (("L0x", "L0_xattn_W", True), ("L2x", "L2_xattn_W", True), ("L3x", "L3_xattn_W", True), ("L2a", "L2_attn_W", False)):
        for c in "qkvo":
            v = a[pre + c]
            put(f"{l}_w{c}", v.T if t else v)
    for c in "qkvo":
        put(f"L1a_w{c}", a["L1_attn_W" + c.upper()])
    put("L1x_wq", a["L1_xattn_Wq"])
    put("L1x_wk", a["L1_xattn_Wkv"][:, :P])
    put("L1x_wv", a["L1_xattn_Wkv"][:, P:])
    put("L1x_wo", a["L1_xattn_Wo"])
    put("L0f_wg", a["L0_ffn_Wg"])
    put("L0f_we", a["L0_ffn_We"].transpose(1, 0, 2).reshape(P, -1))
    put("L0f_be", a["L0_ffn_be"])
    put("L1f_wg", a["L1_ffn_Wg"])
    put("L1f_w1", a["L1_ffn_W1"].transpose(1, 0, 2).reshape(P, -1))
    put("L1f_w2", a["L1_ffn_W2"].reshape(E1, 2, P, P).transpose(2, 0, 1, 3).reshape(P, -1))
    put("L1f_b2", a["L1_ffn_b2"])
    put("L2a_om", np.concatenate([a["L2_attn_omega"].T] * MH, axis=0))
    put("L2a_w1", a["L2_attn_W1"])
    put("L2a_w2", a["L2_attn_W2"].reshape(4, P, P).transpose(1, 0, 2).reshape(P, -1))
    put("L2f_gw", a["L2_ffn_gate_w"])
    put("L2f_wg", a["L2_ffn_w_gate"].transpose(1, 0, 2).reshape(P, -1))
    put("L2f_wu", a["L2_ffn_w_up"].transpose(1, 0, 2).reshape(P, -1))
    put("L2f_wd", a["L2_ffn_w_down"].reshape(8, P, P).transpose(1, 0, 2).reshape(P, -1))
    put("L2f_sg", a["L2_ffn_sw_gate"])
    put("L2f_su", a["L2_ffn_sw_up"])
    put("L2f_sd", a["L2_ffn_sw_down"])
    kqv = a["L3_attn_W_KQV"]
    put("L3a_wk", kqv[0:P].T)
    put("L3a_wq", kqv[P:2 * P].T)
    put("L3a_wv", kqv[2 * P:].T)
    put("L3a_wo", a["L3_attn_W_O"].T)
    put("L3f_lw1", a["L3_ffn_light_w1"])
    put("L3f_lw2", a["L3_ffn_light_w2"])
    put("L3f_hw1", a["L3_ffn_heavy_w1"])
    put("L3f_hw2", a["L3_ffn_heavy_w2"].reshape(4, P, P).transpose(1, 0, 2).reshape(P, -1))
    put("L3f_rt", a["L3_ffn_routing_token"].reshape(P, 1))
    rows = [a["L0_attn_ni"], a["L0_attn_nf"], a["L0_attn_ng"], a["L0_attn_nout"], a["L0_attn_no"],
            a["L0_xattn_q_norm_w"], a["L0_xattn_k_norm_w"], a["L0_ffn_bg"], a["L1_ffn_bg"],
            a["L1_xattn_bkv"][P:], a["L1_xattn_bo"], a["L2_attn_b2"], a["L2_xattn_bv"], a["L2_xattn_bo"],
            a["L3_xattn_bv"], a["L3_xattn_bo"], a["L3_ffn_light_b2"], a["L3_ffn_heavy_b2"]]
    r = np.concatenate(rows).reshape(1, NR)
    c = np.zeros((P, NC), f)
    for name, v in (("L1x_bq", a["L1_xattn_bq"]), ("L1x_bk", a["L1_xattn_bkv"][:P]), ("L2x_bq", a["L2_xattn_bq"]),
                    ("L2x_bk", a["L2_xattn_bk"]), ("L3x_bq", a["L3_xattn_bq"]), ("L1f_b1", a["L1_ffn_b1"].reshape(2 * E1, P)),
                    ("L2a_b1", a["L2_attn_b1"].reshape(4, P)), ("gamma", a["L2_attn_gamma"]), ("beta", a["L2_attn_beta"]),
                    ("L3f_lg", a["L3_ffn_light_gamma"]), ("L3f_lb1", a["L3_ffn_light_b1"]), ("L3f_hg", a["L3_ffn_heavy_gamma"]),
                    ("L3f_hb1", a["L3_ffn_heavy_b1"].reshape(4, P))):
        at, n = COFF[name]
        v = v.reshape(n, -1)
        c[0:v.shape[1], at:at + n] = v.T
    return w, r, c


def kernel(**inputs):
    import concourse.bacc as _bacc
    from concourse.bass_utils import run_bass_kernel_spmd as _run

    a = {n: np.ascontiguousarray(v) for n, v in inputs.items()}
    w, r, c = pack(a)
    k, kb = constants()
    arrays = {"x": a["x"], "ctx": a["ctx_1024"], "mask": a["mask_Bx1xSxS2_ik1"].reshape(B, P, P),
              "weights": w, "rows": r, "cols": c, "consts": k, "bconsts": kb}
    marks = {}
    for _ in range(2):
        nc = _bacc.Bacc("TRN2", target_bir_lowering=False, num_devices=1)
        args = [nc.dram_tensor("in_" + n, v.shape, mybir.dt.from_np(v.dtype), kind="ExternalInput").ap() for n, v in arrays.items()]
        out = nc.dram_tensor("out_0", (B, P, P), F32, kind="ExternalOutput").ap()
        build(nc, *args, out, marks)
    res = _run(nc, [{"in_" + n: v for n, v in arrays.items()}], core_ids=[0])
    return res.results[0]["out_0"]
```

```python
from contextlib import ExitStack

import numpy as np

import concourse.bass as bass
from concourse import mybir

F32 = mybir.dt.float32
BF16 = mybir.dt.bfloat16
I32 = mybir.dt.int32
ALU = mybir.AluOpType
ACT = mybir.ActivationFunctionType
AX = mybir.AxisListType

P = 128
B = 8
GB = 4
GROUPS = B // GB
W4 = GB * P
H = 16
HD = P // H
HG = 4
E0, E1, E2, K2 = 8, 6, 16, 8
HID1 = 256
HE2 = 64
MH, MD = 2, 64
MAGIC = 12582912.0
NEG = -1.0e30
LAYERS = ["pre", "L0a", "L0x", "L0f", "L1a", "L1x", "L1f", "L2a", "L2x", "L2f", "L3a", "L3x", "L3f"]
DESCENT = 50
ROUND = 6
PICKED = float(min(128 * 9 // 8, P))
STAGES = len(LAYERS) - 1


def weight_plan():
    return {
        "L0a": [("L0a_w", 4 * P), ("L2f_gw", P)],
        "L0x": [("L0x_wq", P), ("L0x_wk", P), ("L0x_wv", P), ("L0x_wo", P)],
        "L0f": [("L0f_wg", E0), ("L0f_we", E0 * P), ("L0f_be", P)],
        "L1a": [("L1a_wq", P), ("L1a_wk", P), ("L1a_wv", P), ("L1a_wo", P)],
        "L1x": [("L1x_wq", P), ("L1x_wk", P), ("L1x_wv", P), ("L1x_wo", P)],
        "L1f": [("L1f_wg", E1), ("L1f_w1", E1 * HID1), ("L1f_w2", E1 * 2 * P), ("L1f_b2", P)],
        "L2a": [("L2a_wq", P), ("L2a_wk", P), ("L2a_wv", P), ("L2a_wo", P), ("L2a_om", P),
                ("L2a_w1", 4 * P), ("L2a_w2", 4 * P)],
        "L2x": [("L2x_wq", P), ("L2x_wk", P), ("L2x_wv", P), ("L2x_wo", P)],
        "L2f": [("L2f_wg", E2 * HE2), ("L2f_wu", E2 * HE2), ("L2f_wd", E2 * HE2),
                ("L2f_sg", HE2), ("L2f_su", HE2), ("L2f_sd", P)],
        "L3a": [("L3a_wk", P), ("L3a_wq", P), ("L3a_wv", P), ("L3a_wo", P)],
        "L3x": [("L3x_wq", P), ("L3x_wk", P), ("L3x_wv", P), ("L3x_wo", P)],
        "L3f": [("L3f_lw1", HE2), ("L3f_lw2", P), ("L3f_hw1", 4 * P), ("L3f_hw2", 4 * P)],
    }


ROWS = [("ni", P), ("nf", P), ("ng", P), ("nout", P), ("no", P), ("qn", HD), ("kn", HD), ("bg0", E0), ("bg1", E1),
        ("L1x_bv", P), ("L1x_bo", P), ("L2a_b2", P), ("L2x_bv", P), ("L2x_bo", P), ("L3x_bv", P), ("L3x_bo", P),
        ("L3f_lb2", P), ("L3f_hb2", P), ("L3f_rt", P)]
COLS = [("L1x_bq", 1), ("L1x_bk", 1), ("L2x_bq", 1), ("L2x_bk", 1), ("L3x_bq", 1), ("L1f_b1", 2 * E1),
        ("L2a_b1", 4), ("gamma", 1), ("beta", 1), ("L3f_lg", 1), ("L3f_lb1", 1), ("L3f_hg", 1), ("L3f_hb1", 4)]
CONSTS = [("ident", P), ("heads", H), ("c0", HD), ("s0", HD), ("c3", HD), ("s3", HD), ("keepT", P), ("tri", E0 * E0), ("ident3", E2),
          ("causal", P), ("alibi", H * P)]
BCONSTS = [("identb", P)]


def offsets(plan):
    at, out = 0, {}
    for name, n in plan:
        out[name] = (at, n)
        at += n
    return out, at


WPLAN = weight_plan()
WOFF, NW = offsets([x for v in WPLAN.values() for x in v])
ROFF, NR = offsets(ROWS)
COFF, NC = offsets(COLS)
KOFF, NK = offsets(CONSTS)
BOFF, NB = offsets(BCONSTS)


def weave(*programs):
    at = [next(p, None) for p in programs]
    while any(a is not None for a in at):
        i = min((a, i) for i, a in enumerate(at) if a is not None)[1]
        at[i] = next(programs[i], None)


def build(nc, x_d, ctx_d, mask_d, w_d, r_d, c_d, k_d, b_d, out_d, marks):
    stack = ExitStack()
    known = dict(marks)

    def sb(name, shape, dt=F32):
        return stack.enter_context(nc.sbuf_tensor(name, shape, dt))

    wt = sb("wt", [P, NW])
    rowt = sb("rowt", [P, NR])
    colt = sb("colt", [P, NC])
    kt = sb("kt", [P, NK])
    bt = sb("bt", [P, NB], BF16)
    ones = sb("ones", [P, P])
    negh = sb("negh", [P, GB])
    magic = sb("magic", [P, 2])
    wtern = sb("wtern", [P, 4 * P], BF16)
    wabs, wmean, wrec = sb("wabs", [P, 4]), sb("wmean", [P, 4]), sb("wrec", [P, 4])
    wsc = sb("wsc", [P, 4])
    wtmp = sb("wtmp", [P, 4 * P])
    cw = [sb(f"cw{n}", [P, HD]) for n in range(2)]
    sw = [sb(f"sw{n}", [P, HD]) for n in range(2)]
    gwT = sb("gwT", [P, E2])
    gwn = sb("gwn", [E2, P])
    gsc = sb("gsc", [E2, 2])
    pairs = sb("pairs", [3 * E2, E2 * HE2], BF16)
    rt_s = sb("rt_s", [P, B])
    rt_r = sb("rt_r", [B, P])
    rt_b, rt_e, rt_k = sb("rt_b", [B, P]), sb("rt_e", [B, P]), sb("rt_k", [B, P])
    rt_u = sb("rt_u", [B, 2])
    rt_f = sb("rt_f", [P, B])

    class Tiles:

        def __init__(self, g):
            def own(name, shape, dt=F32):
                return sb(f"{name}{g}", shape, dt)
            self.x = own("x", [P, GB, P])
            self.xn = own("xn", [P, GB, P])
            self.xnT = own("xnT", [P, W4])
            self.ctxT = own("ctxT", [P, W4])
            self.st, self.mv = own("st", [P, GB, 6]), own("mv", [P, GB, 2])
            self.ve, self.rs = own("ve", [P, GB]), own("rs", [P, GB])
            self.tc, self.td = own("tc", [P, GB, P]), own("td", [P, GB, P])
            big = own("big", [P, 8 * W4])
            self.pr = big[:, 0:4 * W4].rearrange("p (h k) -> p h k", k=P)
            self.PT = big[:, 4 * W4:8 * W4].rearrange("p (h k) -> p h k", k=P)
            self.hid = big[:, :].rearrange("p (n c) -> p n c", c=W4)
            self.ta, self.tb = self.PT[:, 0:12, :], self.PT[:, 12:16, :]
            self.s12, self.s12b, self.deq = own("s12", [P, 12]), own("s12b", [P, 12]), own("deq", [P, 12])
            self.ndeq = own("ndeq", [P, 4])
            self.s4, self.s4b = own("s4", [P, 8]), own("s4b", [P, 8])
            self.v2, self.y2, self.h2 = (own(n, [P, 2 * GB * H]) for n in ("v2", "y2", "h2"))
            qk = own("qk", [P, 2 * W4])
            self.QT, self.KT = qk[:, 0:W4], qk[:, W4:2 * W4]
            self.qT3 = qk[:, :].bitcast(BF16)[:, 0:3 * W4].rearrange("p (j n) -> p j n", j=3)
            self.KTm = own("KTm", [P, 2, H // 2, P])
            self.vaug = own("vaug", [P, GB, H, HD + 1])
            self.vlast = own("vlast", [P, H, 32])
            self.vv = own("vv", [P, GB, MH, MD + 1])
            self.mx, self.rc = own("mx", [P, 2, H // 2]), own("rc", [P, H])
            self.co, self.coT = own("co", [P, GB, P]), own("coT", [P, W4])
            self.cin = self.co
            self.mask = self.coT[:, :].bitcast(I32).rearrange("p (b k) -> p b k", b=GB)
            self.dmask = own("dmask", [P, GB, P], BF16)
            self.lg, self.lgm = own("lg", [P, GB, E2]), own("lgm", [P, GB, E2])
            self.sel, self.gw = own("sel", [P, GB, E2]), own("gw", [P, GB, E2])
            self.gws = own("gws", [P, GB, 3, E2], BF16)
            self.gt, self.eq = own("gt", [P, GB, E0, E0]), own("eq", [P, GB, E0, E0])
            self.m8 = own("m8", [P, GB, 8])
            self.gwTT = own("gwTT", [E2, W4])
            self.gwsT = own("gwsT", [3 * E2, W4], BF16)

    tiles = [Tiles(g) for g in range(GROUPS)]
    ps = stack.enter_context(nc.psum_tensor("ps", [P, 8 * 512], F32))

    def banks_of(g):
        def bank(i, n=1):
            return ps[:, (4 * g + i) * 512:(4 * g + i + n) * 512]
        return bank

    def w(name, rows=P):
        at, n = WOFF[name]
        return wt[0:rows, at:at + n]

    def row(name, rows=P):
        at, n = ROFF[name]
        return rowt[0:rows, at:at + n]

    def col(name, i=0, rows=P):
        return colt[0:rows, COFF[name][0] + i:COFF[name][0] + i + 1]

    def const(name):
        at, n = KOFF[name]
        return kt[:, at:at + n]

    def four(t):
        return t.rearrange("p (b d) -> p b d", b=GB)

    ident = const("ident")
    identb = bt[:, BOFF["identb"][0]:BOFF["identb"][0] + P]
    causal = const("causal")
    alibi = const("alibi").rearrange("p (h k) -> p h k", h=H)

    loaded = {n: stack.enter_context(nc.semaphore(f"loaded_{n}"))
              for n in list(WPLAN) + ["rows", "consts", "alibi", "x0", "x1", "ctx0", "ctx1", "mask0", "mask1"]}
    stored = stack.enter_context(nc.semaphore("stored"))
    descent = stack.enter_context(nc.semaphore("descent_step"))
    semaphores = {f"pre_{e}": stack.enter_context(nc.semaphore(f"pre_{e}")) for e in ("tensor", "vector", "gpsimd")}
    semaphores |= {f"{l}_{e}{g}": stack.enter_context(nc.semaphore(f"{l}_{e}{g}"))
                   for l in LAYERS[1:] for e in ("tensor", "vector", "scalar", "gpsimd") for g in range(GROUPS)}

    class Steps:

        def __init__(self, who, group=None):
            self.who, self.group, self.count = who, group, {}

        def begin(self, layer):
            self.layer = layer
            self.sem = f"{layer}_{self.who}" + ("" if self.group is None else str(self.group))

        def step(self, name=None):
            n = self.count[self.sem] = self.count.get(self.sem, 0) + 1
            if name is not None:
                marks[self.group, f"{self.layer}.{name}"] = (self.sem, n)
            return semaphores[self.sem], 1

        def at(self, name, group=None):
            g = None if name.startswith("pre.") else self.group if group is None else group
            sem, n = known.get((g, name), ("pre_vector", 1))
            return semaphores[sem], n

        def last(self, back=0):
            return semaphores[self.sem], self.count[self.sem] - back

    def beat(g, u, k=0):
        return 20 + 10 * u + 6 * g + k

    SCALES = {l: float(P if l == "L2x" else HD) ** -0.5 for l in ("L0x", "L1a", "L1x", "L2x", "L3a")}
    UNITS = 2 * GB
    HH = H // 2
    OW = HD + 1
    LEAD = 3
    LAST_BIAS = {"L1x": "L1x_bo", "L2a": "L2a_b2", "L2x": "L2x_bo", "L3x": "L3x_bo", "L3f": "L3f_lb2"}

    def keys_of(t, b):
        return t.KT[:, b * P:(b + 1) * P].unsqueeze(1).to_broadcast([P, HH, P])

    def heads_of(u):
        return const("heads")[:, (u % 2) * HH:(u % 2 + 1) * HH].unsqueeze(2).to_broadcast([P, HH, P])

    block = stack.enter_context(nc.Block())

    @block.sync
    def _(sp):
        def load_weights(l):
            at = WOFF[WPLAN[l][0][0]][0]
            n = sum(c for _, c in WPLAN[l])
            sp.dma_start(wt[:, at:at + n], w_d[:, at:at + n]).then_inc(loaded[l], 16)

        sp.dma_start(tiles[0].x[:, :, :], x_d[0:GB, :, :].rearrange("b p d -> p b d")).then_inc(loaded["x0"], 16)
        sp.dma_start(tiles[1].x[:, :, :], x_d[GB:B, :, :].rearrange("b p d -> p b d")).then_inc(loaded["x1"], 16)
        sp.dma_start(rowt[:, :], r_d.to_broadcast([P, NR])).then_inc(loaded["rows"], 16)
        sp.dma_start(colt[:, :], c_d).then_inc(loaded["rows"], 16)
        load_weights("L0a")
        first = KOFF["alibi"][0]
        sp.dma_start(kt[:, 0:first], k_d[:, 0:first]).then_inc(loaded["consts"], 16)
        sp.dma_start(bt[:, :], b_d).then_inc(loaded["consts"], 16)
        for g in range(GROUPS):
            t, mine = tiles[g], slice(g * GB, (g + 1) * GB)
            sp.dma_start(t.cin[:, :, :], ctx_d[mine, :, :].rearrange("b p d -> p b d")).then_inc(loaded[f"ctx{g}"], 16)
            sp.dma_start(t.mask, mask_d[mine, :, :].rearrange("b p d -> p b d")).then_inc(loaded[f"mask{g}"], 16)
        for l in list(WPLAN)[1:]:
            load_weights(l)
            if l == "L1a":
                sp.dma_start(kt[:, first:], k_d[:, first:]).then_inc(loaded["alibi"], 16)
        s = [Steps("sync", g) for g in range(GROUPS)]
        for g in range(GROUPS):
            sp.wait_ge(*s[g].at(f"{LAYERS[STAGES]}.x"))
            sp.dma_start(out_d[g * GB:(g + 1) * GB, :, :].rearrange("b p d -> p b d"), tiles[g].x[:, :, :]).then_inc(stored, 16)
        sp.wait_ge(stored, 16 * GROUPS)

    @block.gpsimd
    def _(pool):
        p = Steps("gpsimd")
        p.begin("pre")
        pool.memset(negh[:, :], -0.5).then_inc(*p.step("negh"))
        pool.memset(ones[:, :], 1.0).then_inc(*p.step("ones"))
        pool.memset(magic[:, 0:1], MAGIC).then_inc(*p.step())
        pool.memset(magic[:, 1:2], -MAGIC).then_inc(*p.step())
        for t in tiles:
            pool.memset(t.vaug[:, :, :, :], 1.0).then_inc(*p.step("vaug"))
            pool.memset(t.vlast[:, :, :], 1.0).then_inc(*p.step())
            pool.memset(t.vv[:, :, :, :], 1.0).then_inc(*p.step("vv"))
        pool.memset(rt_k[:, :], 1.0 / PICKED).then_inc(*p.step("rt_k"))
        pool.wait_ge(*p.last())

        def program(g):
            s, t = Steps("gpsimd", g), tiles[g]

            def rsqrt(out, src, name):
                pool.wait_ge(*s.at(f"{s.layer}.{name}"))
                pool.tensor_tensor(out, src, negh[:, :], ALU.pow).then_inc(*s.step(name + "_r"))

            def spread_keys(n, l):
                first = 0 if l in ("L1x", "L2x") else 1
                for u in range(first, UNITS):
                    b = u // 2
                    yield n, ((1 if first == 0 else 19) if u < 2 else beat(g, 0, 1) if u == 2 else beat(g, u - 3, 3))
                    if u == first:
                        pool.wait_ge(*s.at(f"{l}.KT"))
                    if u >= 2:
                        pool.wait_ge(*s.at(f"{l}.S{u - 2}"))
                    pool.tensor_tensor(t.KTm[:, u % 2, :, :], keys_of(t, b), heads_of(u), ALU.mult).then_inc(*s.step(f"keys{u}"))
                    if u == 1:
                        yield from add_bias(n, 19, l)

            def rotate_keys(n, l):
                yield n, 6
                heads = GB * H
                raw = t.ta[:, GB:2 * GB, :].rearrange("p b (h d) -> p (b h) d", h=H)
                new = t.td[:, :, :].rearrange("p b (h d) -> p (b h) d", h=H)
                tmp = t.tb.rearrange("p b (h d) -> p (b h) d", h=H)
                pool.wait_ge(*s.at(f"{l}.kraw"))
                if l == "L0x":
                    pool.wait_ge(*p.at("pre.gwT"))
                    pool.wait_ge(*s.at("L0x.y2"))
                    pool.tensor_tensor(raw, new, t.y2[:, heads:2 * heads].unsqueeze(2).to_broadcast([P, heads, HD]), ALU.mult).then_inc(*s.step())
                    pool.wait_ge(*s.last())
                    cos, sin, one, two = cw[1][:, :], sw[1][:, :], slice(0, HD // 2), slice(HD // 2, HD)
                else:
                    cos, sin, one, two = const("c3"), const("s3"), slice(0, HD, 2), slice(1, HD, 2)
                pool.tensor_tensor(new, raw, cos.unsqueeze(1).to_broadcast([P, heads, HD]), ALU.mult).then_inc(*s.step())
                for a, b in ((one, two), (two, one)):
                    pool.tensor_tensor(tmp[:, :, a], raw[:, :, b], sin[:, a].unsqueeze(1).to_broadcast([P, heads, HD // 2]), ALU.mult).then_inc(*s.step())
                pool.wait_ge(*s.last())
                pool.tensor_tensor(t.td[:, :, :], t.td[:, :, :], t.tb, ALU.add).then_inc(*s.step("krot"))

            def add_bias(n, phase, l):
                if l in LAST_BIAS:
                    yield n, phase
                    pool.wait_ge(*s.at(f"{l}.xn"))
                    pool.tensor_tensor(t.x[:, :, :], t.x[:, :, :], row(LAST_BIAS[l]).unsqueeze(1).to_broadcast([P, GB, P]), ALU.add)\
                        .then_inc(*s.step("xb"))

            for n, l in enumerate(LAYERS[1:STAGES + 1]):
                s.begin(l)
                yield n, 0
                rsqrt(t.rs[:, :], t.ve[:, :], "var")
                if l == "L0a":
                    for k, name in ((2, "ms"), (11, "ms1"), (12, "ms2")):
                        yield n, k
                        rsqrt(t.s4b[:, 0:GB], t.s4[:, 0:GB], name)
                        if g == 0 and k == 2:
                            pool.wait_ge(*p.at("pre.gss"))
                            pool.tensor_tensor(gsc[:, 1:2], gsc[:, 0:1], negh[0:E2, 0:1], ALU.pow).then_inc(*p.step("gss_r"))
                if l in ("L2a", "L3x"):
                    yield from add_bias(n, 4, l)
                if l == "L2a":
                    yield n, 30
                    rsqrt(t.rs[:, :], t.ve[:, :], "var2")
                if l in ("L0x", "L3a"):
                    yield from rotate_keys(n, l)
                if l in ("L0x", "L1a", "L1x", "L2x", "L3a"):
                    yield from spread_keys(n, l)
                if l == "L0f":
                    for e in range(2, E0, 2):
                        yield n, 22 + 4 * e
                        pool.wait_ge(*s.at(f"L0f.x{e}.{GB - 1}"))
                        if e > 2:
                            pool.wait_ge(*s.last())
                        pool.tensor_tensor(t.hid[:, 0, :], t.hid[:, 0, :], t.hid[:, e // 2, :], ALU.add).then_inc(*s.step(f"sum{e}"))
                if l in ("L2f", "L3f"):
                    yield n, 2
                    rsqrt(t.s4b[:, 0:GB], t.s4[:, 0:GB], "ms")
                    yield from add_bias(n, 4, l)
        weave(*(program(g) for g in range(GROUPS)))

    @block.tensor
    def _(pe):
        def mm(out, lhsT, rhs, start=True, stop=True, **k):
            return pe.matmul(out, lhsT, rhs, start=start, stop=stop, **k)

        p = Steps("tensor")
        p.begin("pre")
        pe.wait_ge(*p.at("pre.ones"))
        pe.wait_ge(*p.at("pre.wabs"))
        mm(ps[:, 0:4], ones[:, :], wabs[:, :]).then_inc(*p.step("wsum"))
        pe.wait_ge(loaded["consts"], 32)
        pe.wait_ge(*p.at("pre.gwn"))
        pe.transpose(ps[:, 512:512 + E2], gwn[:, :], ident[0:E2, 0:E2]).then_inc(*p.step("gwTp"))
        pe.wait_ge(*p.at("pre.gwT"))

        def program(g):
            s, t, bank = Steps("tensor", g), tiles[g], banks_of(g)
            x, xn, xnT, ctxT, QT, KT, pr, PT, hid = t.x, t.xn, t.xnT, t.ctxT, t.QT, t.KT, t.pr, t.PT, t.hid

            def seq(bk, b):
                return bank(bk)[:, b * P:(b + 1) * P]

            def turn_rows(bk, src, name):
                for b in range(GB):
                    ins = pe.transpose(seq(bk, b), src[:, b, :], ident)
                ins.then_inc(*s.step(name))

            def project_rows(bk, srcT, weight, name):
                for b in range(GB):
                    ins = mm(seq(bk, b), srcT[:, b * P:(b + 1) * P], weight)
                ins.then_inc(*s.step(name))

            def project_cols(bk, srcT, weight, name):
                mm(bank(bk), weight, srcT[:, :]).then_inc(*s.step(name))

            def attend(n, l):
                def scores(u):
                    b = u // 2
                    pe.wait_ge(*s.at(f"{l}.keys{u}"))
                    for i in range(2):
                        ins = mm(bank(i), QT[:, b * P:(b + 1) * P], t.KTm[:, u % 2, HG * i:HG * i + HG, :])
                    ins.then_inc(*s.step(f"S{u}"))

                def turned(u, i):
                    if u + i:
                        pe.wait_ge(*s.at(f"{l}.PT{u - 1 + i}.{1 - i}"))
                    for j in range(HG):
                        ins = pe.transpose(seq(2, j), pr[:, (u % 2) * HH + HG * i + j, :], ident)
                    ins.then_inc(*s.step(f"T{u}.{i}"))

                def weighted(u, i):
                    b, half = divmod(u, 2)
                    if i == 0:
                        if half == 0 and b:
                            pe.wait_ge(*s.at(f"{l}.co{b - 1}"))
                        pe.wait_ge(*s.at(f"{l}.PT{u}.1"))
                    for j in range(HG * i, HG * i + HG):
                        h, P_h = HH * half + j, PT[:, (u % 2) * HH + j, :]
                        if b < GB - 1:
                            ins = mm(bank(3)[:, h * OW:(h + 1) * OW], P_h, t.vaug[:, b, h, :])
                        else:
                            at = 32 * (h % HG)
                            ins = mm(seq(3, h // HG)[at:at + 32, :], t.vlast[:, h, :], P_h, tile_position=(0, at))
                    if i == 1:
                        ins.then_inc(*s.step(f"O{u}"))

                yield n, 20
                pe.wait_ge(*s.at(f"{l}.QT"))
                pe.wait_ge(*s.at(f"{l}.KT"))
                pe.wait_ge(*s.at(f"{l}.vaug"))
                scores(0)
                for u in range(UNITS):
                    if u + 1 < UNITS:
                        yield n, beat(g, u, 2)
                        pe.wait_ge(*s.at(f"{l}.masked{u}"))
                        scores(u + 1)
                    yield n, beat(g, u, 4)
                    for i in range(2):
                        pe.wait_ge(*s.at(f"{l}.exp{u}.{i}"))
                        turned(u, i)
                        if u:
                            weighted(u - 1, i)
                yield n, beat(g, UNITS)
                for i in range(2):
                    weighted(UNITS - 1, i)
                yield n, beat(g, UNITS, 2)
                pe.wait_ge(*s.at(f"{l}.OT"))
                turn_rows(0, t.td, "OR")

            def out_proj(n, l, weight, turn=2, out=0):
                yield n, 130
                pe.wait_ge(*s.at(f"{l}.co{GB - 1}"))
                turn_rows(turn, t.co, "coTp")
                yield n, 131
                pe.wait_ge(*s.at(f"{l}.coT"))
                project_rows(out, t.coT, weight, "y")

            def gates(bk, weight, n):
                for b in range(GB):
                    ins = mm(bank(bk)[:, b * n:(b + 1) * n], xnT[:, b * P:(b + 1) * P], weight)
                ins.then_inc(*s.step("lg"))

            def turn_gates(n, l, k):
                yield n, 12
                pe.wait_ge(*s.at(f"{l}.gw"))
                for b in range(GB):
                    ins = pe.transpose(bank(3)[0:k, b * P:(b + 1) * P], t.gw[:, b, 0:k], ident)
                ins.then_inc(*s.step("gwTp"))

            def gate_bias(n, l, k, bias, phase):
                yield n, phase
                pe.wait_ge(*s.at(f"{l}.gwT"))
                for b in range(GB):
                    ins = mm(seq(3, b), t.gwTT[0:k, b * P:(b + 1) * P], bias)
                ins.then_inc(*s.step("gb"))

            for n, l in enumerate(LAYERS[1:STAGES + 1]):
                s.begin(l)
                if l != "L0a":
                    yield n, 0
                    if g == 0:
                        pe.wait_ge(loaded[l], 16)
                if l in ("L0x", "L1x", "L2x", "L3x"):
                    if l == "L0x":
                        pe.wait_ge(*s.at("L0a.x"))
                        project_rows(1, ctxT, w("L0x_wk"), "k")
                    else:
                        project_cols(1, ctxT, w(f"{l}_wk"), "k")
                    project_rows(2, ctxT, w(f"{l}_wv"), "v")
                if l not in ("L0a", "L3f"):
                    yield n, 2
                    pe.wait_ge(*s.at(f"{l}.xn"))
                    turn_rows(3, xn, "xnTp")
                if l == "L0a":
                    yield n, 2
                    pe.wait_ge(loaded[f"ctx{g}"], 16)
                    turn_rows(3, t.cin, "cTp")
                    yield n, 4
                    pe.wait_ge(*s.at("L0a.q3"))
                    pe.wait_ge(*s.at("L0a.q3a"))
                    for j in range(3):
                        for b in range(GB):
                            ins = pe.transpose(seq(j, b), t.ta[:, j * GB + b, :], ident)
                    ins.then_inc(*s.step("q3Tp"))
                    yield n, 6
                    pe.wait_ge(*s.at("L0a.q3T"))
                    for j in range(3):
                        for b in range(GB):
                            ins = mm(seq(j, b), t.qT3[:, j, b * P:(b + 1) * P], wtern[:, j * P:(j + 1) * P])
                    ins.then_inc(*s.step("ifg"))
                    yield n, 14
                    pe.wait_ge(*s.at("L0a.ctxT"))
                    pe.wait_ge(*s.at("L0a.qo"))
                    pe.wait_ge(*s.at("L0a.qoa"))
                    turn_rows(3, t.ta, "qoTp")
                    yield n, 16
                    pe.wait_ge(*s.at("L0a.qoT"))
                    for b in range(GB):
                        ins = mm(seq(1, b), t.qT3[:, 0, b * P:(b + 1) * P], wtern[:, 3 * P:4 * P])
                    ins.then_inc(*s.step("y"))
                if l in ("L0x", "L3a"):
                    yield n, 4
                    pe.wait_ge(*s.at(f"{l}.xnT"))
                    project_rows(0, xnT, w(f"{l}_wq"), "q")
                    if l == "L3a":
                        project_rows(1, xnT, w("L3a_wk"), "k")
                        project_rows(2, xnT, w("L3a_wv"), "v")
                    yield n, 8
                    pe.wait_ge(*s.at(f"{l}.qrot"))
                    turn_rows(0, t.tc, "QTp")
                    pe.wait_ge(*s.at(f"{l}.krot"))
                    turn_rows(1, t.td, "KTp")
                    yield from attend(n, l)
                    yield from out_proj(n, l, w(f"{l}_wo"))
                if l in ("L1a", "L1x", "L2x"):
                    yield n, 4
                    pe.wait_ge(*s.at(f"{l}.xnT"))
                    project_cols(0, xnT, w(f"{l}_wq"), "q")
                    if l == "L1a":
                        project_cols(1, xnT, w("L1a_wk"), "k")
                        project_rows(2, xnT, w("L1a_wv"), "v")
                    yield from attend(n, l)
                    yield from out_proj(n, l, w(f"{l}_wo"))
                if l == "L0f":
                    yield n, 4
                    pe.wait_ge(*s.at("L0f.xnT"))
                    gates(3, w("L0f_wg"), E0)
                    for e in range(E0):
                        yield n, (5 if e < 3 else 10 + 4 * e)
                        if e >= 3:
                            pe.wait_ge(*s.at(f"L0f.x{e - 3}.{GB - 1}"))
                        for b in range(GB):
                            ins = mm(seq(e % 3, b), xnT[:, b * P:(b + 1) * P], w("L0f_we")[:, e * P:(e + 1) * P])
                        ins.then_inc(*s.step(f"e{e}"))
                        if e == 2:
                            yield from turn_gates(n, l, E0)
                        if e == E0 // 2:
                            yield from gate_bias(n, l, E0, w("L0f_be", E0), 11 + 4 * e)
                if l == "L1f":
                    yield n, 4
                    pe.wait_ge(*s.at("L1f.xnT"))
                    gates(3, w("L1f_wg"), E1)

                    def hidden(e):
                        for c in range(2):
                            k = 2 * e + c
                            if k >= 2:
                                pe.wait_ge(*s.at(f"L1f.h{k - 2}"))
                            mm(bank(c), w("L1f_w1")[:, k * P:(k + 1) * P], xnT[:, :]).then_inc(*s.step(f"a{k}"))
                    yield n, 10
                    hidden(0)
                    yield from turn_gates(n, l, E1)
                    yield from gate_bias(n, l, E1, w("L1f_b2", E1), 14)
                    for e in range(E1):
                        yield n, 20 + 4 * e
                        if e + 1 < E1:
                            hidden(e + 1)
                        yield n, 22 + 4 * e
                        pe.wait_ge(*s.at(f"L1f.h{2 * e + 1}"))
                        if e:
                            pe.wait_ge(*s.at(f"L1f.x{e - 1}.{GB - 1}"))
                        for b in range(GB):
                            for c in range(2):
                                ins = mm(seq(2, b), hid[:, 2 * (e % 2) + c, b * P:(b + 1) * P],
                                         w("L1f_w2")[:, (2 * e + c) * P:(2 * e + c + 1) * P], start=c == 0, stop=c == 1)
                        ins.then_inc(*s.step(f"e{e}"))
                if l == "L2a":
                    yield n, 4
                    pe.wait_ge(*s.at("L2a.xnT"))
                    project_cols(0, xnT, w("L2a_wq"), "q")
                    project_cols(1, xnT, w("L2a_wk"), "k")
                    project_rows(2, xnT, w("L2a_wv"), "v")
                    for m, src in enumerate((QT, KT)):
                        yield n, 6 + 2 * m
                        pe.wait_ge(*s.at(f"L2a.{'QK'[m]}T"))
                        pe.wait_ge(*s.at("L2a.v1"))
                        for h in range(MH):
                            r = slice(MD * h, MD * h + MD)
                            for b in range(GB):
                                ins = mm(seq(2 - 2 * m + h, b), src[r, b * P:(b + 1) * P], w("L2a_om")[r, :],
                                         tile_position=(MD * h, 0))
                        ins.then_inc(*s.step(f"z{m}"))
                    for m in range(2):
                        yield n, 14 + 2 * m
                        pe.wait_ge(*s.at(f"L2a.phi{m}"))
                        for h in range(MH):
                            for b in range(GB):
                                ins = pe.transpose(seq(2 - 2 * m + h, b), pr[:, 8 * m + GB * h + b, :], ident)
                        ins.then_inc(*s.step(f"phiTp{m}"))
                    yield n, 18
                    pe.wait_ge(*s.at("L2a.phiT0"))
                    pe.wait_ge(*s.at("L2a.phiT1"))
                    for h in range(MH):
                        for b in range(GB):
                            ins = mm(seq(2 + h, b), PT[:, 8 + GB * h + b, :], PT[:, GB * h + b, :])
                        ins.then_inc(*s.step(f"A{h}"))
                    for h in range(MH):
                        yield n, 20 + h
                        pe.wait_ge(*s.at(f"L2a.Am{h}"))
                        for b in range(GB):
                            ins = mm(bank(h)[:, b * (MD + 1):(b + 1) * (MD + 1)], pr[:, GB * h + b, :], t.vv[:, b, h, :])
                        ins.then_inc(*s.step(f"O{h}"))
                    yield n, 24
                    pe.wait_ge(*s.at("L2a.co3"))
                    turn_rows(2, t.co, "coTp")
                    yield n, 26
                    pe.wait_ge(*s.at("L2a.coT"))
                    project_rows(3, t.coT, w("L2a_wo"), "y")
                    yield n, 32
                    pe.wait_ge(*s.at("L2a.hn"))
                    turn_rows(2, t.tc, "hTp")
                    yield n, 34
                    pe.wait_ge(*s.at("L2a.hT"))
                    for c in range(4):
                        mm(bank(c), w("L2a_w1")[:, c * P:(c + 1) * P], KT).then_inc(*s.step(f"f{c}"))
                    yield n, 36
                    pe.wait_ge(*s.at("L2a.g3"))
                    for b in range(GB):
                        for c in range(4):
                            ins = mm(seq(0, b), hid[:, c, b * P:(b + 1) * P], w("L2a_w2")[:, c * P:(c + 1) * P], start=c == 0, stop=c == 3)
                    ins.then_inc(*s.step("y2"))
                if l == "L2f":
                    yield n, 4
                    pe.wait_ge(*s.at("L2f.xnT"))
                    gates(3, gwT[:, :], E2)

                    def gate_up(c):
                        if c:
                            pe.wait_ge(*s.at(f"L2f.mul{c - 1}"))
                        r = P if c < 8 else HE2
                        mm(bank(0)[0:r, :], w("L2f_wg")[:, c * P:(c + 1) * P] if c < 8 else w("L2f_sg"), xnT[:, :]).then_inc(*s.step(f"g{c}"))
                        mm(bank(1)[0:r, :], w("L2f_wu")[:, c * P:(c + 1) * P] if c < 8 else w("L2f_su"), xnT[:, :]).then_inc(*s.step(f"u{c}"))

                    for c in range(LEAD):
                        yield n, 5 + 4 * c
                        gate_up(c)
                    yield n, 16
                    pe.wait_ge(*s.at("L2f.gws"))
                    gwsTp = bank(2).bitcast(BF16)
                    for b in range(GB):
                        ins = pe.transpose(gwsTp[0:3 * E2, b * P:(b + 1) * P], t.gws[:, b, :, :].rearrange("p s e -> p (s e)"), identb)
                    ins.then_inc(*s.step("gwsTp"))
                    yield n, 18
                    pe.wait_ge(*s.at("L2f.gwsT"))
                    for c in range(10):
                        yield n, 20 + 4 * c
                        if c < 8:
                            if c:
                                pe.wait_ge(*s.at(f"L2f.act{c - 1}"))
                            mm(bank(2), pairs[:, c * P:(c + 1) * P], t.gwsT[:, :]).then_inc(*s.step(f"spread{c}"))
                        if c >= 1:
                            d = c - 1
                            r = P if d < 8 else HE2
                            pe.wait_ge(*s.at(f"L2f.act{d}" if d < 8 else "L2f.mul8"))
                            for b in range(GB):
                                ins = mm(seq(3, b), hid[0:r, d % 4, b * P:(b + 1) * P],
                                         w("L2f_wd")[:, d * P:(d + 1) * P] if d < 8 else w("L2f_sd", HE2),
                                         start=(d == 0 and b == 0), stop=(d == 8 and b == GB - 1), skip_group_check=True)
                            ins.then_inc(*s.step(f"down{d}"))
                        if c + LEAD < 9:
                            gate_up(c + LEAD)
                if l == "L3x":
                    yield n, 4
                    pe.wait_ge(*s.at("L3x.xnT"))
                    project_cols(0, xnT, w("L3x_wq"), "q")
                    yield n, 6
                    pe.wait_ge(*s.at("L3x.QT"))
                    pe.wait_ge(*s.at("L3x.KT"))
                    for b in range(GB):
                        ins = mm(seq(3, b), QT[:, b * P:(b + 1) * P], KT[:, b * P:(b + 1) * P])
                    ins.then_inc(*s.step("S"))
                    yield n, 10
                    pe.wait_ge(*s.at("L3x.p"))
                    turn_rows(0, pr, "Tp")
                    yield n, 12
                    pe.wait_ge(*s.at("L3x.V"))
                    pe.wait_ge(*s.at("L3x.PT"))
                    for b in range(GB):
                        ins = mm(seq(1, b), t.tc[:, b, :], PT[:, b, :])
                    ins.then_inc(*s.step("O"))
                    yield n, 14
                    pe.wait_ge(*s.at("L3x.coT"))
                    project_rows(2, t.coT, w("L3x_wo"), "y")
                if l == "L3f":
                    if g == GROUPS - 1:
                        yield n, 3
                        pe.wait_ge(*s.at("L3f.rs", 0))
                        pe.wait_ge(*s.at("L3f.rs"))
                        pe.transpose(bank(2)[0:B, 0:P], rt_s[:, :], ident).then_inc(*s.step("sT"))
                    yield n, 4
                    pe.wait_ge(*s.at("L3f.xr"))
                    turn_rows(3, t.tc, "xrTp")
                    yield n, 9
                    pe.wait_ge(*s.at("L3f.lT"))
                    pe.wait_ge(*s.at("L3f.hT"))
                    mm(bank(0)[0:HE2, :], w("L3f_lw1"), QT).then_inc(*s.step("a0"))
                    if g == GROUPS - 1:
                        pe.wait_ge(*s.at("L3f.smin"))
                    for c in range(4):
                        if c == 3:
                            yield n, 12
                            pe.wait_ge(*s.at("L3f.h0"))
                        mm(bank((c + 1) % 4), w("L3f_hw1")[:, c * P:(c + 1) * P], KT).then_inc(*s.step(f"a{c + 1}"))
                    yield n, 14
                    pe.wait_ge(*s.at("L3f.h4"))
                    for b in range(GB):
                        mm(seq(1, b), hid[0:HE2, 4, b * P:(b + 1) * P], w("L3f_lw2", HE2))
                    for b in range(GB):
                        for c in range(4):
                            mm(seq(2, b), hid[:, c, b * P:(b + 1) * P], w("L3f_hw2")[:, c * P:(c + 1) * P], start=c == 0, stop=False)
                        ins = mm(seq(2, b), ones[0:1, :], row("L3f_hb2", 1), start=False)
                    ins.then_inc(*s.step("y"))
                    if g == GROUPS - 1:
                        yield n, 16
                        pe.wait_ge(*s.at("L3f.f"))
                        pe.transpose(bank(3)[:, 0:B], rt_e[:, :], ident[0:B, 0:B]).then_inc(*s.step("fT"))
        weave(*(program(g) for g in range(GROUPS)))

    @block.scalar
    def _(act):
        p = Steps("scalar")
        act.wait_ge(loaded["rows"], 32)
        act.wait_ge(loaded["consts"], 32)
        act.wait_ge(*p.at("pre.vv"))

        def program(g):
            s, t, bank = Steps("scalar", g), tiles[g], banks_of(g)
            QT, KT, pr, PT, hid, tc = t.QT, t.KT, t.pr, t.PT, t.hid, t.tc

            def read(out, src, need, name):
                act.wait_ge(*s.at(f"{s.layer}.{need}"))
                act.activation(out, src, ACT.Copy).then_inc(*s.step(name))

            def rounded(k, name):
                act.wait_ge(*s.at(f"L0a.{name}_s"))
                for i in range(k - k // 3, k):
                    act.activation(t.ta[:, i, :], t.ta[:, i, :], ACT.Identity, scale=t.s12b[:, i:i + 1], bias=magic[:, 0:1]).then_inc(*s.step(name + "a"))

            def values():
                act.wait_ge(*s.at(f"{s.layer}.v"))
                V = bank(2).rearrange("p (b h d) -> p b h d", b=GB, h=H)
                act.activation(t.vaug[:, :, :, 0:HD], V, ACT.Copy).then_inc(*s.step("vaug"))
                act.activation(t.vlast[:, :, 0:HD], V[:, GB - 1, :, :], ACT.Copy).then_inc(*s.step("vaug"))

            def attend(n, l):
                for u in range(UNITS):
                    yield n, beat(g, u, 3)
                    act.wait_ge(*s.at(f"{l}.top{u}"))
                    for j in range(HH):
                        P_h = pr[:, (u % 2) * HH + j, :]
                        act.activation(P_h, P_h, ACT.Exp, scale=SCALES[l], bias=t.mx[:, u % 2, j:j + 1]).then_inc(*s.step(f"exp{u}.{j // HG}"))
                    for i in range(2):
                        yield n, beat(g, u, 4 + i)
                        if u >= 2 and i == 0:
                            act.wait_ge(*s.at(f"{l}.O{u - 2}"))
                        at = (u % 2) * HH + HG * i
                        read(PT[:, at:at + HG, :], bank(2).rearrange("p (j k) -> p j k", j=HG), f"T{u}.{i}", f"PT{u}.{i}")
                yield n, beat(g, UNITS, 1)
                read(t.td[:, :, :], four(bank(3)), f"O{UNITS - 1}", "OT")
                yield n, 130
                read(t.coT[:, :], bank(2), "coTp", "coT")

            for n, l in enumerate(LAYERS[1:STAGES + 1]):
                s.begin(l)
                if l in ("L1x", "L2x", "L3x"):
                    yield n, 1
                    act.wait_ge(*s.at(f"{l}.k"))
                    if l == "L3x":
                        act.activation(KT, bank(1), ACT.Copy).then_inc(*s.step("KT"))
                    else:
                        act.activation(KT, bank(1), ACT.Identity, bias=col(f"{l}_bk")).then_inc(*s.step("KT"))
                if l == "L0x":
                    yield n, 1
                    values()
                yield n, 2
                if l not in ("L0a", "L3f"):
                    read(t.xnT[:, :], bank(3), "xnTp", "xnT")
                if l == "L0a":
                    read(t.ctxT[:, :], bank(3), "cTp", "ctxT")
                    yield n, 3
                    rounded(12, "q3")
                    yield n, 4.5
                    act.wait_ge(*s.at("L0a.q3Tp"))
                    act.activation(t.qT3, bank(0, 3).rearrange("p (j n) -> p j n", j=3), ACT.Identity, bias=magic[:, 1:2]).then_inc(*s.step("q3i"))
                    yield n, 7
                    act.wait_ge(*s.at("L0a.ndeq"))
                    act.wait_ge(*s.at("L0a.ifg"))
                    for b in range(GB):
                        act.activation(tc[:, b, :], bank(1)[:, b * P:(b + 1) * P], ACT.Exp, scale=t.ndeq[:, b:b + 1]).then_inc(*s.step("ef"))
                    yield n, 9
                    act.wait_ge(*s.at("L0a.efc"))
                    act.activation(tc[:, :, :], tc[:, :, :], ACT.Ln, bias=1.0).then_inc(*s.step("ln"))
                    yield n, 10
                    act.wait_ge(*s.last())
                    act.activation(tc[:, :, :], tc[:, :, :], ACT.Exp, scale=-float(P)).then_inc(*s.step("f128"))
                    yield n, 13
                    rounded(GB, "qo")
                    yield n, 14.5
                    act.wait_ge(*s.at("L0a.qoTp"))
                    act.activation(t.qT3[:, 0, :], bank(3), ACT.Identity, bias=magic[:, 1:2]).then_inc(*s.step("qoi"))
                if l in ("L0x", "L3a"):
                    yield n, 5
                    if l == "L0x":
                        for m, nm in ((1, "k"), (0, "q")):
                            act.wait_ge(*s.at(f"L0x.{nm}"))
                            act.activation(t.ta[:, m * GB:m * GB + GB, :], four(bank(m)), ACT.Square).then_inc(*s.step(f"{nm}sq"))
                        read(t.td[:, :, :], four(bank(1)), "k", "kraw")
                    if l == "L3a":
                        read(t.ta[:, GB:2 * GB, :], four(bank(1)), "k", "kraw")
                        values()
                    yield n, 9
                    read(QT, bank(0), "QTp", "QT")
                    read(KT, bank(1), "KTp", "KT")
                    yield from attend(n, l)
                if l in ("L1a", "L1x", "L2x"):
                    yield n, 5
                    act.wait_ge(*s.at(f"{l}.q"))
                    if l == "L1a":
                        act.activation(QT, bank(0), ACT.Copy).then_inc(*s.step("QT"))
                    else:
                        act.activation(QT, bank(0), ACT.Identity, bias=col(f"{l}_bq")).then_inc(*s.step("QT"))
                    if l == "L1a":
                        read(KT, bank(1), "k", "KT")
                        values()
                    yield from attend(n, l)
                if l in ("L0f", "L1f"):
                    k = E0 if l == "L0f" else E1
                    yield n, 8
                    act.wait_ge(*s.at(f"{l}.lgs"))
                    act.activation(t.lgm[:, :, 0:k], t.lgm[:, :, 0:k], ACT.Exp).then_inc(*s.step("lge"))
                    if l == "L1f":
                        for i in range(2):
                            yield n, 11
                            act.wait_ge(*s.at(f"L1f.a{i}"))
                            act.activation(hid[:, i, :], bank(i), ACT.Gelu, bias=col("L1f_b1", i)).then_inc(*s.step(f"h{i}"))
                    if l == "L1f":
                        yield n, 13
                        read(t.gwTT[0:k, :], bank(3)[0:k, :], "gwTp", "gwT")
                if l == "L0f":
                    act.wait_ge(*s.at("L0f.gw"))
                    for e in range(0, E0, 2):
                        yield n, 21 + 4 * e
                        if e == 2:
                            read(t.gwTT[0:k, :], bank(3)[0:k, :], "gwTp", "gwT")
                            yield n, 30
                        act.wait_ge(*s.at(f"L0f.e{e}"))
                        for b in range(GB):
                            act.activation(hid[:, e // 2, b * P:(b + 1) * P], bank(e % 3)[:, b * P:(b + 1) * P], ACT.Copy,
                                           scale=t.gw[:, b, e:e + 1]).then_inc(*s.step(f"x{e}.{b}"))
                if l == "L1f":
                    for i in range(2, 2 * E1):
                        e, c = divmod(i, 2)
                        yield n, 16 + 4 * e
                        act.wait_ge(*s.at(f"L1f.a{i}"))
                        if e >= 2:
                            act.wait_ge(*s.at(f"L1f.e{e - 2}"))
                        act.activation(hid[:, 2 * (e % 2) + c, :], bank(c), ACT.Gelu, bias=col("L1f_b1", i)).then_inc(*s.step(f"h{i}"))
                if l == "L2a":
                    yield n, 5
                    for m, (dst, nm) in enumerate(((QT, "q"), (KT, "k"))):
                        act.wait_ge(*s.at(f"L2a.{nm}"))
                        act.activation(dst, bank(m), ACT.Copy, scale=float(MD) ** -0.25).then_inc(*s.step(nm.upper() + "T"))
                    act.wait_ge(*s.at("L2a.v"))
                    act.activation(t.vv[:, :, :, 0:MD], bank(2).rearrange("p (b h d) -> p b h d", b=GB, h=MH), ACT.Copy).then_inc(*s.step("v1"))
                    for m in range(2):
                        yield n, 10 + m
                        act.wait_ge(*s.at(f"L2a.zs{m}"))
                        act.activation(pr[:, 8 * m:8 * m + 8, :], pr[:, 8 * m:8 * m + 8, :], ACT.Exp).then_inc(*s.step(f"ze{m}"))
                    for m in range(2):
                        yield n, 15 + 2 * m
                        act.wait_ge(*s.at(f"L2a.phiTp{m}"))
                        act.activation(PT[:, 8 * m:8 * m + 8, :], bank(2 - 2 * m, 2).rearrange("p (h k) -> p h k", k=P), ACT.Copy)\
                           .then_inc(*s.step(f"phiT{m}"))
                    yield n, 25
                    read(t.coT[:, :], bank(2), "coTp", "coT")
                    yield n, 33
                    act.wait_ge(*s.at("L2a.hTp"))
                    act.activation(KT, bank(2), ACT.Identity, bias=col("beta"), scale=col("gamma")).then_inc(*s.step("hT"))
                    yield n, 35
                    for c in range(4):
                        act.wait_ge(*s.at(f"L2a.f{c}"))
                        act.activation(hid[:, c, :], bank(c), ACT.Relu, bias=col("L2a_b1", c)).then_inc(*s.step(f"g{c}"))
                if l == "L2f":
                    yield n, 6
                    act.wait_ge(*s.at("L2f.lgs"))
                    act.activation(t.lgm[:, :, :], t.lgm[:, :, :], ACT.Exp, scale=-1.0).then_inc(*s.step("lge"))
                    for c in range(9):
                        r = P if c < 8 else HE2
                        if c == LEAD:
                            yield n, 17
                            read(t.gwsT[:, :], bank(2).bitcast(BF16)[0:3 * E2, 0:W4], "gwsTp", "gwsT")
                        yield n, ((7, 10, 14)[c] if c < LEAD else 21 + 4 * (c - LEAD))
                        act.wait_ge(*s.at(f"L2f.g{c}"))
                        act.activation(hid[0:r, 4 + c % 2, :], bank(0)[0:r, :], ACT.Silu).then_inc(*s.step(f"silu{c}"))
                if l == "L3x":
                    yield n, 5
                    act.wait_ge(*s.at("L3x.q"))
                    act.activation(QT, bank(0), ACT.Identity, bias=col("L3x_bq")).then_inc(*s.step("QT"))
                    yield n, 8
                    act.wait_ge(*s.at("L3x.sub"))
                    act.activation(pr[:, 0:GB, :], pr[:, 0:GB, :], ACT.Exp, scale=float(P) ** -0.5).then_inc(*s.step("exp"))
                    yield n, 11
                    read(PT[:, 0:GB, :], four(bank(0)), "Tp", "PT")
                    yield n, 13
                    read(t.coT[:, :], bank(1), "O", "coT")
                if l == "L3f":
                    if g == GROUPS - 1:
                        yield n, 4
                        act.wait_ge(*s.at("L3f.smin"))
                        act.activation(rt_e[:, :], rt_r[:, :], ACT.Exp).then_inc(*s.step("E"))
                    yield n, 7
                    act.wait_ge(*s.at("L3f.xrTp"))
                    act.activation(QT, bank(3), ACT.Copy, scale=col("L3f_lg")).then_inc(*s.step("lT"))
                    act.activation(KT, bank(3), ACT.Copy, scale=col("L3f_hg")).then_inc(*s.step("hT"))
                    yield n, 10
                    act.wait_ge(*s.at("L3f.a0"))
                    act.activation(hid[0:HE2, 4, :], bank(0)[0:HE2, :], ACT.Gelu, bias=col("L3f_lb1", 0, HE2)).then_inc(*s.step("h0"))
                    for c in range(4):
                        if c == 3:
                            yield n, 13
                        act.wait_ge(*s.at(f"L3f.a{c + 1}"))
                        act.activation(hid[:, c, :], bank((c + 1) % 4), ACT.Gelu, bias=col("L3f_hb1", c)).then_inc(*s.step(f"h{c + 1}"))
        weave(*(program(g) for g in range(GROUPS)))

    @block.vector
    def _(dve):
        def wide(v, n=P):
            return v.unsqueeze(2).to_broadcast([P, v.shape[1], n])

        def over(v, n=GB):
            return v.unsqueeze(1).to_broadcast([P, n, v.shape[1]])

        p = Steps("vector")
        p.begin("pre")

        def prologue():
            dve.wait_ge(loaded["L0a"], 16)
            dve.wait_ge(loaded["rows"], 32)
            dve.wait_ge(loaded["consts"], 32)
            wv = w("L0a_w").rearrange("p (m n) -> p m n", m=4)
            dve.tensor_reduce(wabs[:, :], wv, AX.X, ALU.add, apply_absolute_value=True).then_inc(*p.step("wabs"))
            half = HD // 2
            for n, c in enumerate((row("qn"), row("kn"))):
                dve.tensor_tensor(cw[n][:, :], const("c0"), c, ALU.mult).then_inc(*p.step())
                dve.tensor_tensor(sw[n][:, 0:half], const("s0")[:, 0:half], c[:, half:HD], ALU.mult).then_inc(*p.step())
                dve.tensor_tensor(sw[n][:, half:HD], const("s0")[:, half:HD], c[:, 0:half], ALU.mult).then_inc(*p.step())
            dve.tensor_copy(pairs[:, :].rearrange("p (e k) -> p e k", e=E2),
                            const("ident3")[0:3 * E2, :].unsqueeze(2).to_broadcast([3 * E2, E2, HE2])).then_inc(*p.step("pairs"))
            gwr = w("L2f_gw", E2)
            dve.tensor_tensor(gwn[:, :], gwr, gwr, ALU.mult).then_inc(*p.step())
            dve.wait_ge(*p.last())
            dve.tensor_reduce(gsc[:, 0:1], gwn[:, :], AX.X, ALU.add).then_inc(*p.step())
            dve.wait_ge(*p.last())
            dve.tensor_scalar(gsc[:, 0:1], gsc[:, 0:1], 1e-24, None, ALU.max).then_inc(*p.step("gss"))
            dve.wait_ge(*p.at("pre.wsum"))
            dve.tensor_scalar(wmean[:, :], ps[:, 0:4], 1.0 / (P * P), 1e-5, ALU.mult, ALU.max).then_inc(*p.step())
            dve.wait_ge(*p.last())
            dve.tensor_scalar(wsc[:, :], wmean[:, :], 1.0 / 127.0, None, ALU.mult).then_inc(*p.step())
            dve.reciprocal(wrec[:, :], wmean[:, :]).then_inc(*p.step())
            dve.wait_ge(*p.last())
            wtv = wtmp[:, :].rearrange("p (m n) -> p m n", m=4)
            for m in range(4):
                dve.tensor_scalar(wtv[:, m, :], wv[:, m, :], wrec[:, m:m + 1], MAGIC, ALU.mult, ALU.add).then_inc(*p.step())
            dve.wait_ge(*p.last())
            dve.tensor_scalar(wtmp[:, :], wtmp[:, :], MAGIC, 1.0, ALU.subtract, ALU.min).then_inc(*p.step())
            dve.wait_ge(*p.last())
            dve.tensor_scalar(wtern[:, :], wtmp[:, :], -1.0, None, ALU.max).then_inc(*p.step("wtern"))
            dve.wait_ge(*p.at("pre.gss_r"))
            dve.tensor_scalar(gwn[:, :], gwr, gsc[:, 1:2], None, ALU.mult).then_inc(*p.step("gwn"))
            dve.wait_ge(*p.at("pre.gwTp"))
            dve.tensor_copy(gwT[:, :], ps[:, 512:512 + E2]).then_inc(*p.step("gwT"))

        def program(g):
            s, t, bank = Steps("vector", g), tiles[g], banks_of(g)
            x, xn, tc, td, ta, tb, s4, s4b, s12, s12b, deq = t.x, t.xn, t.tc, t.td, t.ta, t.tb, t.s4, t.s4b, t.s12, t.s12b, t.deq
            pr, PT, hid, lg, lgm, sel, gw, gt, eq, qT3 = t.pr, t.PT, t.hid, t.lg, t.lgm, t.sel, t.gw, t.gt, t.eq, t.qT3

            def variance(src, eps, name):
                for b in range(GB):
                    dve.bn_stats(t.st[:, b, :], src[:, b, :]).then_inc(*s.step())
                for b in range(GB):
                    dve.wait_ge(*s.last(GB - 1))
                    dve.bn_aggr(t.mv[:, b, :], t.st[:, b, :]).then_inc(*s.step())
                dve.wait_ge(*s.last())
                dve.tensor_scalar(t.ve[:, :], t.mv[:, :, 1], eps, None, ALU.add).then_inc(*s.step(name))

            def squares(src):
                for b in range(GB):
                    dve.scalar_tensor_tensor(tb[:, b, :], src[:, b, :], 1.0, src[:, b, :], ALU.mult, ALU.mult,
                                             accum_out=s4[:, b:b + 1]).then_inc(*s.step())
                dve.wait_ge(*s.last())

            def mean_square(src, eps, name):
                squares(src)
                dve.tensor_scalar(s4[:, 0:GB], s4[:, 0:GB], 1.0 / P, eps, ALU.mult, ALU.add).then_inc(*s.step(name))

            def by_rms(dst, src, weight=None):
                for b in range(GB):
                    if weight is None:
                        dve.tensor_scalar(dst[:, b, :], src[:, b, :], s4b[:, b:b + 1], None, ALU.mult).then_inc(*s.step())
                    else:
                        dve.scalar_tensor_tensor(dst[:, b, :], src[:, b, :], s4b[:, b:b + 1], row(weight), ALU.mult, ALU.mult).then_inc(*s.step())
                dve.wait_ge(*s.last())

            def quantise(k, name):
                dve.tensor_reduce(s12[:, 0:k], ta[:, 0:k, :], AX.X, ALU.max, apply_absolute_value=True).then_inc(*s.step())
                dve.wait_ge(*s.last())
                dve.tensor_scalar(s12[:, 0:k], s12[:, 0:k], 1e-5, None, ALU.max).then_inc(*s.step())
                dve.wait_ge(*s.last())
                dve.reciprocal(s12b[:, 0:k], s12[:, 0:k]).then_inc(*s.step())
                dve.wait_ge(*s.last())
                dve.tensor_scalar(s12b[:, 0:k], s12b[:, 0:k], 127.0, None, ALU.mult).then_inc(*s.step(name + "_s"))
                dve.wait_ge(*s.last())
                for i in range(k - k // 3):
                    dve.tensor_scalar(ta[:, i, :], ta[:, i, :], s12b[:, i:i + 1], MAGIC, ALU.mult, ALU.add).then_inc(*s.step(name))

            def rotate(v, cos, sin, out, name, swap):
                h = GB * H
                tmp = ta[:, 8:12, :].rearrange("p b (h d) -> p (b h) d", h=H)
                o = out[:, :, :].rearrange("p b (h d) -> p (b h) d", h=H)
                dve.tensor_tensor(o, v, cos.unsqueeze(1).to_broadcast([P, h, HD]), ALU.mult).then_inc(*s.step())
                one, two = (slice(0, HD // 2), slice(HD // 2, HD)) if swap == "half" else (slice(0, HD, 2), slice(1, HD, 2))
                for a, b in ((one, two), (two, one)):
                    dve.tensor_tensor(tmp[:, :, a], v[:, :, b], sin[:, a].unsqueeze(1).to_broadcast([P, h, HD // 2]), ALU.mult).then_inc(*s.step())
                dve.wait_ge(*s.last())
                dve.tensor_tensor(out[:, :, :], out[:, :, :], ta[:, 8:12, :], ALU.add).then_inc(*s.step(name))
                dve.wait_ge(*s.last())

            def attend(n, l):
                def normal(b):
                    dve.wait_ge(*s.at(f"{l}.O{2 * b + 1}" if b < GB - 1 else f"{l}.OR"))
                    O = (bank(3)[:, 0:H * OW] if b < GB - 1 else bank(0)).rearrange("p (h d) -> p h d", h=H)
                    dve.reciprocal(t.rc[:, :], O[:, :, HD]).then_inc(*s.step())
                    dve.wait_ge(*s.last())
                    dve.tensor_tensor(t.co[:, b, :].rearrange("p (h d) -> p h d", h=H), O[:, :, 0:HD],
                                      wide(t.rc[:, :], HD), ALU.mult).then_inc(*s.step(f"co{b}"))

                if l in ("L0x", "L1a", "L3a"):
                    yield n, 19
                    dve.wait_ge(*s.at(f"{l}.KT"))
                    dve.tensor_tensor(t.KTm[:, 0, :, :], keys_of(t, 0), heads_of(0), ALU.mult).then_inc(*s.step("keys0"))
                if l in ("L1x", "L2x"):
                    yield n, 3
                    dve.wait_ge(*s.at(f"{l}.v"))
                    for b in range(GB):
                        dve.tensor_tensor(t.vaug[:, b, :, 0:HD] if b < GB - 1 else t.vlast[:, :, 0:HD], bank(2)[:, b * P:(b + 1) * P].rearrange("p (h d) -> p h d", h=H),
                                          row(f"{l}_bv").rearrange("p (h d) -> p h d", h=H), ALU.add).then_inc(*s.step("vaug"))
                if l == "L1x" and g == 0:
                    dve.wait_ge(loaded["alibi"], 16)
                for u in range(UNITS):
                    yield n, beat(g, u, 1)
                    dve.wait_ge(*s.at(f"{l}.S{u}"))
                    if u >= 2:
                        dve.wait_ge(*s.at(f"{l}.T{u - 2}.1"))
                    b, half = divmod(u, 2)
                    S, mine = bank(0, 2).rearrange("p (h k) -> p h k", h=HH), pr[:, half * HH:(half + 1) * HH, :]
                    mask = alibi[:, half * HH:(half + 1) * HH, :] if l == "L1x" else over(t.dmask[:, b, :] if l == "L2x" else causal, HH)
                    dve.tensor_tensor(mine, S, mask, ALU.add).then_inc(*s.step(f"masked{u}"))
                    dve.wait_ge(*s.last())
                    dve.tensor_reduce(t.mx[:, half, :], mine, AX.X, ALU.max).then_inc(*s.step())
                    dve.wait_ge(*s.last())
                    dve.tensor_scalar(t.mx[:, half, :], t.mx[:, half, :], -SCALES[l], None, ALU.mult).then_inc(*s.step(f"top{u}"))
                    if u >= 3 and u % 2 == 1:
                        yield n, beat(g, u, 3)
                        normal(u // 2 - 1)
                yield n, beat(g, UNITS, 3)
                normal(GB - 1)

            def add(n, l, bk, need="y", name="x"):
                yield n, 200
                dve.wait_ge(*s.at(f"{l}.{need}"))
                if l in LAST_BIAS:
                    dve.wait_ge(*s.at(f"{l}.xb"))
                dve.tensor_tensor(x[:, :, :], four(bank(bk)), x[:, :, :], ALU.add).then_inc(*s.step(name))
                dve.wait_ge(*s.last())

            def top2(n, l, k, bias):
                yield n, 6
                dve.wait_ge(*s.at(f"{l}.lg"))
                L = lg[:, :, 0:k]
                dve.tensor_tensor(L, bank(3)[:, 0:GB * k].rearrange("p (b e) -> p b e", b=GB), over(row(bias)), ALU.add).then_inc(*s.step())
                dve.wait_ge(*s.last())
                dve.tensor_reduce(s4[:, 0:GB], L, AX.X, ALU.max).then_inc(*s.step())
                dve.wait_ge(*s.last())
                dve.tensor_tensor(lgm[:, :, 0:k], L, wide(s4[:, 0:GB], k), ALU.subtract).then_inc(*s.step("lgs"))
                mine = L.unsqueeze(3).to_broadcast([P, GB, k, k])
                other = L.unsqueeze(2).to_broadcast([P, GB, k, k])
                tri = const("tri").rearrange("p (a c) -> p a c", a=E0)[:, 0:k, 0:k]
                dve.tensor_tensor(gt[:, :, 0:k, 0:k], other, mine, ALU.is_gt).then_inc(*s.step())
                dve.tensor_tensor(eq[:, :, 0:k, 0:k], other, mine, ALU.is_equal).then_inc(*s.step())
                dve.wait_ge(*s.last())
                for b in range(GB):
                    dve.tensor_tensor(eq[:, b, 0:k, 0:k], eq[:, b, 0:k, 0:k], tri, ALU.mult).then_inc(*s.step())
                dve.wait_ge(*s.last())
                for b in range(GB):
                    dve.tensor_tensor(gt[:, b, 0:k, 0:k], gt[:, b, 0:k, 0:k], eq[:, b, 0:k, 0:k], ALU.add).then_inc(*s.step())
                dve.wait_ge(*s.last())
                for b in range(GB):
                    dve.tensor_reduce(sel[:, b, 0:k], gt[:, b, 0:k, 0:k], AX.X, ALU.add).then_inc(*s.step())
                dve.wait_ge(*s.last())
                yield n, 11
                dve.wait_ge(*s.at(f"{l}.lge"))
                dve.scalar_tensor_tensor(gw[:, :, 0:k], sel[:, :, 0:k], 2.0, lgm[:, :, 0:k], ALU.is_lt, ALU.mult).then_inc(*s.step())
                dve.wait_ge(*s.last())
                dve.tensor_reduce(s4[:, 0:GB], gw[:, :, 0:k], AX.X, ALU.add).then_inc(*s.step())
                dve.wait_ge(*s.last())
                dve.reciprocal(s4b[:, 0:GB], s4[:, 0:GB]).then_inc(*s.step())
                dve.wait_ge(*s.last())
                dve.tensor_tensor(gw[:, :, 0:k], gw[:, :, 0:k], wide(s4b[:, 0:GB], k), ALU.mult).then_inc(*s.step("gw"))
                dve.wait_ge(*s.last())

            def mix(n, l, experts, banks, phase):
                for e in experts:
                    yield n, phase(e)
                    dve.wait_ge(*s.at(f"{l}.e{e}"))
                    for b in range(GB):
                        dve.wait_ge(*s.last(GB - 1))
                        dve.scalar_tensor_tensor(x[:, b, :], bank(banks[e])[:, b * P:(b + 1) * P], gw[:, b, e:e + 1], x[:, b, :],
                                                 ALU.mult, ALU.add).then_inc(*s.step(f"x{e}.{b}"))
                    if e == experts[len(experts) // 2 - 1]:
                        yield n, phase(e) + 1
                        dve.wait_ge(*s.last())
                        dve.wait_ge(*s.at(f"{l}.gb"))
                        dve.tensor_tensor(x[:, :, :], four(bank(3)), x[:, :, :], ALU.add).then_inc(*s.step())
                        dve.wait_ge(*s.last())
                dve.wait_ge(*s.last())
                if l == "L0f":
                    yield n, 199
                    dve.wait_ge(*s.at(f"L0f.sum{E0 - 2}"))
                    dve.tensor_tensor(x[:, :, :], four(t.hid[:, 0, :]), x[:, :, :], ALU.add).then_inc(*s.step())
                    dve.wait_ge(*s.last())

            for n, l in enumerate(LAYERS[1:STAGES + 1]):
                s.begin(l)
                yield n, 0
                if l == "L0a":
                    dve.wait_ge(loaded[f"x{g}"], 16)
                variance(x, 1e-5, "var")
                yield n, 1
                dve.wait_ge(*s.at(f"{l}.var_r"))
                for b in range(GB):
                    dve.tensor_scalar(xn[:, b, :], x[:, b, :], t.mv[:, b, 0:1], t.rs[:, b:b + 1], ALU.subtract, ALU.mult).then_inc(*s.step("xn"))
                if l == "L0a":
                    yield n, 2
                    dve.wait_ge(*s.last())
                    mean_square(xn[:, :, :], 1e-8, "ms")
                    yield n, 3
                    if g == 0:
                        prologue()
                    dve.wait_ge(loaded[f"mask{g}"], 16)
                    dve.tensor_scalar(t.dmask[:, :, :], t.mask, 0.0, -1e20, ALU.is_equal, ALU.mult).then_inc(*s.step("dmask"))
                    dve.wait_ge(*s.at("L0a.ms_r"))
                    by_rms(tc, xn)
                    for j, nm in enumerate(("ni", "nf", "ng")):
                        dve.tensor_tensor(ta[:, j * GB:(j + 1) * GB, :], tc[:, :, :], over(row(nm)), ALU.mult).then_inc(*s.step())
                    dve.wait_ge(*s.last())
                    quantise(12, "q3")
                    for j in range(3):
                        dve.tensor_scalar(deq[:, j * GB:(j + 1) * GB], s12[:, j * GB:(j + 1) * GB], wsc[:, j:j + 1], None, ALU.mult).then_inc(*s.step())
                    dve.wait_ge(*s.last())
                    dve.tensor_scalar(t.ndeq[:, :], deq[:, GB:2 * GB], -1.0, None, ALU.mult).then_inc(*s.step("ndeq"))
                    yield n, 5
                    dve.wait_ge(*s.at("L0a.q3i"))
                    dve.tensor_scalar(qT3, qT3, 127.0, -128.0, ALU.min, ALU.max).then_inc(*s.step("q3T"))
                    yield n, 8
                    dve.wait_ge(*s.at("L0a.ef"))
                    dve.tensor_scalar(tc[:, :, :], tc[:, :, :], 1e18, None, ALU.min).then_inc(*s.step("efc"))
                    yield n, 11
                    dve.wait_ge(*s.at("L0a.f128"))
                    for b in range(GB):
                        dve.scalar_tensor_tensor(tc[:, b, :], tc[:, b, :], 1.0, bank(2)[:, b * P:(b + 1) * P], ALU.subtract, ALU.mult,
                                                 accum_out=s4[:, b:b + 1]).then_inc(*s.step())
                    dve.wait_ge(*s.last())
                    dve.scalar_tensor_tensor(s4[:, 0:GB], s4[:, 0:GB], -1.0, deq[:, 2 * GB:3 * GB], ALU.mult, ALU.mult).then_inc(*s.step())
                    dve.wait_ge(*s.last())
                    dve.tensor_tensor(s4[:, 0:GB], s4[:, 0:GB], deq[:, 0:GB], ALU.mult).then_inc(*s.step())
                    dve.wait_ge(*s.last())
                    for b in range(GB):
                        dve.tensor_scalar(td[:, b, :], bank(0)[:, b * P:(b + 1) * P], s4[:, b:b + 1], None, ALU.mult).then_inc(*s.step())
                    dve.wait_ge(*s.last())
                    mean_square(td[:, :, :], 1.1920929e-07, "ms1")
                    yield n, 12
                    dve.wait_ge(*s.at("L0a.ms1_r"))
                    by_rms(td, td, "nout")
                    dve.wait_ge(*s.last())
                    mean_square(td[:, :, :], 1e-8, "ms2")
                    yield n, 13
                    dve.wait_ge(*s.at("L0a.ms2_r"))
                    by_rms(ta, td, "no")
                    quantise(GB, "qo")
                    dve.tensor_scalar(deq[:, 0:GB], s12[:, 0:GB], wsc[:, 3:4], None, ALU.mult).then_inc(*s.step())
                    yield n, 15
                    dve.wait_ge(*s.at("L0a.qoi"))
                    dve.tensor_scalar(qT3[:, 0, :], qT3[:, 0, :], 127.0, -128.0, ALU.min, ALU.max).then_inc(*s.step("qoT"))
                    dve.wait_ge(*s.last())
                    yield n, 17
                    dve.wait_ge(*s.at("L0a.y"))
                    for b in range(GB):
                        dve.scalar_tensor_tensor(x[:, b, :], bank(1)[:, b * P:(b + 1) * P], deq[:, b:b + 1], x[:, b, :],
                                                 ALU.mult, ALU.add).then_inc(*s.step("x"))
                    dve.wait_ge(*s.last())
                if l == "L0x":
                    v2, y2, h2, hh = t.v2, t.y2, t.h2, GB * H
                    yield n, 6
                    dve.wait_ge(*s.last())
                    for m, nm in ((0, "q"), (1, "k")):
                        dve.wait_ge(*s.at(f"L0x.{nm}sq"))
                        v = ta[:, m * GB:m * GB + GB, :].rearrange("p b (h d) -> p (b h) d", h=H)
                        dve.tensor_reduce(v2[:, m * hh:(m + 1) * hh], v, AX.X, ALU.add).then_inc(*s.step())
                    dve.wait_ge(*s.last())
                    dve.tensor_scalar(v2[:, :], v2[:, :], 1.0 / HD, 1e-10, ALU.mult, ALU.add).then_inc(*s.step())
                    dve.wait_ge(*s.last())
                    dve.tensor_scalar(h2[:, :].bitcast(I32), v2[:, :].bitcast(I32), 1, None, ALU.logical_shift_right).then_inc(*s.step())
                    dve.wait_ge(*s.last())
                    dve.tensor_scalar(y2[:, :].bitcast(I32), h2[:, :].bitcast(I32), -1.0, float(0x5F3759DF), ALU.mult, ALU.add).then_inc(*s.step())
                    dve.wait_ge(*s.last())
                    for _ in range(3):
                        dve.tensor_tensor(h2[:, :], y2[:, :], y2[:, :], ALU.mult).then_inc(*s.step())
                        dve.wait_ge(*s.last())
                        dve.scalar_tensor_tensor(h2[:, :], h2[:, :], -0.5, v2[:, :], ALU.mult, ALU.mult).then_inc(*s.step())
                        dve.wait_ge(*s.last())
                        dve.scalar_tensor_tensor(y2[:, :], h2[:, :], 1.5, y2[:, :], ALU.add, ALU.mult).then_inc(*s.step("y2"))
                        dve.wait_ge(*s.last())
                    v = ta[:, 0:GB, :].rearrange("p b (h d) -> p (b h) d", h=H)
                    dve.tensor_tensor(v, bank(0).rearrange("p (h d) -> p h d", d=HD), wide(y2[:, 0:hh], HD), ALU.mult).then_inc(*s.step())
                    dve.wait_ge(*s.last())
                    rotate(v, cw[0][:, :], sw[0][:, :], tc, "qrot", "half")
                if l == "L3a":
                    yield n, 6
                    dve.wait_ge(*s.last())
                    dve.wait_ge(*s.at("L3a.q"))
                    rotate(bank(0).rearrange("p (h d) -> p h d", d=HD), const("c3"), const("s3"), tc, "qrot", "pair")
                if l in ("L0x", "L1a", "L1x", "L2x", "L3a"):
                    yield from attend(n, l)
                    yield from add(n, l, 0)
                if l == "L0f":
                    yield from top2(n, l, E0, "bg0")
                    yield from mix(n, l, range(1, E0, 2), [e % 3 for e in range(E0)], lambda e: 21 + 4 * e)
                if l == "L1f":
                    yield from top2(n, l, E1, "bg1")
                    yield from mix(n, l, range(E1), [2] * E1, lambda e: 23 + 4 * e)
                if l == "L2a":
                    for m in range(2):
                        yield n, 7 + 2 * m
                        dve.wait_ge(*s.at(f"L2a.z{m}"))
                        Z = bank(2 - 2 * m, 2).rearrange("p (h k) -> p h k", k=P)
                        dve.tensor_reduce(s4[:, :], Z, AX.X, ALU.max).then_inc(*s.step())
                        dve.wait_ge(*s.last())
                        dve.tensor_tensor(pr[:, 8 * m:8 * m + 8, :], Z, wide(s4[:, :]), ALU.subtract).then_inc(*s.step(f"zs{m}"))
                        dve.wait_ge(*s.last())
                    for m in range(2):
                        yield n, 12 + m
                        dve.wait_ge(*s.at(f"L2a.ze{m}"))
                        dve.tensor_scalar(pr[:, 8 * m:8 * m + 8, :], pr[:, 8 * m:8 * m + 8, :], float(P) ** -0.5, 1e-6, ALU.mult, ALU.add).then_inc(*s.step(f"phi{m}"))
                    for h in range(MH):
                        yield n, 19 + h
                        dve.wait_ge(*s.at(f"L2a.A{h}"))
                        dve.tensor_tensor(pr[:, GB * h:GB * h + GB, :], four(bank(2 + h)), over(const("keepT")), ALU.mult).then_inc(*s.step(f"Am{h}"))
                    for h in range(MH):
                        yield n, 22 + h
                        dve.wait_ge(*s.at(f"L2a.O{h}"))
                        O = bank(h)[:, 0:GB * (MD + 1)].rearrange("p (b d) -> p b d", b=GB)
                        dve.tensor_scalar(s4[:, 0:GB], O[:, :, MD], 1e-6, None, ALU.add).then_inc(*s.step())
                        dve.wait_ge(*s.last())
                        dve.reciprocal(s4b[:, 0:GB], s4[:, 0:GB]).then_inc(*s.step())
                        dve.wait_ge(*s.last())
                        dve.tensor_tensor(t.co[:, :, h * MD:(h + 1) * MD], O[:, :, 0:MD], wide(s4b[:, 0:GB], MD), ALU.mult).then_inc(*s.step("co3"))
                        dve.wait_ge(*s.last())
                    yield n, 27
                    dve.wait_ge(*s.at("L2a.y"))
                    dve.tensor_tensor(tc[:, :, :], four(bank(3)), xn[:, :, :], ALU.add).then_inc(*s.step())
                    dve.wait_ge(*s.last())
                    variance(tc, 1e6, "var2")
                    yield n, 31
                    dve.wait_ge(*s.at("L2a.var2_r"))
                    for b in range(GB):
                        dve.tensor_scalar(tc[:, b, :], tc[:, b, :], t.mv[:, b, 0:1], t.rs[:, b:b + 1], ALU.subtract, ALU.mult).then_inc(*s.step("hn"))
                    yield from add(n, l, 0, "y2")
                if l == "L2f":
                    yield n, 2
                    dve.wait_ge(*s.last())
                    squares(xn)
                    dve.tensor_scalar(s4[:, 0:GB], s4[:, 0:GB], 1e-24, None, ALU.max).then_inc(*s.step("ms"))
                    yield n, 5
                    dve.wait_ge(*s.at("L2f.ms_r"))
                    dve.wait_ge(*s.at("L2f.lg"))
                    dve.tensor_tensor(lgm[:, :, :], bank(3)[:, 0:GB * E2].rearrange("p (b e) -> p b e", b=GB),
                                      wide(s4b[:, 0:GB], E2), ALU.mult).then_inc(*s.step("lgs"))
                    def times_up(c):
                        r = P if c < 8 else HE2
                        dve.wait_ge(*s.at(f"L2f.silu{c}"))
                        dve.wait_ge(*s.at(f"L2f.u{c}"))
                        if c >= 4:
                            dve.wait_ge(*s.at(f"L2f.down{c - 4}"))
                        dve.tensor_tensor(hid[0:r, c % 4, :], bank(1)[0:r, :], hid[0:r, 4 + c % 2, :], ALU.mult)\
                           .then_inc(*s.step(f"mul{c}"))

                    yield n, 7
                    times_up(0)
                    yield n, 8
                    dve.wait_ge(*s.at("L2f.lge"))
                    dve.tensor_scalar(lg[:, :, :], lgm[:, :, :], 1.0, None, ALU.add).then_inc(*s.step())
                    dve.wait_ge(*s.last())
                    dve.reciprocal(lgm[:, :, :], lg[:, :, :]).then_inc(*s.step())
                    dve.wait_ge(*s.last())
                    for b in range(GB):
                        dve.max(t.m8[:, b, :], lgm[:, b, :]).then_inc(*s.step())
                    dve.wait_ge(*s.last())
                    for b in range(GB):
                        dve.match_replace(sel[:, b, :], t.m8[:, b, :], lgm[:, b, :], -1.0).then_inc(*s.step())
                    dve.tensor_reduce(s4[:, 0:GB], t.m8[:, :, :], AX.X, ALU.add).then_inc(*s.step())
                    dve.wait_ge(*s.last())
                    dve.scalar_tensor_tensor(gw[:, :, :], sel[:, :, :], 0.0, lgm[:, :, :], ALU.is_lt, ALU.mult).then_inc(*s.step())
                    dve.reciprocal(s4b[:, 0:GB], s4[:, 0:GB]).then_inc(*s.step())
                    dve.wait_ge(*s.last())
                    dve.tensor_tensor(gw[:, :, :], gw[:, :, :], wide(s4b[:, 0:GB], E2), ALU.mult).then_inc(*s.step())
                    yield n, 11
                    times_up(1)
                    yield n, 12
                    dve.wait_ge(*s.last())
                    for part in range(3):
                        dve.wait_ge(*s.last())
                        dve.tensor_copy(t.gws[:, :, part, :], gw[:, :, :]).then_inc(*s.step("gws"))
                        if part < 2:
                            dve.wait_ge(*s.last())
                            dve.tensor_tensor(gw[:, :, :], gw[:, :, :], t.gws[:, :, part, :], ALU.subtract).then_inc(*s.step())
                    yield n, 15
                    times_up(2)
                    for c in range(8):
                        yield n, 22 + 4 * c
                        dve.wait_ge(*s.at(f"L2f.spread{c}"))
                        dve.wait_ge(*s.at(f"L2f.mul{c}"))
                        dve.tensor_tensor(hid[:, c % 4, :], bank(2), hid[:, c % 4, :], ALU.mult).then_inc(*s.step(f"act{c}"))
                        if c + LEAD < 9:
                            times_up(c + LEAD)
                    yield from add(n, l, 3, "down8")
                if l == "L3x":
                    yield n, 3
                    dve.wait_ge(*s.at("L3x.v"))
                    dve.tensor_tensor(tc[:, :, :], four(bank(2)), over(row("L3x_bv")), ALU.add).then_inc(*s.step("V"))
                    yield n, 7
                    dve.wait_ge(*s.at("L3x.S"))
                    S = four(bank(3))
                    dve.tensor_reduce(s4[:, 0:GB], S, AX.X, ALU.max).then_inc(*s.step())
                    dve.wait_ge(*s.last())
                    dve.tensor_tensor(pr[:, 0:GB, :], S, wide(s4[:, 0:GB]), ALU.subtract).then_inc(*s.step("sub"))
                    yield n, 9
                    dve.wait_ge(*s.at("L3x.exp"))
                    dve.tensor_reduce(s4[:, 0:GB], pr[:, 0:GB, :], AX.X, ALU.add).then_inc(*s.step())
                    dve.wait_ge(*s.last())
                    dve.reciprocal(s4b[:, 0:GB], s4[:, 0:GB]).then_inc(*s.step())
                    dve.wait_ge(*s.last())
                    for b in range(GB):
                        dve.tensor_scalar(pr[:, b, :], pr[:, b, :], s4b[:, b:b + 1], None, ALU.mult).then_inc(*s.step("p"))
                    yield from add(n, l, 2)
                if l == "L3f":
                    yield n, 2
                    dve.wait_ge(*s.last())
                    for b in range(GB):
                        dve.scalar_tensor_tensor(tb[:, b, :], xn[:, b, :], 1.0, row("L3f_rt"), ALU.mult, ALU.mult,
                                                 accum_out=rt_s[:, g * GB + b:g * GB + b + 1]).then_inc(*s.step("rs"))
                    dve.wait_ge(*s.last())
                    squares(xn)
                    dve.tensor_scalar(s4[:, 0:GB], s4[:, 0:GB], 1e-24, None, ALU.max).then_inc(*s.step("ms"))
                    yield n, 3
                    dve.wait_ge(*s.at("L3f.ms_r"))
                    dve.tensor_scalar(s4b[:, 0:GB], s4b[:, 0:GB], float(P) ** 0.5, None, ALU.mult).then_inc(*s.step())
                    dve.wait_ge(*s.last())
                    for b in range(GB):
                        dve.tensor_scalar(tc[:, b, :], xn[:, b, :], s4b[:, b:b + 1], None, ALU.mult).then_inc(*s.step("xr"))
                    if g == GROUPS - 1:
                        yield n, 3.5
                        dve.wait_ge(*s.at("L3f.sT"))
                        dve.tensor_scalar(rt_r[:, :], bank(2)[0:B, 0:P], 0.0, None, ALU.min).then_inc(*s.step("smin"))
                        dve.memset(rt_u[:, 0:1], float(P) / PICKED).then_inc(descent, 1)
                        yield n, 5
                        dve.wait_ge(*s.at("L3f.E"))
                        dve.wait_ge(descent, 1)
                        dve.scalar_tensor_tensor(rt_b[:, :], rt_e[:, :], rt_u[:, 0:1], rt_k[:, :], ALU.min, ALU.mult,
                                                 accum_out=rt_u[:, 1:2]).then_inc(descent, 1)
                        with dve.Fori(0, (DESCENT - 2) // ROUND) as i:
                            for k in range(ROUND):
                                dve.wait_ge(descent, ROUND * i + 2 + k)
                                dve.scalar_tensor_tensor(rt_b[:, :], rt_e[:, :], rt_u[:, 1 - k % 2:2 - k % 2], rt_k[:, :], ALU.min, ALU.mult,
                                                         accum_out=rt_u[:, k % 2:k % 2 + 1]).then_inc(descent, 1)
                        dve.wait_ge(descent, DESCENT)
                        dve.tensor_scalar(rt_u[:, 1:2], rt_u[:, 1:2], 1e-37, None, ALU.max).then_inc(descent, 1)
                        dve.wait_ge(descent, DESCENT + 1)
                        dve.reciprocal(rt_u[:, 0:1], rt_u[:, 1:2]).then_inc(*s.step())
                        dve.wait_ge(*s.last())
                        dve.tensor_scalar(rt_b[:, :], rt_e[:, :], rt_u[:, 1:2], rt_u[:, 0:1], ALU.min, ALU.mult).then_inc(*s.step())
                        dve.wait_ge(*s.last())
                        dve.tensor_scalar(rt_r[:, :], rt_b[:, :], -1.0, 1.0, ALU.mult, ALU.add).then_inc(*s.step())
                        dve.wait_ge(*s.last())
                        dve.tensor_tensor(rt_e[:, :], rt_b[:, :], rt_r[:, :], ALU.add).then_inc(*s.step("f"))
                        yield n, 17
                        dve.wait_ge(*s.at("L3f.fT"))
                        dve.tensor_copy(rt_f[:, :], bank(3)[:, 0:B]).then_inc(*s.step("rf"))
                    yield n, 18
                    dve.wait_ge(*s.at("L3f.xb"))
                    dve.wait_ge(*s.at("L3f.y"))
                    dve.wait_ge(*s.at("L3f.rf", GROUPS - 1))
                    for b in range(GB):
                        dve.scalar_tensor_tensor(x[:, b, :], bank(2)[:, b * P:(b + 1) * P], rt_f[:, g * GB + b:g * GB + b + 1], x[:, b, :],
                                                 ALU.mult, ALU.add).then_inc(*s.step())
                    dve.wait_ge(*s.last())
                    yield from add(n, l, 1)
        weave(*(program(g) for g in range(GROUPS)))
    stack.close()


def constants():
    f = np.float32
    k = np.zeros((P, NK), f)

    def put(name, v):
        k[:, KOFF[name][0]:KOFF[name][0] + KOFF[name][1]] = v
    put("ident", np.eye(P, dtype=f))
    r = np.arange(P)
    put("heads", (r[:, None] // HD == np.arange(H)[None, :]).astype(f))
    pos = np.arange(P, dtype=f)
    inv = (f(1.0) / (f(500000.0) ** (np.arange(0, HD, 2, dtype=f) / f(HD)))).astype(f)
    fr = np.outer(pos, inv).astype(f)
    emb = np.concatenate([fr, fr], -1)
    put("c0", np.cos(emb))
    put("s0", np.concatenate([-np.sin(fr), np.sin(fr)], -1))
    inv3 = (f(1.0) / (f(10000.0) ** (np.arange(0, HD, 2, dtype=f) / f(HD)))).astype(f)
    fr3 = (pos[:, None] * inv3[None, :]).astype(f)
    put("c3", np.repeat(np.cos(fr3), 2, axis=1))
    s3 = np.repeat(np.sin(fr3), 2, axis=1)
    s3[:, 0::2] *= -1
    put("s3", s3)
    put("keepT", (r[:, None] <= r[None, :]).astype(f))
    put("ident3", (r[:, None] % E2 == np.arange(E2)[None, :]).astype(f))
    e = np.arange(E0)
    put("tri", np.tile((e[None, :] < e[:, None]).astype(f).reshape(1, -1), (P, 1)))
    bf = mybir.dt.np(BF16)
    kb = np.zeros((P, NB), bf)
    kb[:, 0:P] = np.eye(P)
    put("causal", np.where(r[None, :] > r[:, None], f(NEG), f(0.0)))
    slopes = np.array([2.0 ** (-8.0 * (h + 1) / H) for h in range(H)], f)
    rel = np.abs(r[None, :] - r[:, None]).astype(f)
    bias = (-slopes[None, :, None] * rel[:, None, :]).reshape(P, H * P)
    put("alibi", (bias.astype(np.float64) * np.sqrt(float(HD))).astype(f))
    return k, kb


def pack(a):
    f = np.float32
    w = np.zeros((P, NW), f)

    def put(name, v):
        at, n = WOFF[name]
        w[0:v.shape[0], at:at + n] = v
    put("L0a_w", np.concatenate([a[f"L0_attn_W{c}"].T for c in "ifgo"], axis=1))
    for l, pre, t in (("L0x", "L0_xattn_W", True), ("L2x", "L2_xattn_W", True), ("L3x", "L3_xattn_W", True), ("L2a", "L2_attn_W", False)):
        for c in "qkvo":
            v = a[pre + c]
            put(f"{l}_w{c}", v.T if t else v)
    for c in "qkvo":
        put(f"L1a_w{c}", a["L1_attn_W" + c.upper()])
    put("L1x_wq", a["L1_xattn_Wq"])
    put("L1x_wk", a["L1_xattn_Wkv"][:, :P])
    put("L1x_wv", a["L1_xattn_Wkv"][:, P:])
    put("L1x_wo", a["L1_xattn_Wo"])
    put("L0f_wg", a["L0_ffn_Wg"])
    put("L0f_we", a["L0_ffn_We"].transpose(1, 0, 2).reshape(P, -1))
    put("L0f_be", a["L0_ffn_be"])
    put("L1f_wg", a["L1_ffn_Wg"])
    put("L1f_w1", a["L1_ffn_W1"].transpose(1, 0, 2).reshape(P, -1))
    put("L1f_w2", a["L1_ffn_W2"].reshape(E1, 2, P, P).transpose(2, 0, 1, 3).reshape(P, -1))
    put("L1f_b2", a["L1_ffn_b2"])
    put("L2a_om", np.concatenate([a["L2_attn_omega"].T] * MH, axis=0))
    put("L2a_w1", a["L2_attn_W1"])
    put("L2a_w2", a["L2_attn_W2"].reshape(4, P, P).transpose(1, 0, 2).reshape(P, -1))
    put("L2f_gw", a["L2_ffn_gate_w"])
    put("L2f_wg", a["L2_ffn_w_gate"].transpose(1, 0, 2).reshape(P, -1))
    put("L2f_wu", a["L2_ffn_w_up"].transpose(1, 0, 2).reshape(P, -1))
    put("L2f_wd", a["L2_ffn_w_down"].reshape(8, P, P).transpose(1, 0, 2).reshape(P, -1))
    put("L2f_sg", a["L2_ffn_sw_gate"])
    put("L2f_su", a["L2_ffn_sw_up"])
    put("L2f_sd", a["L2_ffn_sw_down"])
    kqv = a["L3_attn_W_KQV"]
    put("L3a_wk", kqv[0:P].T)
    put("L3a_wq", kqv[P:2 * P].T)
    put("L3a_wv", kqv[2 * P:].T)
    put("L3a_wo", a["L3_attn_W_O"].T)
    put("L3f_lw1", a["L3_ffn_light_w1"])
    put("L3f_lw2", a["L3_ffn_light_w2"])
    put("L3f_hw1", a["L3_ffn_heavy_w1"])
    put("L3f_hw2", a["L3_ffn_heavy_w2"].reshape(4, P, P).transpose(1, 0, 2).reshape(P, -1))
    rows = [a["L0_attn_ni"], a["L0_attn_nf"], a["L0_attn_ng"], a["L0_attn_nout"], a["L0_attn_no"],
            a["L0_xattn_q_norm_w"], a["L0_xattn_k_norm_w"], a["L0_ffn_bg"], a["L1_ffn_bg"],
            a["L1_xattn_bkv"][P:], a["L1_xattn_bo"], a["L2_attn_b2"], a["L2_xattn_bv"], a["L2_xattn_bo"],
            a["L3_xattn_bv"], a["L3_xattn_bo"], a["L3_ffn_light_b2"], a["L3_ffn_heavy_b2"],
            a["L3_ffn_routing_token"].reshape(P)]
    r = np.concatenate(rows).reshape(1, NR)
    c = np.zeros((P, NC), f)
    for name, v in (("L1x_bq", a["L1_xattn_bq"]), ("L1x_bk", a["L1_xattn_bkv"][:P]), ("L2x_bq", a["L2_xattn_bq"]),
                    ("L2x_bk", a["L2_xattn_bk"]), ("L3x_bq", a["L3_xattn_bq"]), ("L1f_b1", a["L1_ffn_b1"].reshape(2 * E1, P)),
                    ("L2a_b1", a["L2_attn_b1"].reshape(4, P)), ("gamma", a["L2_attn_gamma"]), ("beta", a["L2_attn_beta"]),
                    ("L3f_lg", a["L3_ffn_light_gamma"]), ("L3f_lb1", a["L3_ffn_light_b1"]), ("L3f_hg", a["L3_ffn_heavy_gamma"]),
                    ("L3f_hb1", a["L3_ffn_heavy_b1"].reshape(4, P))):
        at, n = COFF[name]
        v = v.reshape(n, -1)
        c[0:v.shape[1], at:at + n] = v.T
    return w, r, c


def kernel(**inputs):
    import concourse.bacc as _bacc
    from concourse.bass_utils import run_bass_kernel_spmd as _run

    a = {n: np.ascontiguousarray(v) for n, v in inputs.items()}
    w, r, c = pack(a)
    k, kb = constants()
    arrays = {"x": a["x"], "ctx": a["ctx_1024"], "mask": a["mask_Bx1xSxS2_ik1"].reshape(B, P, P),
              "weights": w, "rows": r, "cols": c, "consts": k, "bconsts": kb}
    marks = {}
    for _ in range(2):
        nc = _bacc.Bacc("TRN2", target_bir_lowering=False, num_devices=1)
        args = [nc.dram_tensor("in_" + n, v.shape, mybir.dt.from_np(v.dtype), kind="ExternalInput").ap() for n, v in arrays.items()]
        out = nc.dram_tensor("out_0", (B, P, P), F32, kind="ExternalOutput").ap()
        build(nc, *args, out, marks)
    res = _run(nc, [{"in_" + n: v for n, v in arrays.items()}], core_ids=[0])
    return res.results[0]["out_0"]
```
